# Optimizing a Trainium2 kernel written in Bass

```python
import numpy as np
import jax
import jax.numpy as jnp

def _softmax(x, axis=-1):
    return jax.nn.softmax(x, axis=axis)

def _gelu(x):
    return jax.nn.gelu(x, approximate=True)

def _silu(x):
    return jax.nn.silu(x)

def _sigmoid(x):
    return jax.nn.sigmoid(x)

def _layernorm(x, axis=-1, eps=1e-05):
    m = jnp.mean(x, axis=axis, keepdims=True)
    v = jnp.var(x, axis=axis, keepdims=True)
    return (x - m) / jnp.sqrt(v + eps)

def _scatter_add(tgt, idx, src, axis=0):
    return tgt.at[idx].add(src)

def _segment_sum(src, seg, n):
    return jax.ops.segment_sum(src, seg, n)
kernel_name = 'mk_adaln_d2_jaxref_r8_5ecf64'

def setup_inputs(seed: int=0):
    np.random.seed(seed)
    _w = jnp.asarray

    def _L0_attn_setup():
        import jax, jax.numpy as jnp
        import numpy as np
        B, S, D, H, DH = (4, 256, 128, 16, 64)
        key = jax.random.key(seed)
        k1, k2, k3, k4, k5 = jax.random.split(key, 5)
        scale = 1.0 / np.sqrt(D)
        return {'x': jax.random.normal(k1, (B, S, D), dtype=jnp.float32), 'w_qkv': jax.random.normal(k2, (D, 3, H, DH), dtype=jnp.float32) * scale, 'b_qkv': jax.random.normal(k3, (3, H, DH), dtype=jnp.float32) * 0.02, 'w_out': jax.random.normal(k4, (H, DH, D), dtype=jnp.float32) * (1.0 / np.sqrt(H * DH)), 'b_out': jax.random.normal(k5, (D,), dtype=jnp.float32) * 0.02}
    _L0_attn_in = _L0_attn_setup()

    def _L0_ffn_setup():
        import jax, jax.numpy as jnp
        import numpy as np
        B, L, D = (4, 128, 128)
        E, H = (8, 512)
        CAPACITY = 6
        key = jax.random.key(seed)
        ks = jax.random.split(key, 6)
        x = jax.random.normal(ks[0], (B, L, D), dtype=jnp.float32)
        gate_weight = jax.random.normal(ks[1], (E, D), dtype=jnp.float32) * 0.006
        w1 = jax.random.normal(ks[2], (E, H, D), dtype=jnp.float32) * 0.02
        b1 = jnp.zeros((E, H), dtype=jnp.float32)
        w2 = jax.random.normal(ks[3], (E, D, H), dtype=jnp.float32) * 0.02
        b2 = jnp.zeros((E, D), dtype=jnp.float32)
        return {'x': x, 'gate_weight': gate_weight, 'w1': w1, 'b1': b1, 'w2': w2, 'b2': b2}
    _L0_ffn_in = _L0_ffn_setup()
    _L0_c = _w((lambda *s: np.random.randn(*s).astype(np.float32) * 0.05)(4, 128))
    _L0_wmod = _w((lambda *s: np.random.randn(*s).astype(np.float32) * 0.05)(128, 6 * 128) * 128 ** (-0.5))

    def _L1_attn_setup():
        import jax, jax.numpy as jnp
        import numpy as np
        B, S, D = (2, 256, 128)
        H = 16
        HD = D // H

        def _rope_tables(seq_len, head_dim, dtype):
            pos = jnp.arange(seq_len, dtype=dtype)
            inv = jnp.power(10000.0, -2.0 * jnp.arange(head_dim // 2, dtype=dtype) / head_dim)
            ang = pos[:, None] * inv[None, :]
            cos_pos = jnp.repeat(jnp.cos(ang), 2, axis=-1)
            sin_pos = jnp.repeat(jnp.sin(ang), 2, axis=-1)
            return (cos_pos, sin_pos)

        def _rotate_half_interleaved(x):
            x2 = jnp.stack([-x[..., 1::2], x[..., 0::2]], axis=-1)
            return x2.reshape(x.shape)
        key = jax.random.key(seed)
        ks = jax.random.split(key, 4)
        scale = 1.0 / np.sqrt(D)
        return {'hidden_states': jax.random.normal(ks[0], (B, S, D), jnp.float32), 'Wq': jax.random.normal(ks[1], (D, D), jnp.float32) * scale, 'bq': jnp.zeros((D,), jnp.float32), 'Wk': jax.random.normal(ks[2], (D, D), jnp.float32) * scale, 'bk': jnp.zeros((D,), jnp.float32), 'Wv': jax.random.normal(ks[3], (D, D), jnp.float32) * scale, 'bv': jnp.zeros((D,), jnp.float32)}
    _L1_attn_in = _L1_attn_setup()

    def _L1_ffn_setup():
        import jax, jax.numpy as jnp
        import numpy as np
        import math
        N_EMBD = 128
        HIDDEN = 4 * N_EMBD
        N_EXPERTS = 8
        TOP_K = 2
        B, T = (4, 256)

        def new_gelu(x):
            c = math.sqrt(2.0 / math.pi)
            return 0.5 * x * (1.0 + jnp.tanh(c * (x + 0.044715 * x * x * x)))

        def _moe_forward(x, Wfc_s, bfc_s, Wproj_s, bproj_s, Wr, Wfc, bfc, Wproj, bproj):
            Bb, Tt, C = x.shape
            xf = x.reshape(Bb * Tt, C)
            N = Bb * Tt
            shared = new_gelu(xf @ Wfc_s + bfc_s) @ Wproj_s + bproj_s
            logits = xf @ Wr
            probs = jax.nn.softmax(logits, axis=-1)
            topk_p, topk_i = jax.lax.top_k(probs, TOP_K)
            topk_p = topk_p / jnp.sum(topk_p, axis=-1, keepdims=True)
            gate = jnp.zeros((N, N_EXPERTS), dtype=xf.dtype)
            gate = gate.at[jnp.arange(N)[:, None], topk_i].add(topk_p)
            routed = jnp.zeros_like(xf)
            for e in range(N_EXPERTS):
                h = new_gelu(xf @ Wfc[e] + bfc[e]) @ Wproj[e] + bproj[e]
                routed = routed + h * gate[:, e:e + 1]
            return (shared + routed).reshape(Bb, Tt, C)
        key = jax.random.key(seed)
        ks = jax.random.split(key, 10)
        s = 0.02
        return {'x': jax.random.normal(ks[0], (B, T, N_EMBD), dtype=jnp.float32), 'Wfc_s': jax.random.normal(ks[1], (N_EMBD, HIDDEN), dtype=jnp.float32) * s, 'bfc_s': jnp.zeros((HIDDEN,), dtype=jnp.float32), 'Wproj_s': jax.random.normal(ks[2], (HIDDEN, N_EMBD), dtype=jnp.float32) * s, 'bproj_s': jnp.zeros((N_EMBD,), dtype=jnp.float32), 'Wr': jax.random.normal(ks[3], (N_EMBD, N_EXPERTS), dtype=jnp.float32) * s, 'Wfc': jax.random.normal(ks[4], (N_EXPERTS, N_EMBD, HIDDEN), dtype=jnp.float32) * s, 'bfc': jnp.zeros((N_EXPERTS, HIDDEN), dtype=jnp.float32), 'Wproj': jax.random.normal(ks[5], (N_EXPERTS, HIDDEN, N_EMBD), dtype=jnp.float32) * s, 'bproj': jnp.zeros((N_EXPERTS, N_EMBD), dtype=jnp.float32)}
    _L1_ffn_in = _L1_ffn_setup()
    _L1_c = _w((lambda *s: np.random.randn(*s).astype(np.float32) * 0.05)(4, 128))
    _L1_wmod = _w((lambda *s: np.random.randn(*s).astype(np.float32) * 0.05)(128, 6 * 128) * 128 ** (-0.5))
    _d = {'L0_attn_x': _L0_attn_in['x'], 'L0_attn_w_qkv': _L0_attn_in['w_qkv'], 'L0_attn_b_qkv': _L0_attn_in['b_qkv'], 'L0_attn_w_out': _L0_attn_in['w_out'], 'L0_attn_b_out': _L0_attn_in['b_out'], 'L0_ffn_gate_weight': _L0_ffn_in['gate_weight'], 'L0_ffn_w1': _L0_ffn_in['w1'], 'L0_ffn_b1': _L0_ffn_in['b1'], 'L0_ffn_w2': _L0_ffn_in['w2'], 'L0_ffn_b2': _L0_ffn_in['b2'], 'L0_c': _L0_c, 'L0_wmod': _L0_wmod, 'L1_attn_Wq': _L1_attn_in['Wq'], 'L1_attn_bq': _L1_attn_in['bq'], 'L1_attn_Wk': _L1_attn_in['Wk'], 'L1_attn_bk': _L1_attn_in['bk'], 'L1_attn_Wv': _L1_attn_in['Wv'], 'L1_attn_bv': _L1_attn_in['bv'], 'L1_ffn_Wfc_s': _L1_ffn_in['Wfc_s'], 'L1_ffn_bfc_s': _L1_ffn_in['bfc_s'], 'L1_ffn_Wproj_s': _L1_ffn_in['Wproj_s'], 'L1_ffn_bproj_s': _L1_ffn_in['bproj_s'], 'L1_ffn_Wr': _L1_ffn_in['Wr'], 'L1_ffn_Wfc': _L1_ffn_in['Wfc'], 'L1_ffn_bfc': _L1_ffn_in['bfc'], 'L1_ffn_Wproj': _L1_ffn_in['Wproj'], 'L1_ffn_bproj': _L1_ffn_in['bproj'], 'L1_c': _L1_c, 'L1_wmod': _L1_wmod}
    _x0 = _d['L0_attn_x']
    _d['L0_attn_x'] = jax.random.normal(jax.random.fold_in(jax.random.key(seed), 1), (4, 1024, 128), dtype=_x0.dtype)
    del _x0
    return _d

def reference(L0_attn_x, L0_attn_w_qkv, L0_attn_b_qkv, L0_attn_w_out, L0_attn_b_out, L0_ffn_gate_weight, L0_ffn_w1, L0_ffn_b1, L0_ffn_w2, L0_ffn_b2, L0_c, L0_wmod, L1_attn_Wq, L1_attn_bq, L1_attn_Wk, L1_attn_bk, L1_attn_Wv, L1_attn_bv, L1_ffn_Wfc_s, L1_ffn_bfc_s, L1_ffn_Wproj_s, L1_ffn_bproj_s, L1_ffn_Wr, L1_ffn_Wfc, L1_ffn_bfc, L1_ffn_Wproj, L1_ffn_bproj, L1_c, L1_wmod):

    def _L0_attn_ref(x, w_qkv, b_qkv, w_out, b_out):
        import jax, jax.numpy as jnp
        import numpy as np
        B, S, D, H, DH = (4, 256, 128, 16, 64)
        qkv = jnp.einsum('bsd,dthe->bsthe', x, w_qkv) + b_qkv
        q, k, v = (qkv[:, :, 0], qkv[:, :, 1], qkv[:, :, 2])
        head_dim = q.shape[-1]
        scores = jnp.einsum('bqhe,bkhe->bhqk', q, k) / jnp.sqrt(jnp.float32(head_dim))
        seq = scores.shape[-1]
        causal = (jnp.arange(seq)[:, None] >= jnp.arange(seq)[None, :]).astype(scores.dtype)
        scores = scores - 1000000000.0 * (1.0 - causal)
        weights = jax.nn.softmax(scores, axis=-1)
        answers = jnp.einsum('bhqk,bkhe->bqhe', weights, v)
        out = jnp.einsum('bqhe,hed->bqd', answers, w_out) + b_out
        return out

    def _L0_ffn_ref(x, gate_weight, w1, b1, w2, b2):
        import jax, jax.numpy as jnp
        import numpy as np
        B, L, D = (4, 128, 128)
        E, H = (8, 512)
        CAPACITY = 6
        logits = jnp.einsum('bld,ed->ble', x, gate_weight)
        expert_k = B * L * CAPACITY
        kth_val = jnp.sort(logits.reshape(-1))[expert_k - 1]
        mask = (logits >= kth_val).astype(x.dtype)
        gates = logits * mask
        h = jax.nn.gelu(jnp.einsum('bld,ehd->bleh', x, w1) + b1, approximate=True)
        y = jnp.einsum('bleh,edh->blde', h, w2) + b2.T[None, None]
        out = jnp.einsum('blde,ble->bld', y, gates)
        return out

    def _L1_attn_ref(hidden_states, Wq, bq, Wk, bk, Wv, bv):
        import jax, jax.numpy as jnp
        import numpy as np
        B, S, D = (2, 256, 128)
        H = 16
        HD = D // H

        def _rope_tables(seq_len, head_dim, dtype):
            pos = jnp.arange(seq_len, dtype=dtype)
            inv = jnp.power(10000.0, -2.0 * jnp.arange(head_dim // 2, dtype=dtype) / head_dim)
            ang = pos[:, None] * inv[None, :]
            cos_pos = jnp.repeat(jnp.cos(ang), 2, axis=-1)
            sin_pos = jnp.repeat(jnp.sin(ang), 2, axis=-1)
            return (cos_pos, sin_pos)

        def _rotate_half_interleaved(x):
            x2 = jnp.stack([-x[..., 1::2], x[..., 0::2]], axis=-1)
            return x2.reshape(x.shape)
        b, s, d = hidden_states.shape
        q = hidden_states @ Wq + bq
        k = hidden_states @ Wk + bk
        v = hidden_states @ Wv + bv
        q = q.reshape(b, s, H, HD).transpose(0, 2, 1, 3)
        k = k.reshape(b, s, H, HD).transpose(0, 2, 1, 3)
        v = v.reshape(b, s, H, HD).transpose(0, 2, 1, 3)
        cos_pos, sin_pos = _rope_tables(s, HD, hidden_states.dtype)
        q = q * cos_pos + _rotate_half_interleaved(q) * sin_pos
        k = k * cos_pos + _rotate_half_interleaved(k) * sin_pos
        scores = jnp.einsum('bhqd,bhkd->bhqk', q, k) / jnp.sqrt(jnp.asarray(HD, hidden_states.dtype))
        probs = jax.nn.softmax(scores, axis=-1)
        ctx = jnp.einsum('bhqk,bhkd->bhqd', probs, v)
        ctx = ctx.transpose(0, 2, 1, 3).reshape(b, s, d)
        return ctx

    def _L1_ffn_ref(x, Wfc_s, bfc_s, Wproj_s, bproj_s, Wr, Wfc, bfc, Wproj, bproj):
        import jax, jax.numpy as jnp
        import numpy as np
        import math
        N_EMBD = 128
        HIDDEN = 4 * N_EMBD
        N_EXPERTS = 8
        TOP_K = 2
        B, T = (4, 256)

        def new_gelu(x):
            c = math.sqrt(2.0 / math.pi)
            return 0.5 * x * (1.0 + jnp.tanh(c * (x + 0.044715 * x * x * x)))

        def _moe_forward(x, Wfc_s, bfc_s, Wproj_s, bproj_s, Wr, Wfc, bfc, Wproj, bproj):
            Bb, Tt, C = x.shape
            xf = x.reshape(Bb * Tt, C)
            N = Bb * Tt
            shared = new_gelu(xf @ Wfc_s + bfc_s) @ Wproj_s + bproj_s
            logits = xf @ Wr
            probs = jax.nn.softmax(logits, axis=-1)
            topk_p, topk_i = jax.lax.top_k(probs, TOP_K)
            topk_p = topk_p / jnp.sum(topk_p, axis=-1, keepdims=True)
            gate = jnp.zeros((N, N_EXPERTS), dtype=xf.dtype)
            gate = gate.at[jnp.arange(N)[:, None], topk_i].add(topk_p)
            routed = jnp.zeros_like(xf)
            for e in range(N_EXPERTS):
                h = new_gelu(xf @ Wfc[e] + bfc[e]) @ Wproj[e] + bproj[e]
                routed = routed + h * gate[:, e:e + 1]
            return (shared + routed).reshape(Bb, Tt, C)
        return _moe_forward(x, Wfc_s, bfc_s, Wproj_s, bproj_s, Wr, Wfc, bfc, Wproj, bproj)
    x = L0_attn_x
    mod = (_silu(L0_c) @ L0_wmod).reshape(L0_c.shape[0], 6, 1, -1)
    sa, ca, ga, sb, cb, gb = (mod[:, 0], mod[:, 1], mod[:, 2], mod[:, 3], mod[:, 4], mod[:, 5])
    ga = (2 * (ga >= 0) - 1) * jnp.maximum(jnp.abs(ga), 0.25)
    gb = (2 * (gb >= 0) - 1) * jnp.maximum(jnp.abs(gb), 0.25)
    h = _layernorm(x, axis=-1) * (1 + ca) + sa
    x = x + ga * _L0_attn_ref(h, L0_attn_w_qkv, L0_attn_b_qkv, L0_attn_w_out, L0_attn_b_out)
    h = _layernorm(x, axis=-1) * (1 + cb) + sb
    x = x + gb * _L0_ffn_ref(h, L0_ffn_gate_weight, L0_ffn_w1, L0_ffn_b1, L0_ffn_w2, L0_ffn_b2)
    mod = (_silu(L1_c) @ L1_wmod).reshape(L1_c.shape[0], 6, 1, -1)
    sa, ca, ga, sb, cb, gb = (mod[:, 0], mod[:, 1], mod[:, 2], mod[:, 3], mod[:, 4], mod[:, 5])
    ga = (2 * (ga >= 0) - 1) * jnp.maximum(jnp.abs(ga), 0.25)
    gb = (2 * (gb >= 0) - 1) * jnp.maximum(jnp.abs(gb), 0.25)
    h = _layernorm(x, axis=-1) * (1 + ca) + sa
    x = x + ga * _L1_attn_ref(h, L1_attn_Wq, L1_attn_bq, L1_attn_Wk, L1_attn_bk, L1_attn_Wv, L1_attn_bv)
    h = _layernorm(x, axis=-1) * (1 + cb) + sb
    x = x + gb * _L1_ffn_ref(h, L1_ffn_Wfc_s, L1_ffn_bfc_s, L1_ffn_Wproj_s, L1_ffn_bproj_s, L1_ffn_Wr, L1_ffn_Wfc, L1_ffn_bfc, L1_ffn_Wproj, L1_ffn_bproj)
    return x

_drawn_inputs = setup_inputs


def setup_inputs(seed=0):
    import zlib

    import numpy as np

    out = dict(_drawn_inputs(seed))
    spreads = {'L0_ffn_b1': (0.0, 0.8),
     'L0_ffn_b2': (0.0, 0.8),
     'L1_attn_bq': (0.0, 0.8),
     'L1_attn_bk': (0.0, 0.8),
     'L1_attn_bv': (0.0, 0.31),
     'L1_ffn_bfc_s': (0.0, 0.8),
     'L1_ffn_bproj_s': (0.0, 0.316),
     'L1_ffn_bfc': (0.0, 0.8),
     'L1_ffn_bproj': (0.0, 0.443)}
    factors = {'L0_attn_b_qkv': 8.0,
     'L0_attn_b_out': 8.0,
     'L0_ffn_gate_weight': 8.0,
     'L0_ffn_w1': 8.0,
     'L0_ffn_w2': 8.0,
     'L1_attn_Wq': 3.662,
     'L1_attn_Wk': 3.524,
     'L1_attn_Wv': 3.204,
     'L1_ffn_Wfc_s': 4.277,
     'L1_ffn_Wproj_s': 3.838,
     'L1_ffn_Wr': 3.194,
     'L1_ffn_Wfc': 5.993,
     'L1_ffn_Wproj': 5.457}
    for name, (base, spread) in spreads.items():
        noise = np.random.default_rng([zlib.crc32(name.encode()), seed]).standard_normal(out[name].shape)
        drawn = base * np.exp(spread * noise) if base else spread * noise
        out[name] = jnp.asarray(drawn.astype(out[name].dtype))
    for name, factor in factors.items():
        out[name] = (out[name] * factor).astype(out[name].dtype)
    return out
```

```python
from contextlib import ExitStack

import numpy as np

import concourse.bass as bass
from concourse import mybir

P = 128
BATCH = 4
SEQ = 1024
CH = 128
TOK = BATCH * SEQ
CHUNK = 512
NCHUNK = TOK // CHUNK
NTILE = TOK // P
HEADS0 = 16
DH0 = 64
PAIRS = HEADS0 // 2
EXPERTS = 8
HID = 512
HT = HID // P
KTH = BATCH * 128 * 6
HEADS1 = 16
DH1 = CH // HEADS1
QUADS = 4
EPS = 1e-5
WS = 16.0
SH = 1024.0

F32 = mybir.dt.float32
F16 = mybir.dt.float16
BF16 = mybir.dt.bfloat16
I32 = mybir.dt.int32
ALU = mybir.AluOpType
ACT = mybir.ActivationFunctionType
AX_X = mybir.AxisListType.X
ds = bass.ds

CONST = {}
_at = 0
for _name, _n in (("ident", P), ("mask_qk", P), ("mask_kq", P), ("place_ctx", 32), ("place_sum", 32), ("prefer", EXPERTS),
                  ("key_pad", 1), ("rot_sign", 1), ("gate_sel", EXPERTS * P), ("q_sel", QUADS * 2 * P),
                  ("k_sel", QUADS * 2 * P), ("cos", SEQ), ("sin", SEQ)):
    CONST[_name] = (_at, _n)
    _at += _n
CONST_COLS = _at

ROW_AT = {}
_at = 0
for _name, _n in (("b_out", 1), ("bq", 1), ("bk", 1), ("bv", 1), ("bq_rot", 1), ("bk_rot", 1), ("c0", BATCH), ("c1", BATCH),
                  ("gate0", EXPERTS), ("bv0", PAIRS), ("b1", EXPERTS * HT), ("bfc_s", HT), ("bfc", EXPERTS * HT),
                  ("bproj_s", 1)):
    ROW_AT[_name] = (_at, _n)
    _at += _n
ROWS = _at

SA, CA, GA, SB, CB, GB = range(6)


def constants():
    c = np.zeros((P, CONST_COLS), np.float32)

    def put(name, a):
        at, n = CONST[name]
        c[:a.shape[0], at:at + n] = a.reshape(a.shape[0], n)

    r = np.arange(P)
    put("ident", np.eye(P, dtype=np.float32))
    far = -1e9 * np.sqrt(DH0) * WS * WS
    put("mask_qk", np.where(r[None, :] > r[:, None], far, 0.0))
    put("mask_kq", np.where(r[:, None] > r[None, :], far, 0.0))
    ctx, tot, pad = np.zeros((P, 32)), np.zeros((P, 32)), np.zeros((P, 1))
    q_sel, k_sel = np.zeros((P, QUADS, 2, P)), np.zeros((P, QUADS, 2, P))
    for j in range(4):
        pad[32 * j + 3 * DH1] = SH
        for d in range(DH1):
            ctx[32 * j + d, DH1 * j + d] = 1
            tot[32 * j + DH1, DH1 * j + d] = 1
            for g in range(QUADS):
                ch = (4 * g + j) * DH1 + d
                for copy, (q_low, k_low) in enumerate(((0, 0), (1, 0), (0, 1))):
                    q_sel[ch, g, q_low, 32 * j + DH1 * copy + d] = 1
                    k_sel[ch, g, k_low, 32 * j + DH1 * copy + d] = 1
    put("place_ctx", ctx)
    put("place_sum", tot)
    put("key_pad", pad)
    put("q_sel", q_sel)
    put("k_sel", k_sel)
    put("prefer", np.tile(np.arange(EXPERTS, 0, -1), (P, 1)))
    put("rot_sign", np.where(r % 2 == 0, -1.0, 1.0)[:, None])
    sel = np.zeros((3 * EXPERTS, EXPERTS, P))
    for e in range(EXPERTS):
        sel[e::EXPERTS, e, :] = 1
    put("gate_sel", sel)
    pos = np.arange(SEQ, dtype=np.float32)
    inv = np.power(np.float32(10000.0), np.float32(-2.0) * np.arange(DH1 // 2, dtype=np.float32) / np.float32(DH1)).astype(np.float32)
    ang = (pos[:, None] * inv[None, :]).astype(np.float32)
    put("cos", np.tile(np.repeat(np.cos(ang), 2, axis=-1).T, (HEADS1, 1)))
    put("sin", np.tile(np.repeat(np.sin(ang), 2, axis=-1).T, (HEADS1, 1)))
    return c


class Chip:
    pass


class Link:

    def __init__(self, eng, sem):
        self.eng, self.sem, self.n = eng, sem, 0

    def __call__(self, ins):
        self.n += 1
        ins.then_inc(self.sem, 1)
        self.eng.wait_ge(self.sem, self.n)


def apart(eng, chip):
    eng.sem_inc(chip.apart, 1)


def const(chip, name, rows=P):
    at, n = CONST[name]
    return chip.consts[0:rows, at:at + n]


def col(chip, name, k=0):
    return chip.cols[:, ROW_AT[name][0] + k:ROW_AT[name][0] + k + 1]


def setup(nc, chip, dram):
    with ExitStack() as ctx:
        def sb(name, shape, dt):
            return ctx.enter_context(nc.sbuf_tensor(name, shape, dt))

        def sem(name):
            return ctx.enter_context(nc.semaphore(name))

        bank = [ctx.enter_context(nc.psum_tensor(f"setup_bank{i}", [P, 512], F32)) for i in range(8)]
        x_tok = sb("x_tok", [P, NTILE, CH], F32)
        rows = sb("rows", [P, P], F32)
        dup_rows = sb("dup_rows", [48, P], F32)
        wmod = sb("wmod", [P, 2, 6 * CH], F32)
        w1_raw = sb("w1_raw", [P, EXPERTS * HT, CH], F32)
        w2_raw = sb("w2_raw", [P, EXPERTS, HID], F32)
        silu = sb("silu", [P, 3, 2 * BATCH], F32)
        mag = sb("mag", [P, 2, 2, 2, BATCH], F32)

        loaded_const, loaded_rows = sem("loaded_const"), sem("loaded_rows")
        loaded_x = [sem(f"loaded_x{n}") for n in range(NCHUNK)]
        loaded_wmod, loaded_qkv, loaded_w1, loaded_w2 = sem("loaded_wmod"), sem("loaded_qkv"), sem("loaded_w1"), sem("loaded_w2")
        loaded_small = sem("loaded_small")
        rows_clear, turned_rows, cols_ready = sem("rows_clear"), sem("turned_rows"), sem("cols_ready")
        silu_exp, silu_ready = sem("silu_exp"), sem("silu_ready")
        turned_x, x_by_act, x_by_dve = sem("turned_x"), sem("x_by_act"), sem("x_by_dve")
        mod_done, mod_taken = sem("mod_done"), sem("mod_taken")
        turned_w1, w1_high, w1_low = sem("turned_w1"), sem("w1_high"), sem("w1_low")
        turned_w2, w2_by_act, w2_by_dve = sem("turned_w2"), sem("w2_by_act"), sem("w2_by_dve")
        high_done = sem("high_done")
        dve_chain = sem("setup_dve_chain")
        N_ROW_LOADS = 16

        block = ctx.enter_context(nc.Block())

        @block.sync
        def _(sp):
            sp.wait_ge(rows_clear, 1)
            for h in range(2):
                sp.dma_start(dup_rows[:, h * DH0:(h + 1) * DH0], dram["L0_attn_b_qkv"].rearrange("t h e -> (t h) e")).then_inc(loaded_rows, 16)

            def row(name, src):
                at, n = ROW_AT[name]
                sp.dma_start(rows[at:at + n, :], src).then_inc(loaded_rows, 16)

            vec = "(a b) -> a b"
            row("b_out", dram["L0_attn_b_out"].rearrange(vec, b=CH))
            row("bq", dram["L1_attn_bq"].rearrange(vec, b=CH))
            row("bk", dram["L1_attn_bk"].rearrange(vec, b=CH))
            row("bv", dram["L1_attn_bv"].rearrange(vec, b=CH))
            row("c0", dram["L0_c"])
            row("c1", dram["L1_c"])
            row("gate0", dram["L0_ffn_gate_weight"])
            row("bv0", dram["L0_attn_b_qkv"][2].rearrange("(a b) e -> a (b e)", b=2))
            row("b1", dram["L0_ffn_b1"].rearrange("e (j p) -> (e j) p", p=P))
            row("bfc_s", dram["L1_ffn_bfc_s"].rearrange(vec, b=CH))
            row("bproj_s", dram["L1_ffn_bproj_s"].rearrange(vec, b=CH))
            row("bfc", dram["L1_ffn_bfc"].rearrange("e (j p) -> (e j) p", p=P))
            for name, src in (("bq_rot", "L1_attn_bq"), ("bk_rot", "L1_attn_bk")):
                at = ROW_AT[name][0]
                pairs = dram[src].rearrange("(a i two) -> a i two", a=1, two=2)
                out = rows[at:at + 1, :].rearrange("a (i two) -> a i two", two=2)
                sp.dma_start(out[:, :, 0:1], pairs[:, :, 1:2], allow_slow_non_contiguous=True).then_inc(loaded_rows, 16)
                sp.dma_start(out[:, :, 1:2], pairs[:, :, 0:1], allow_slow_non_contiguous=True).then_inc(loaded_rows, 16)
            sp.dma_start(wmod[:, 0, :], dram["L0_wmod"]).then_inc(loaded_wmod, 16)
            sp.dma_start(wmod[:, 1, :], dram["L1_wmod"]).then_inc(loaded_wmod, 16)
            sp.dma_start(chip.w_qkv_raw[:], dram["L0_attn_w_qkv"].rearrange("d t h e -> d (t h e)")).then_inc(loaded_qkv, 16)
            sp.dma_start(chip.w_out_raw[:], dram["L0_attn_w_out"].rearrange("(p s) e d -> (s e) p d", s=2)).then_inc(loaded_qkv, 16)
            sp.dma_start(w2_raw[:], dram["L0_ffn_w2"].rearrange("e d h -> d e h")).then_inc(loaded_w2, 16)
            sp.dma_start(chip.w_router1[:], dram["L1_ffn_Wr"]).then_inc(loaded_small, 16)
            for k, name in enumerate(("L1_attn_Wq", "L1_attn_Wk", "L1_attn_Wv")):
                sp.dma_start(chip.w1_attn_raw[:, k, :], dram[name]).then_inc(loaded_small, 16)
            for k in range(3):
                sp.dma_start(chip.b2_rows[EXPERTS * k:EXPERTS * (k + 1), :], dram["L0_ffn_b2"]).then_inc(loaded_small, 16)
                sp.dma_start(chip.bproj_rows[EXPERTS * k:EXPERTS * (k + 1), :], dram["L1_ffn_bproj"]).then_inc(loaded_small, 16)
            sp.wait_ge(loaded_small, 16 * 10)

        @block.scalar
        def _(act):
            act.dma_start(chip.consts[:], dram["consts"]).then_inc(loaded_const, 16)
            x_view = dram["L0_attn_x"].rearrange("b (t p) c -> p (b t) c", p=P)
            for n in range(NCHUNK):
                act.dma_start(x_tok[:, 4 * n:4 * n + 4, :], x_view[:, 4 * n:4 * n + 4, :]).then_inc(loaded_x[n], 16)
            act.dma_start(w1_raw[:], dram["L0_ffn_w1"].rearrange("e (j p) d -> p (e j) d", p=P)).then_inc(loaded_w1, 16)
            act.wait_ge(cols_ready, 1)
            c_cols = chip.cols[:, ROW_AT["c0"][0]:ROW_AT["c0"][0] + 2 * BATCH]
            nc.scalar.activation(silu[:, 0, :], c_cols, ACT.Exp, scale=-1.0).then_inc(silu_exp, 1)
            for n in range(1, NCHUNK, 2):
                act.wait_ge(turned_x, n + 1)
                nc.scalar.copy(chip.xT[:, n * CHUNK:(n + 1) * CHUNK], bank[n][:]).then_inc(x_by_act, 1)
            act.wait_ge(loaded_qkv, 32)
            qkv = chip.w_qkv_raw[:].rearrange("c (t h e) -> c t h e", t=3, h=HEADS0)
            for t in range(2):
                for twice in range(2):
                    nc.scalar.mul(chip.w_qk[:, 0, :, t, twice, :], qkv[:, t, :, :], WS).then_inc(high_done, 1)
            nc.scalar.mul(chip.w_v[:, 0, :], chip.w_qkv_raw[:, 2 * HEADS0 * DH0:], WS).then_inc(high_done, 1)
            nc.scalar.mul(chip.w_out[:, 0, :, :], chip.w_out_raw[:], WS).then_inc(high_done, 1)
            for k in range(8):
                act.wait_ge(turned_w1, k + 1)
                nc.scalar.mul(chip.w1T[:, 0, 4 * k:4 * k + 4, :], bank[k][:].rearrange("p (a b) -> p a b", a=4), WS).then_inc(w1_high, 1)
            for k in range(1, 8, 2):
                act.wait_ge(turned_w2, k + 1)
                nc.scalar.copy(chip.w2T[:, 4 * k:4 * k + 4, :], bank[k][:].rearrange("p (a b) -> p a b", a=4)).then_inc(w2_by_act, 1)

        @block.tensor
        def _(pe):
            ident = const(chip, "ident")
            pe.wait_ge(loaded_const, 16)
            pe.wait_ge(loaded_rows, 16 * (2 + 16))
            pe.transpose(bank[7][:, 0:48], dup_rows[:], ident[0:48, 0:48]).then_inc(turned_rows, 1)
            pe.transpose(bank[7][:, 64:64 + ROWS], rows[0:ROWS, :], ident[0:ROWS, 0:ROWS]).then_inc(turned_rows, 1)
            for n in range(NCHUNK):
                pe.wait_ge(loaded_x[n], 16)
                if n == 7:
                    pe.wait_ge(cols_ready, 1)
                for i in range(4):
                    ins = pe.transpose(bank[n][:, i * P:(i + 1) * P], x_tok[:, 4 * n + i, :], ident)
                ins.then_inc(turned_x, 1)
            pe.wait_ge(silu_ready, 1)
            pe.wait_ge(loaded_wmod, 32)
            pe.wait_ge(x_by_dve, 1)
            for layer in range(2):
                for k in range(6):
                    ins = pe.matmul(bank[0][:, (layer * 6 + k) * BATCH:(layer * 6 + k + 1) * BATCH],
                                    wmod[:, layer, k * CH:(k + 1) * CH],
                                    silu[:, 2, layer * BATCH:(layer + 1) * BATCH], start=True, stop=True)
            ins.then_inc(mod_done, 1)
            pe.wait_ge(loaded_w1, 16)
            pe.wait_ge(mod_taken, 1)
            pe.wait_ge(x_by_act, 4)
            pe.wait_ge(x_by_dve, 4)
            for k in range(8):
                for i in range(4):
                    ins = pe.transpose(bank[k][:, i * P:(i + 1) * P], w1_raw[:, 4 * k + i, :], ident)
                ins.then_inc(turned_w1, 1)
            pe.wait_ge(loaded_w2, 16)
            for k in range(8):
                pe.wait_ge(w1_low, k + 1)
                for i in range(4):
                    ins = pe.transpose(bank[k][:, i * P:(i + 1) * P], w2_raw[:, k, i * P:(i + 1) * P], ident)
                ins.then_inc(turned_w2, 1)

        @block.gpsimd
        def _(pool):
            nc.gpsimd.memset(rows[:], 0.0).then_inc(rows_clear, 1)
            nc.gpsimd.memset(chip.mean_ones[:], 1.0 / CH)
            nc.gpsimd.memset(chip.ones[:], 1.0)
            nc.gpsimd.memset(chip.sum_ones[:], WS)
            nc.gpsimd.memset(chip.eps[:], EPS)
            pool.wait_ge(loaded_const, 16)
            nc.gpsimd.tensor_copy(chip.ident16[:], const(chip, "ident"))
            nc.gpsimd.tensor_copy(chip.identb[:], const(chip, "ident"))
            nc.gpsimd.tensor_copy(chip.mask_qk[:], const(chip, "mask_qk"))
            nc.gpsimd.tensor_copy(chip.mask_kq[:], const(chip, "mask_kq"))
            nc.gpsimd.tensor_copy(chip.gate_sel[:], const(chip, "gate_sel", 3 * EXPERTS))
            nc.gpsimd.tensor_copy(chip.q_sel[:], const(chip, "q_sel"))
            nc.gpsimd.tensor_copy(chip.k_sel[:], const(chip, "k_sel"))

        @block.vector
        def _(dve):
            link = Link(dve, dve_chain)
            dve.wait_ge(turned_rows, 2)
            link(nc.vector.tensor_copy(chip.cols[:, 0:ROWS], bank[7][:, 64:64 + ROWS]))
            nc.vector.tensor_scalar(chip.bqk[:], bank[7][:, 0:2 * HEADS0], WS, None, ALU.mult).then_inc(cols_ready, 1)
            dve.wait_ge(silu_exp, 1)
            link(nc.vector.tensor_scalar(silu[:, 1, :], silu[:, 0, :], 1.0, None, ALU.add))
            link(nc.vector.reciprocal(silu[:, 0, :], silu[:, 1, :]))
            c_cols = chip.cols[:, ROW_AT["c0"][0]:ROW_AT["c0"][0] + 2 * BATCH]
            nc.vector.tensor_tensor(silu[:, 2, :], silu[:, 0, :], c_cols, ALU.mult).then_inc(silu_ready, 1)
            for n in range(0, NCHUNK, 2):
                dve.wait_ge(turned_x, n + 1)
                nc.vector.tensor_copy(chip.xT[:, n * CHUNK:(n + 1) * CHUNK], bank[n][:]).then_inc(x_by_dve, 1)
            dve.wait_ge(mod_done, 1)
            mod = chip.mod
            link(nc.vector.tensor_copy(mod[:].rearrange("p l k b -> p (l k b)"), bank[0][:, 0:12 * BATCH]))
            nc.vector.memset(silu[:, 1, 0:1], 0.0).then_inc(mod_taken, 1)
            for k in (CA, CB):
                link(nc.vector.tensor_scalar(mod[:, :, k, :], mod[:, :, k, :], 1.0, None, ALU.add))
            for n, k in enumerate((GA, GB)):
                g = mod[:, :, k, :]
                size, sign = mag[:, 0, n, :, :], mag[:, 1, n, :, :]
                link(nc.vector.scalar_tensor_tensor(size, g, -1.0, g, ALU.mult, ALU.max))
                link(nc.vector.tensor_scalar(size, size, 0.25, None, ALU.max))
                link(nc.vector.tensor_scalar(sign, g, 0.0, 2.0, ALU.is_ge, ALU.mult))
                link(nc.vector.scalar_tensor_tensor(g, sign, -1.0, size, ALU.add, ALU.mult))
            link(nc.vector.tensor_scalar(chip.g_bias[:, 0, :], mod[:, 0, GA, :], col(chip, "b_out"), None, ALU.mult))
            link(nc.vector.tensor_scalar(chip.g_bias[:, 1, :], mod[:, 1, GA, :], col(chip, "bv"), None, ALU.mult))
            link(nc.vector.tensor_scalar(chip.g_bias[:, 2, :], mod[:, 1, GB, :], col(chip, "bproj_s"), None, ALU.mult))
            link(nc.vector.tensor_scalar(chip.ga_scaled[:], mod[:, 0, GA, :], 1.0 / WS, None, ALU.mult))
            at = ROW_AT["bq"][0]
            link(nc.vector.tensor_scalar(chip.bqk1[:, 0:2], chip.cols[:, at:at + 2], WS, None, ALU.mult))
            at = ROW_AT["bq_rot"][0]
            link(nc.vector.tensor_scalar(chip.bqk1[:, 2:4], chip.cols[:, at:at + 2], const(chip, "rot_sign"), WS, ALU.mult, ALU.mult))
            dve.wait_ge(loaded_qkv, 32)
            qkv = chip.w_qkv_raw[:].rearrange("c (t h e) -> c t h e", t=3, h=HEADS0)
            for t in range(2):
                for twice in range(2):
                    dve.wait_ge(high_done, 2 * t + twice + 1)
                    nc.vector.scalar_tensor_tensor(chip.w_qk[:, 1, :, t, twice, :], qkv[:, t, :, :], WS,
                                                   chip.w_qk[:, 0, :, t, twice, :], ALU.mult, ALU.subtract)
            dve.wait_ge(high_done, 6)
            nc.vector.scalar_tensor_tensor(chip.w_v[:, 1, :], chip.w_qkv_raw[:, 2 * HEADS0 * DH0:], WS, chip.w_v[:, 0, :],
                                           ALU.mult, ALU.subtract)
            nc.vector.scalar_tensor_tensor(chip.w_out[:, 1, :, :], chip.w_out_raw[:], WS, chip.w_out[:, 0, :, :],
                                           ALU.mult, ALU.subtract)
            for k in range(8):
                dve.wait_ge(w1_high, k + 1)
                nc.vector.scalar_tensor_tensor(chip.w1T[:, 1, 4 * k:4 * k + 4, :], bank[k][:].rearrange("p (a b) -> p a b", a=4),
                                               WS, chip.w1T[:, 0, 4 * k:4 * k + 4, :], ALU.mult, ALU.subtract).then_inc(w1_low, 1)
            for k in range(0, 8, 2):
                dve.wait_ge(turned_w2, k + 1)
                nc.vector.tensor_copy(chip.w2T[:, 4 * k:4 * k + 4, :], bank[k][:].rearrange("p (a b) -> p a b", a=4)).then_inc(w2_by_dve, 1)


def layer_norm(nc, chip, name, layer, shift, scale, bias_of=None, router=None, logits=None):
    with ExitStack() as ctx:
        def sb(what, shape, dt):
            return ctx.enter_context(nc.sbuf_tensor(f"{name}_{what}", shape, dt))

        def sem(what):
            return ctx.enter_context(nc.semaphore(f"{name}_{what}"))

        mean = [ctx.enter_context(nc.psum_tensor(f"{name}_mean{u}", [P, CHUNK], F32)) for u in range(2)]
        var = [ctx.enter_context(nc.psum_tensor(f"{name}_var{u}", [P, CHUNK], F32)) for u in range(2)]
        logit = [ctx.enter_context(nc.psum_tensor(f"{name}_logit{u}", [P, 4, EXPERTS], F32)) for u in range(2)]
        centred, square, deviation, inverse, h32 = (
            [sb(f"{what}{u}", [P, CHUNK], F32) for u in range(2)] for what in ("centred", "square", "deviation", "inverse", "h32"))
        x_whole, mean_ready, centred_ready, square_ready, var_ready, deviation_ready = (
            sem(w) for w in ("x_whole", "mean_ready", "centred_ready", "square_ready", "var_ready", "deviation_ready"))
        inverse_ready, normed_ready, h_ready, high_ready, logit_ready = (
            sem(w) for w in ("inverse_ready", "normed_ready", "h_ready", "high_ready", "logit_ready"))
        block = ctx.enter_context(nc.Block())

        def chunk(a, t, u):
            return a[:, ds(t * SEQ + u * CHUNK, CHUNK)]

        @block.tensor
        def _(pe):
            with pe.Fori(0, BATCH) as t:
                for u in range(2):
                    if bias_of is not None:
                        pe.wait_ge(x_whole, 2 * t + u + 1)
                    pe.matmul(mean[u][:], chip.mean_ones[:], chunk(chip.xT, t, u), start=True, stop=True).then_inc(mean_ready, 1)
                for u in range(2):
                    pe.wait_ge(square_ready, 2 * t + u + 1)
                    pe.matmul(var[u][:], chip.mean_ones[:], square[u][:], start=True, stop=True).then_inc(var_ready, 1)
                if router is not None:
                    for u in range(2):
                        pe.wait_ge(h_ready, 2 * t + u + 1)
                        for i in range(4):
                            ins = pe.matmul(logit[u][:, i, :], h32[u][:, i * P:(i + 1) * P], router, start=True, stop=True)
                        ins.then_inc(logit_ready, 1)

        @block.scalar
        def _(act):
            with act.Fori(0, BATCH) as t:
                for u in range(2):
                    act.wait_ge(centred_ready, 2 * t + u + 1)
                    nc.scalar.square(square[u][:], centred[u][:]).then_inc(square_ready, 1)
                for u in range(2):
                    act.wait_ge(var_ready, 2 * t + u + 1)
                    nc.scalar.activation(deviation[u][:], var[u][:], ACT.Sqrt, bias=chip.eps[:, 0:1]).then_inc(deviation_ready, 1)
                for u in range(2):
                    act.wait_ge(h_ready, 2 * t + u + 1)
                    apart(act, chip)
                    nc.scalar.copy(chunk(chip.h_high, t, u), h32[u][:]).then_inc(high_ready, 1)

        @block.vector
        def _(dve):
            with dve.Fori(0, BATCH) as t:
                for u in range(2):
                    if bias_of is not None:
                        nc.vector.tensor_scalar(chunk(chip.xT, t, u), chunk(chip.xT, t, u), chip.g_bias[:, bias_of, ds(t, 1)], None,
                                                ALU.add).then_inc(x_whole, 1)
                for u in range(2):
                    dve.wait_ge(mean_ready, 2 * t + u + 1)
                    nc.vector.tensor_tensor(centred[u][:], chunk(chip.xT, t, u), mean[u][:], ALU.subtract).then_inc(centred_ready, 1)
                for u in range(2):
                    dve.wait_ge(deviation_ready, 2 * t + u + 1)
                    nc.vector.reciprocal(inverse[u][:], deviation[u][:]).then_inc(inverse_ready, 1)
                for u in range(2):
                    dve.wait_ge(inverse_ready, 2 * t + u + 1)
                    nc.vector.tensor_tensor(centred[u][:], centred[u][:], inverse[u][:], ALU.mult).then_inc(normed_ready, 1)
                for u in range(2):
                    dve.wait_ge(normed_ready, 2 * t + u + 1)
                    nc.vector.tensor_scalar(h32[u][:], centred[u][:], chip.mod[:, layer, scale, ds(t, 1)],
                                            chip.mod[:, layer, shift, ds(t, 1)], ALU.mult, ALU.add).then_inc(h_ready, 1)
                for u in range(2):
                    dve.wait_ge(high_ready, 2 * t + u + 1)
                    nc.vector.tensor_tensor(chunk(chip.h_low, t, u), h32[u][:], chunk(chip.h_high, t, u), ALU.subtract)
                if router is not None:
                    for u in range(2):
                        dve.wait_ge(logit_ready, 2 * t + u + 1)
                        nc.vector.tensor_copy(logits[:, ds(t * 8 + u * 4, 4), :], logit[u][:])



UNITS = [(j, c) for j in range(SEQ // P) for c in range(2) if P * j < CHUNK * (c + 1)]
NU = len(UNITS)


def unit(u):
    j, c = UNITS[u]
    first = max(P * j, CHUNK * c)
    return j, c, first, CHUNK * (c + 1) - first, first == P * j


def row_jobs(s):
    return [("max", s, i, c) for i in range(SEQ // P) for c in range(2) if CHUNK * c <= P * i]


STEP_JOBS = [
    [("sum", 0), ("sum", 1), ("q", 0, 0), ("q", 0, 1), ("k", 0, 0)],
    [("k", 0, 1), ("q", 1, 0), ("q", 1, 1)],
    [("k", 1, 0), ("k", 1, 1), ("out", 0)],
    [("out", 1), ("v", 0)] + row_jobs(0)[0:1],
    row_jobs(0)[1:4],
    row_jobs(0)[4:8],
    row_jobs(0)[8:12],
    [("shift", 0, 0)] + row_jobs(1)[0:4],
    [("shift", 0, 1)] + row_jobs(1)[4:8],
    row_jobs(1)[8:12],
    [("v", 1)],
    [("shift", 1, 0), ("shift", 1, 1)],
]
CLOSING = ("sum", "out")


def slot_jobs(close, prepare):
    steps = [[x for x in step if (close if x[0] in CLOSING else prepare)] for step in STEP_JOBS]
    number = {}
    for step in steps:
        for x in step:
            number[x] = len(number)
    return steps, number


ALL_JOBS = len(slot_jobs(True, True)[1])
PREPARE_JOBS = len(slot_jobs(False, True)[1])
HIGHS = 8
BANKS = 4


class Job:

    def __init__(self, first, k, t, per_turn):
        n = first + k
        self.bank = n % BANKS
        self.before = n // BANKS + per_turn // BANKS * t
        self.done = n + 1 + per_turn * t


def attention0(nc, chip):
    SCALE = 1.0 / (float(np.sqrt(DH0)) * WS * WS)
    PER_TURN = 2 * ALL_JOBS
    assert PER_TURN % BANKS == 0
    with ExitStack() as ctx:
        def sb(name, shape, dt):
            return ctx.enter_context(nc.sbuf_tensor(name, shape, dt))

        def sem(name):
            return ctx.enter_context(nc.semaphore(name))

        def two(name, shape, dt):
            return [[sb(f"{name}{v}{s}", shape, dt) for s in range(2)] for v in range(2)]

        q_twice = two("q_twice", [P, SEQ], F16)
        q_low = two("q_low", [96, SEQ], F16)
        k_both = two("k_both", [P, SEQ], F16)
        k_high = two("k_high", [96, SEQ], F16)
        v = two("v", [P, SEQ // P, DH0], F32)
        total = two("total", [P, SEQ], F32)
        probs = two("probs", [P, CHUNK], F32)
        maxima = [sb(f"maxima{s}", [P, 2, 8], F32) for s in range(2)]
        minus_max = [sb(f"minus_max{s}", [P, 8, 32], F16) for s in range(2)]
        inverse = [sb(f"inverse{c}", [P, CHUNK], F32) for c in range(2)]
        normed = [sb(f"normed{c}", [P, CHUNK], F32) for c in range(2)]
        o_high = [sb(f"o_high{c}", [P, CHUNK], F16) for c in range(2)]
        o_low = [sb(f"o_low{c}", [P, CHUNK], F16) for c in range(2)]
        scores = [ctx.enter_context(nc.psum_tensor(f"scores{s}", [P, CHUNK], F32)) for s in range(2)]
        spare = [ctx.enter_context(nc.psum_tensor(f"spare{k}", [P, CHUNK], F32)) for k in range(BANKS)]
        o_psum = [ctx.enter_context(nc.psum_tensor(f"o{c}", [P, CHUNK], F32)) for c in range(2)]

        pads_clear, buffers_clear = sem("pads_clear"), sem("buffers_clear")
        job_ready = sem("job_ready")
        bank_free = [sem(f"bank_free{k}") for k in range(BANKS)]
        high_ready = sem("high_ready")
        split_ready = sem("split_ready")
        max_ready = sem("max_ready")
        minus_ready = sem("minus_ready")
        shift_ready = sem("shift_ready")
        score_ready = [sem(f"score_ready{s}") for s in range(2)]
        probs_ready = [sem(f"probs_ready{s}") for s in range(2)]
        pv_done = [sem(f"pv_done{s}") for s in range(2)]
        added = [sem(f"added{s}") for s in range(2)]
        inverse_ready, normed_ready = sem("inverse_ready"), sem("normed_ready")
        o_high_ready, o_low_ready = sem("o_high_ready"), sem("o_low_ready")
        block = ctx.enter_context(nc.Block())
        ADDS = NU - 2

        def where(i):
            return i // PAIRS, i % PAIRS

        def weights(half, t, s, pair):
            return chip.w_qk[:, half, ds(2 * pair + s, 1), t, :, :].rearrange("c h w e -> c (h w e)")

        def bias(t, s, pair):
            return chip.bqk[:, ds(t * HEADS0 + 2 * pair + s, 1)]

        def tokens(a, batch, first, n):
            return a[:, ds(batch * SEQ + first, n)]

        def whole(run, slot):
            slot(-1, 1, 0, 0, False, True, False)
            slot(0, 0, 0, PREPARE_JOBS, False, True, True)
            first = 2 * PREPARE_JOBS
            with run.Fori(0, BATCH * PAIRS // 2 - 1) as t:
                slot(2 * t + 1, 1, t, first, True, True, True)
                slot(2 * t + 2, 0, t, first + ALL_JOBS, True, True, True)
            done = first + PER_TURN * (BATCH * PAIRS // 2 - 1)
            closing = ALL_JOBS - PREPARE_JOBS
            slot(BATCH * PAIRS - 1, 1, 0, done, True, False, True)
            slot(BATCH * PAIRS, 0, 0, done + closing, True, False, False)

        @block.tensor
        def _(pe):
            pe.wait_ge(buffers_clear, 1)

            def product(out, high, low, x_high, x_low):
                pe.matmul(out, high, x_high, start=True, stop=False)
                pe.matmul(out, low, x_high, start=False, stop=False)
                return pe.matmul(out, high, x_low, start=False, stop=True)

            def run_job(x, job, i, parity):
                out = spare[job.bank]
                nxt, n_par = i + 1, 1 - parity
                pe.wait_ge(bank_free[job.bank], job.before)
                if x[0] in ("q", "k"):
                    batch, pair = where(nxt)
                    _, s, c = x
                    t = 0 if x[0] == "q" else 1
                    ins = product(out[:], weights(0, t, s, pair), weights(1, t, s, pair),
                                  tokens(chip.h_high, batch, c * CHUNK, CHUNK), tokens(chip.h_low, batch, c * CHUNK, CHUNK))
                elif x[0] == "v":
                    batch, pair = where(nxt)
                    _, s = x
                    wv = [chip.w_v[:, half, ds((2 * pair + s) * DH0, DH0)] for half in range(2)]
                    for k in range(SEQ // P):
                        h_high, h_low = (tokens(h, batch, k * P, P) for h in (chip.h_high, chip.h_low))
                        o = out[:, k * DH0:(k + 1) * DH0]
                        pe.matmul(o, h_high, wv[0], start=True, stop=False)
                        pe.matmul(o, h_high, wv[1], start=False, stop=False)
                        ins = pe.matmul(o, h_low, wv[0], start=False, stop=True)
                elif x[0] == "max":
                    _, s, k, c = x
                    if (k, c) == (0, 0):
                        pe.wait_ge(split_ready, 4 * nxt + 2 * s + 2)
                    n = min(P * (k + 1) - CHUNK * c, CHUNK)
                    diagonal = c == k // 4
                    ins = pe.matmul(out[:, 0:n], q_twice[n_par][s][:, k * P:(k + 1) * P], k_both[n_par][s][:, c * CHUNK:c * CHUNK + n],
                                    start=True, stop=not diagonal)
                    if diagonal:
                        ins = pe.matmul(out[:, n - P:n], chip.identb[:], chip.mask_qk[:], start=False, stop=True)
                elif x[0] == "shift":
                    _, s, c = x
                    pe.wait_ge(minus_ready, 2 * nxt + s + 1)
                    for k in range(4):
                        ins = pe.matmul(out[64:96, k * P:(k + 1) * P], minus_max[s][:, 4 * c + k, :], chip.ident16[:],
                                        start=True, stop=True)
                elif x[0] == "sum":
                    _, c = x
                    for s in range(2):
                        pe.wait_ge(added[s], ADDS * i)
                        ins = pe.matmul(out[64 * s:64 * s + 64, :], chip.sum_ones[:], total[n_par][s][:, c * CHUNK:(c + 1) * CHUNK],
                                        start=True, stop=True)
                else:
                    _, c = x
                    _, pair = where(i - 1)
                    pe.wait_ge(o_low_ready, 2 * (i - 1) + c + 1)
                    wo = [chip.w_out[:, half, ds(pair, 1), :].rearrange("p a c -> p (a c)") for half in range(2)]
                    ins = product(out[:], wo[0], wo[1], o_high[c][:], o_low[c][:])
                ins.then_inc(job_ready, 1)

            def slot(i, parity, t, first, close, prepare, attend):
                steps, number = slot_jobs(close, prepare)
                if attend:
                    pe.wait_ge(shift_ready, i + 1)
                for u in range(NU):
                    j, c, q0, n, diagonal = unit(u)
                    for s in range(2):
                        if not attend:
                            break
                        pe.wait_ge(probs_ready[s], NU * i + u)
                        pe.matmul(scores[s][:, 0:n], k_both[parity][s][:, j * P:(j + 1) * P], q_twice[parity][s][:, q0:q0 + n],
                                  start=True, stop=False)
                        ins = pe.matmul(scores[s][:, 0:n], k_high[parity][s][:, j * P:(j + 1) * P], q_low[parity][s][:, q0:q0 + n],
                                        start=False, stop=not diagonal)
                        if diagonal:
                            ins = pe.matmul(scores[s][:, 0:P], chip.identb[:], chip.mask_kq[:], start=False, stop=True)
                        ins.then_inc(score_ready[s], 1)
                    for x in steps[u]:
                        run_job(x, Job(first, number[x], t, PER_TURN), i, parity)
                    if attend:
                        if close and u < 2:
                            pe.wait_ge(normed_ready, 2 * (i - 1) + u + 1)
                        for s in range(2):
                            pe.wait_ge(probs_ready[s], NU * i + u + 1)
                            p = total[parity][s][:, c * CHUNK:(c + 1) * CHUNK] if u < 2 else probs[u % 2][s][:, 0:n]
                            pe.matmul(o_psum[c][64 * s:64 * s + 64, q0 - c * CHUNK:q0 - c * CHUNK + n], v[parity][s][:, j, :], p,
                                      start=(j == 0), stop=(j == 4 * c + 3)).then_inc(pv_done[s], 1)

            whole(pe, slot)

        @block.scalar
        def _(act):
            def run_job(x, job, i, parity):
                nxt, n_par = i + 1, 1 - parity
                src = spare[job.bank]
                if x[0] in ("q", "k"):
                    _, pair = where(nxt)
                    _, s, c = x
                    t = 0 if x[0] == "q" else 1
                    out = (q_twice if t == 0 else k_both)[n_par][s]
                    act.wait_ge(job_ready, job.done)
                    apart(act, chip)
                    nc.scalar.activation(out[:, c * CHUNK:(c + 1) * CHUNK], src[:], ACT.Identity, bias=bias(t, s, pair))\
                        .then_inc(high_ready, 1)
                elif x[0] == "v":
                    act.wait_ge(job_ready, job.done)
                    nc.scalar.copy(v[n_par][x[1]][:], src[:].rearrange("p (k e) -> p k e", e=DH0)).then_inc(bank_free[job.bank], 1)
                elif x[0] == "shift":
                    _, s, c = x
                    act.wait_ge(job_ready, job.done)
                    nc.scalar.copy(q_low[n_par][s][64:96, c * CHUNK:(c + 1) * CHUNK], src[64:96, :]).then_inc(bank_free[job.bank], 1)
                    if (s, c) == (1, 1):
                        act.wait_ge(bank_free[job.bank], job.before + 1)
                        act.sem_inc(shift_ready, 1)

            def slot(i, parity, t, first, close, prepare, attend):
                steps, number = slot_jobs(close, prepare)
                for u in range(NU):
                    _, c, _, n, _ = unit(u)
                    for s in range(2):
                        if not attend:
                            break
                        if u in (2, 3):
                            act.wait_ge(added[s], ADDS * i)
                        if u >= 4:
                            act.wait_ge(pv_done[s], NU * i + u - 1)
                            act.wait_ge(added[s], ADDS * i + u - 3)
                        act.wait_ge(score_ready[s], NU * i + u + 1)
                        out = total[parity][s][:, c * CHUNK:(c + 1) * CHUNK] if u < 2 else probs[u % 2][s][:, 0:n]
                        nc.scalar.activation(out, scores[s][:, 0:n], ACT.Exp, scale=SCALE).then_inc(probs_ready[s], 1)
                    for x in steps[u]:
                        run_job(x, Job(first, number[x], t, PER_TURN), i, parity)
                    if close and u in (1, 2):
                        c = u - 1
                        _, pair = where(i - 1)
                        act.wait_ge(normed_ready, 2 * (i - 1) + c + 1)
                        apart(act, chip)
                        nc.scalar.activation(o_high[c][:], normed[c][:], ACT.Identity, bias=chip.bv0[:, ds(pair, 1)])\
                            .then_inc(o_high_ready, 1)

            whole(act, slot)

        @block.gpsimd
        def _(pool):
            for par in range(2):
                for s in range(2):
                    nc.gpsimd.memset(q_low[par][s][64:96, :], 0.0)
                    nc.gpsimd.memset(k_high[par][s][64:96, :], 0.0).then_inc(pads_clear, 1)
            pool.wait_ge(pads_clear, 4)
            for par in range(2):
                for s in range(2):
                    nc.gpsimd.memset(k_high[par][s][64:65, :], SH).then_inc(pads_clear, 1)
            pool.wait_ge(pads_clear, 8)
            for s in range(2):
                ins = nc.gpsimd.memset(minus_max[s][:], 0.0)
            ins.then_inc(buffers_clear, 1)

            def slot(i, parity, t, first, close, prepare, attend):
                if not attend:
                    return
                for u in range(2, NU):
                    _, _, q0, n, _ = unit(u)
                    for s in range(2):
                        if u == 2:
                            pool.wait_ge(pv_done[s], NU * i + 2)
                        pool.wait_ge(added[s], ADDS * i + u - 2)
                        pool.wait_ge(probs_ready[s], NU * i + u + 1)
                        acc = total[parity][s][:, q0:q0 + n]
                        nc.gpsimd.tensor_tensor(acc, acc, probs[u % 2][s][:, 0:n], ALU.add).then_inc(added[s], 1)

            whole(pool, slot)

        @block.vector
        def _(dve):
            dve.wait_ge(buffers_clear, 1)

            def run_job(x, job, i, parity, number, jobs_of):
                nxt, n_par = i + 1, 1 - parity
                src = spare[job.bank]
                if x[0] in ("q", "k"):
                    _, pair = where(nxt)
                    _, s, c = x
                    at = slice(c * CHUNK, (c + 1) * CHUNK)
                    t = 0 if x[0] == "q" else 1
                    k = [y for y in number if y[0] in ("q", "k")].index(x)
                    dve.wait_ge(high_ready, HIGHS * nxt + k + 1)
                    if t == 0:
                        nc.vector.scalar_tensor_tensor(q_low[n_par][s][0:64, at], src[0:64, :], chip.bqk[0:64, ds(2 * pair + s, 1)],
                                                       q_twice[n_par][s][0:64, at], ALU.add, ALU.subtract)\
                            .then_inc(bank_free[job.bank], 1)
                    else:
                        low = k_both[n_par][s][64:128, at]
                        nc.vector.scalar_tensor_tensor(low, src[64:128, :], chip.bqk[64:128, ds(HEADS0 + 2 * pair + s, 1)], low,
                                                       ALU.add, ALU.subtract).then_inc(bank_free[job.bank], 1)
                        nc.vector.tensor_copy(k_high[n_par][s][0:64, at], k_both[n_par][s][0:64, at]).then_inc(split_ready, 1)
                elif x[0] == "max":
                    _, s, k, c = x
                    n = min(P * (k + 1) - CHUNK * c, CHUNK)
                    dve.wait_ge(job_ready, job.done)
                    nc.vector.tensor_reduce(maxima[s][:, c, k:k + 1], src[:, 0:n], AX_X, ALU.max).then_inc(bank_free[job.bank], 1)
                    if (k, c) == (7, 1):
                        dve.wait_ge(bank_free[job.bank], job.before + 1)
                        nc.vector.tensor_tensor(maxima[s][:, 0, 4:8], maxima[s][:, 0, 4:8], maxima[s][:, 1, 4:8], ALU.max)\
                            .then_inc(max_ready, 1)
                        dve.wait_ge(max_ready, 2 * nxt + s + 1)
                        nc.vector.tensor_scalar(minus_max[s][:, :, 0:1], maxima[s][:, 0, :].unsqueeze(2), -1.0 / SH, None, ALU.mult)\
                            .then_inc(minus_ready, 1)
                elif x[0] == "sum":
                    _, c = x
                    dve.wait_ge(job_ready, job.done)
                    nc.vector.reciprocal(inverse[c][:], src[:]).then_inc(bank_free[job.bank], 1)
                    dve.wait_ge(bank_free[job.bank], job.before + 1)
                    nc.vector.tensor_tensor(normed[c][:], o_psum[c][:], inverse[c][:], ALU.mult).then_inc(normed_ready, 1)
                elif x[0] == "out":
                    _, c = x
                    batch, _ = where(i - 1)
                    dve.wait_ge(job_ready, job.done)
                    here = tokens(chip.xT, batch, c * CHUNK, CHUNK)
                    nc.vector.scalar_tensor_tensor(here, src[:], chip.ga_scaled[:, ds(batch, 1)], here, ALU.mult, ALU.add)\
                        .then_inc(bank_free[job.bank], 1)

            def slot(i, parity, t, first, close, prepare, attend):
                steps, number = slot_jobs(close, prepare)
                for u in range(NU):
                    for x in steps[u]:
                        run_job(x, Job(first, number[x], t, PER_TURN), i, parity, number, None)
                    if close and u in (1, 2):
                        c = u - 1
                        _, pair = where(i - 1)
                        dve.wait_ge(o_high_ready, 2 * (i - 1) + c + 1)
                        nc.vector.scalar_tensor_tensor(o_low[c][:], normed[c][:], chip.bv0[:, ds(pair, 1)], o_high[c][:],
                                                       ALU.add, ALU.subtract).then_inc(o_low_ready, 1)

            whole(dve, slot)


def gates(nc, chip, layer):
    with ExitStack() as ctx:
        def sb(what, shape, dt):
            return ctx.enter_context(nc.sbuf_tensor(f"gates{layer}_{what}", shape, dt))

        def sem(what):
            return ctx.enter_context(nc.semaphore(f"gates{layer}_{what}"))

        logits = chip.logits
        gate, rest = sb("gate", [P, NTILE, EXPERTS], F32), sb("rest", [P, NTILE, EXPERTS], F32)
        parts = sb("parts", [P, NTILE, 3, EXPERTS], BF16)
        turned = [ctx.enter_context(nc.psum_tensor(f"gates{layer}_turned{k}", [3 * EXPERTS, 8 * P], BF16)) for k in range(4)]
        chain, parts_ready, turned_ready = sem("chain"), sem("parts_ready"), sem("turned_ready")
        if layer == 0:
            below, count, passed = sb("below", [P, NTILE * EXPERTS], F32), sb("count", [P, 1], F32), sb("passed", [P, 1], I32)
            key, bit, trial, flip, bound = (sb(w, [P, 1], I32) for w in ("key", "bit", "trial", "flip", "bound"))
            number = ctx.enter_context(nc.psum_tensor("gates0_number", [P, 1], F32))
            state_ready, trial_ready, flip_ready, bound_ready = (
                sem(w) for w in ("state_ready", "trial_ready", "flip_ready", "bound_ready"))
            counted, summed, passed_ready = sem("counted"), sem("summed"), sem("passed_ready")
        else:
            shifted, powers, ready = sb("shifted", [P, NTILE, EXPERTS], F32), sem("powers"), sem("ready")
            one, first, second = (sb(w, [P, NTILE, EXPERTS], F32) for w in ("one", "first", "second"))
            stat = sb("stat", [P, NTILE], F32)
        block = ctx.enter_context(nc.Block())

        @block.vector
        def _(dve):
            link = Link(dve, chain)
            if layer == 0:
                flat = logits[:].rearrange("p t e -> p (t e)")
                nc.vector.memset(key[:], 0)
                nc.vector.memset(bit[:], -(1 << 31)).then_inc(state_ready, 1)
                with dve.Fori(0, 32) as t:
                    dve.wait_ge(state_ready, t + 1)
                    nc.vector.tensor_tensor(trial[:], key[:], bit[:], ALU.bitwise_or).then_inc(trial_ready, 1)
                    dve.wait_ge(trial_ready, t + 1)
                    nc.vector.tensor_scalar(flip[:], trial[:], 31, 0x7FFFFFFF, ALU.arith_shift_right, ALU.bitwise_and)\
                        .then_inc(flip_ready, 1)
                    dve.wait_ge(flip_ready, t + 1)
                    nc.vector.scalar_tensor_tensor(bound[:], flip[:], -1, trial[:], ALU.bitwise_xor, ALU.bitwise_xor)\
                        .then_inc(bound_ready, 1)
                    dve.wait_ge(bound_ready, t + 1)
                    nc.vector.tensor_scalar(below[:], flat, bound[:].bitcast(F32), 0.0, ALU.is_lt, ALU.add, accum_out=count[:])\
                        .then_inc(counted, 1)
                    dve.wait_ge(summed, t + 1)
                    nc.vector.tensor_scalar(passed[:], number[:], float(KTH - 1), None, ALU.is_le).then_inc(passed_ready, 1)
                    dve.wait_ge(passed_ready, t + 1)
                    apart(dve, chip)
                    nc.vector.copy_predicated(key[:], passed[:], trial[:])
                    nc.vector.tensor_scalar(bit[:], bit[:], 1, None, ALU.logical_shift_right).then_inc(state_ready, 1)
                dve.wait_ge(state_ready, 33)
                link(nc.vector.tensor_scalar(flip[:], key[:], 31, 0x7FFFFFFF, ALU.arith_shift_right, ALU.bitwise_and))
                link(nc.vector.scalar_tensor_tensor(bound[:], flip[:], -1, key[:], ALU.bitwise_xor, ALU.bitwise_xor))
                link(nc.vector.scalar_tensor_tensor(gate[:], logits[:], bound[:].bitcast(F32), logits[:], ALU.is_ge, ALU.mult))
            else:
                def spread(a):
                    return a.unsqueeze(2).broadcast_to([P, NTILE, EXPERTS])

                link(nc.vector.tensor_reduce(stat[:], logits[:], AX_X, ALU.max))
                nc.vector.tensor_tensor(shifted[:], logits[:], spread(stat[:]), ALU.subtract).then_inc(ready, 1)
                dve.wait_ge(powers, 1)
                link(nc.vector.tensor_reduce(stat[:], one[:], AX_X, ALU.add))
                link(nc.vector.reciprocal(stat[:], stat[:]))
                link(nc.vector.tensor_tensor(shifted[:], one[:], spread(stat[:]), ALU.mult))
                at, n = CONST["prefer"]
                prefer = chip.consts[:, at:at + n].unsqueeze(1).broadcast_to([P, NTILE, EXPERTS])
                left = shifted
                for mark in (first, second):
                    link(nc.vector.tensor_reduce(stat[:], left[:], AX_X, ALU.max))
                    link(nc.vector.tensor_tensor(one[:], left[:], spread(stat[:]), ALU.is_equal))
                    link(nc.vector.tensor_tensor(one[:], one[:], prefer, ALU.mult))
                    link(nc.vector.tensor_reduce(stat[:], one[:], AX_X, ALU.max))
                    link(nc.vector.tensor_tensor(mark[:], one[:], spread(stat[:]), ALU.is_equal))
                    if mark is first:
                        link(nc.vector.scalar_tensor_tensor(rest[:], first[:], -2.0, shifted[:], ALU.mult, ALU.add))
                        left = rest
                link(nc.vector.tensor_tensor(one[:], first[:], second[:], ALU.add))
                link(nc.vector.tensor_tensor(one[:], one[:], shifted[:], ALU.mult))
                link(nc.vector.tensor_reduce(stat[:], one[:], AX_X, ALU.add))
                link(nc.vector.reciprocal(stat[:], stat[:]))
                link(nc.vector.tensor_tensor(gate[:], one[:], spread(stat[:]), ALU.mult))
            link(nc.vector.tensor_copy(parts[:, :, 0, :], gate[:]))
            link(nc.vector.tensor_tensor(rest[:], gate[:], parts[:, :, 0, :], ALU.subtract))
            link(nc.vector.tensor_copy(parts[:, :, 1, :], rest[:]))
            nc.vector.tensor_tensor(parts[:, :, 2, :], rest[:], parts[:, :, 1, :], ALU.subtract).then_inc(parts_ready, 1)
            for k in range(4):
                dve.wait_ge(turned_ready, k + 1)
                nc.vector.tensor_copy(chip.gates_f32[:, k * SEQ:(k + 1) * SEQ], turned[k][:])
                ins = nc.vector.tensor_copy(chip.gates_b16[:, k * SEQ:(k + 1) * SEQ], turned[k][:])
            link(ins)

        @block.scalar
        def _(act):
            if layer == 1:
                act.wait_ge(ready, 1)
                nc.scalar.activation(one[:], shifted[:], ACT.Exp).then_inc(powers, 1)

        @block.tensor
        def _(pe):
            if layer == 0:
                with pe.Fori(0, 32) as t:
                    pe.wait_ge(counted, t + 1)
                    pe.matmul(number[:], chip.ones[:], count[:], start=True, stop=True).then_inc(summed, 1)
            pe.wait_ge(parts_ready, 1)
            for k in range(4):
                for i in range(8):
                    ins = pe.transpose(turned[k][:, i * P:(i + 1) * P], parts[:, 8 * k + i, :, :].rearrange("p a e -> p (a e)"), chip.identb[:])
                ins.then_inc(turned_ready, 1)


def experts(nc, chip, layer, w_up, w_down, bias_name, bias_rows, ungated):
    TILES = EXPERTS * HT + ungated
    GATED = EXPERTS * HT
    RING = 4
    with ExitStack() as ctx:
        def sem(what):
            return ctx.enter_context(nc.semaphore(f"experts{layer}_{what}"))

        hidden = [ctx.enter_context(nc.psum_tensor(f"hidden{layer}_{k}", [P, CHUNK], F32)) for k in range(RING)]
        gate = [ctx.enter_context(nc.psum_tensor(f"gate{layer}_{k}", [P, CHUNK], F32)) for k in range(2)]
        y = ctx.enter_context(nc.psum_tensor(f"y{layer}", [P, CHUNK], F32))
        active = [ctx.enter_context(nc.sbuf_tensor(f"active{layer}_{k}", [P, CHUNK], F32)) for k in range(RING)]
        weighed = [ctx.enter_context(nc.sbuf_tensor(f"weighed{layer}_{k}", [P, CHUNK], F32)) for k in range(RING)]
        up_ready, gate_ready, active_ready, weighed_ready = sem("up_ready"), sem("gate_ready"), sem("active_ready"), sem("weighed_ready")
        down_done, y_ready, y_taken = sem("down_done"), sem("y_ready"), sem("y_taken")
        x_biased = sem("x_biased")
        block = ctx.enter_context(nc.Block())

        @block.tensor
        def _(pe):
            with pe.Fori(0, NCHUNK) as n:
                h_high, h_low = (h[:, ds(n * CHUNK, CHUNK)] for h in (chip.h_high, chip.h_low))

                def up(k):
                    if k >= RING:
                        pe.wait_ge(active_ready, n * TILES + k - RING + 1)
                    pe.matmul(hidden[k % RING][:], w_up[:, 0, k, :], h_high, start=True, stop=False)
                    pe.matmul(hidden[k % RING][:], w_up[:, 1, k, :], h_high, start=False, stop=False)
                    pe.matmul(hidden[k % RING][:], w_up[:, 0, k, :], h_low, start=False, stop=True).then_inc(up_ready, 1)

                def spread_gate(e):
                    if e >= 2:
                        pe.wait_ge(weighed_ready, n * GATED + HT * (e - 1))
                    apart(pe, chip)
                    pe.matmul(gate[e % 2][:], chip.gate_sel[:, e * P:(e + 1) * P], chip.gates_b16[:, ds(n * CHUNK, CHUNK)],
                              start=True, stop=True).then_inc(gate_ready, 1)

                for k in range(RING - 1):
                    up(k)
                spread_gate(0)
                for k in range(TILES):
                    if k + RING - 1 < TILES:
                        up(k + RING - 1)
                    ahead = k + 2 - ungated
                    if ahead >= HT and ahead % HT == 0 and ahead // HT < EXPERTS:
                        spread_gate(ahead // HT)
                    if k == 0:
                        pe.wait_ge(y_taken, n)
                    if k < ungated:
                        pe.wait_ge(active_ready, n * TILES + k + 1)
                        src = active[k % RING]
                    else:
                        pe.wait_ge(weighed_ready, n * GATED + k - ungated + 1)
                        src = weighed[k % RING]
                    pe.matmul(y[:], w_down[:, k, :], src[:], start=(k == 0), stop=False).then_inc(down_done, 1)
                pe.matmul(y[:], bias_rows[:], chip.gates_f32[:, ds(n * CHUNK, CHUNK)], start=False, stop=True).then_inc(y_ready, 1)

        @block.scalar
        def _(act):
            with act.Fori(0, NCHUNK) as n:
                for k in range(TILES):
                    if k >= RING:
                        if k - RING < ungated:
                            act.wait_ge(down_done, n * TILES + k - RING + 1)
                        else:
                            act.wait_ge(weighed_ready, n * GATED + k - RING - ungated + 1)
                    act.wait_ge(up_ready, n * TILES + k + 1)
                    nc.scalar.activation(active[k % RING][:], hidden[k % RING][:], ACT.Gelu_apprx_tanh, bias=col(chip, bias_name, k),
                                         scale=1.0 / WS).then_inc(active_ready, 1)

        @block.vector
        def _(dve):
            with dve.Fori(0, NCHUNK) as n:
                here = chip.xT[:, ds(n * CHUNK, CHUNK)]
                if layer == 1:
                    nc.vector.tensor_scalar(here, here, chip.g_bias[:, 2, ds(n // 2, 1)], None, ALU.add).then_inc(x_biased, 1)
                for k in range(ungated, TILES):
                    e = (k - ungated) // HT
                    if (k - ungated) % HT == 0:
                        dve.wait_ge(gate_ready, n * EXPERTS + e + 1)
                    if k >= ungated + RING:
                        dve.wait_ge(down_done, n * TILES + k - RING + 1)
                    dve.wait_ge(active_ready, n * TILES + k + 1)
                    nc.vector.tensor_tensor(weighed[k % RING][:], active[k % RING][:], gate[e % 2][:], ALU.mult).then_inc(weighed_ready, 1)
                dve.wait_ge(y_ready, n + 1)
                if layer == 1:
                    dve.wait_ge(x_biased, n + 1)
                nc.vector.scalar_tensor_tensor(here, y[:], chip.mod[:, layer, GB, ds(n // 2, 1)], here, ALU.mult, ALU.add)\
                    .then_inc(y_taken, 1)


def project1(nc, chip, dram):
    with ExitStack() as ctx:
        def sb(name, shape, dt):
            return ctx.enter_context(nc.sbuf_tensor(name, shape, dt))

        def sem(name):
            return ctx.enter_context(nc.semaphore(name))

        Q, K, V, QR, KR = range(5)
        raw = sb("w1_attn", [P, 5, CH], F32)
        w = sb("w1_attn_split", [P, 2, 5, CH], F16)
        straight = [[sb(f"straight{x}{u}", [P, CHUNK], F32) for u in range(2)] for x in range(2)]
        turned = [[sb(f"turned{x}{u}", [P, CHUNK], F32) for u in range(2)] for x in range(2)]
        psum = [ctx.enter_context(nc.psum_tensor(f"project{k}", [P, CHUNK], F32)) for k in range(8)]
        chain, split_ready, project_ready, value_taken = sem("project_chain"), sem("project_split"), sem("project_ready"), sem("value_taken")
        straight_ready, turned_ready, rotated, high_ready = sem("straight_ready"), sem("turned1_ready"), sem("rotated"), sem("high1_ready")
        block = ctx.enter_context(nc.Block())
        highs = (chip.q1[0], chip.k1[0])
        lows = (chip.q1[1], chip.k1[1])

        @block.tensor
        def _(pe):
            pe.wait_ge(split_ready, 1)
            with pe.Fori(0, BATCH) as t:
                for u in range(2):
                    at = ds(t * SEQ + u * CHUNK, CHUNK)
                    for x in range(2):
                        for part, k in enumerate(((Q, QR), (K, KR))[x]):
                            out = psum[4 * u + 2 * x + part][:]
                            pe.wait_ge(rotated, 4 * t)
                            pe.matmul(out, w[:, 0, k, :], chip.h_high[:, at], start=True, stop=False)
                            pe.matmul(out, w[:, 1, k, :], chip.h_high[:, at], start=False, stop=False)
                            pe.matmul(out, w[:, 0, k, :], chip.h_low[:, at], start=False, stop=True).then_inc(project_ready, 1)

        @block.scalar
        def _(act):
            with act.Fori(0, BATCH) as t:
                for u in range(2):
                    for x in range(2):
                        act.wait_ge(rotated, 4 * t + 2 * u + x + 1)
                        apart(act, chip)
                        nc.scalar.copy(highs[x][:, ds(t * SEQ + u * CHUNK, CHUNK)], straight[x][u][:]).then_inc(high_ready, 1)

        @block.vector
        def _(dve):
            link = Link(dve, chain)
            link(nc.vector.tensor_copy(raw[:, 0:3, :], chip.w1_attn_raw[:]))
            for x in range(2):
                src = raw[:, x, :].rearrange("c (i two) -> c i two", two=2)
                dst = raw[:, QR + x, :].rearrange("c (i two) -> c i two", two=2)
                link(nc.vector.tensor_scalar(dst[:, :, 0:1], src[:, :, 1:2], -1.0, None, ALU.mult))
                link(nc.vector.tensor_copy(dst[:, :, 1:2], src[:, :, 0:1]))
            link(nc.vector.tensor_scalar(w[:, 0, :, :], raw[:], WS, None, ALU.mult))
            nc.vector.scalar_tensor_tensor(w[:, 1, :, :], raw[:], WS, w[:, 0, :, :], ALU.mult, ALU.subtract).then_inc(split_ready, 1)
            with dve.Fori(0, BATCH) as t:
                for u in range(2):
                    at = CONST["cos"][0] + u * CHUNK
                    cos = chip.consts[:, at:at + CHUNK]
                    at = CONST["sin"][0] + u * CHUNK
                    sin = chip.consts[:, at:at + CHUNK]
                    for x in range(2):
                        dve.wait_ge(project_ready, 8 * t + 4 * u + 2 * x + 1)
                        nc.vector.scalar_tensor_tensor(straight[x][u][:], psum[4 * u + 2 * x][:], chip.bqk1[:, x:x + 1], cos, ALU.add, ALU.mult)\
                            .then_inc(straight_ready, 1)
                        dve.wait_ge(project_ready, 8 * t + 4 * u + 2 * x + 2)
                        nc.vector.scalar_tensor_tensor(turned[x][u][:], psum[4 * u + 2 * x + 1][:], chip.bqk1[:, 2 + x:3 + x], sin, ALU.add, ALU.mult)\
                            .then_inc(turned_ready, 1)
                    for x in range(2):
                        dve.wait_ge(turned_ready, 4 * t + 2 * u + x + 1)
                        dve.wait_ge(straight_ready, 4 * t + 2 * u + x + 1)
                        nc.vector.tensor_tensor(straight[x][u][:], straight[x][u][:], turned[x][u][:], ALU.add).then_inc(rotated, 1)
                    for x in range(2):
                        dve.wait_ge(high_ready, 4 * t + 2 * u + x + 1)
                        chunk = ds(t * SEQ + u * CHUNK, CHUNK)
                        nc.vector.tensor_tensor(lows[x][:, chunk], straight[x][u][:], highs[x][:, chunk], ALU.subtract)

    with ExitStack() as ctx:
        psum = [ctx.enter_context(nc.psum_tensor(f"value_rows{k}", [P, CHUNK], F32)) for k in range(2)]
        w = ctx.enter_context(nc.sbuf_tensor("wv1_split", [P, 2, CH], F16))
        v_split, v_ready, v_taken = (ctx.enter_context(nc.semaphore(x)) for x in ("v_split", "v_ready", "v_taken"))
        block = ctx.enter_context(nc.Block())

        @block.tensor
        def _(pe):
            pe.wait_ge(v_split, 2)
            for n in range(NCHUNK):
                if n >= 2:
                    pe.wait_ge(v_taken, n - 1)
                for i in range(4):
                    out = psum[n % 2][:, i * P:(i + 1) * P]
                    at = n * CHUNK + i * P
                    pe.matmul(out, chip.h_high[:, at:at + P], w[:, 0, :], start=True, stop=False)
                    pe.matmul(out, chip.h_high[:, at:at + P], w[:, 1, :], start=False, stop=False)
                    ins = pe.matmul(out, chip.h_low[:, at:at + P], w[:, 0, :], start=False, stop=True)
                ins.then_inc(v_ready, 1)

        @block.scalar
        def _(act):
            for n in range(NCHUNK):
                act.wait_ge(v_ready, n + 1)
                nc.scalar.copy(chip.v1[:, 4 * n:4 * n + 4, :], psum[n % 2][:].rearrange("p (a b) -> p a b", a=4)).then_inc(v_taken, 1)

        @block.vector
        def _(dve):
            nc.vector.tensor_scalar(w[:, 0, :], chip.w1_attn_raw[:, 2, :], WS, None, ALU.mult).then_inc(v_split, 1)
            dve.wait_ge(v_split, 1)
            nc.vector.scalar_tensor_tensor(w[:, 1, :], chip.w1_attn_raw[:, 2, :], WS, w[:, 0, :], ALU.mult, ALU.subtract).then_inc(v_split, 1)


STEPS1 = 2 * (SEQ // P)
MAX_JOBS = [("max", j, k) for j in range(4) for k in range(SEQ // P)]
STEP_JOBS1 = [[("xq",), ("xk",)]] + [[] for _ in range(14)] + [[("shift",)]]
for _n, _x in enumerate(MAX_JOBS):
    STEP_JOBS1[1 + _n * 13 // len(MAX_JOBS)].append(_x)
JOBS1 = {}
for _step in STEP_JOBS1:
    for _x in _step:
        JOBS1[_x] = len(JOBS1)
PER_QUAD = len(JOBS1)
CLOSE_JOBS = 2


def attention1(nc, chip):
    SCALE = 1.0 / (float(np.sqrt(DH1)) * WS * WS)
    PER_TURN = QUADS * PER_QUAD + CLOSE_JOBS
    UNITS1 = 4 * STEPS1
    assert PER_TURN % 2 == 0
    with ExitStack() as ctx:
        def sb(name, shape, dt):
            return ctx.enter_context(nc.sbuf_tensor(name, shape, dt))

        def sem(name):
            return ctx.enter_context(nc.semaphore(name))

        xq = [sb(f"xq{v}", [P, SEQ], F16) for v in range(2)]
        xq_shift = [sb(f"xq_shift{v}", [P, SEQ], F16) for v in range(2)]
        xk = [sb(f"xk{v}", [P, SEQ], F16) for v in range(2)]
        values = [sb(f"values{v}", [P, SEQ // P, 4, 32], F32) for v in range(2)]
        probs = [[sb(f"probs1_{v}{j}", [P, CHUNK], F32) for j in range(4)] for v in range(2)]
        context = [sb(f"context{g}", [P, SEQ], F32) for g in range(QUADS)]
        maxima = sb("quad_maxima", [P, 4, SEQ // P], F32)
        minus_max = sb("quad_minus_max", [P, SEQ // P, P], F16)
        inverse = sb("quad_inverse", [P, SEQ], F32)
        normed = sb("quad_normed", [P, SEQ], F32)
        wide = [ctx.enter_context(nc.psum_tensor(f"wide{k}", [P, SEQ], F32)) for k in range(2)]
        scores = [ctx.enter_context(nc.psum_tensor(f"scores1_{k}", [P, CHUNK], F32)) for k in range(2)]
        o_psum = [ctx.enter_context(nc.psum_tensor(f"o1_{c}", [P, CHUNK], F32)) for c in range(2)]

        pads_clear, buffers_clear = sem("pads1_clear"), sem("buffers1_clear")
        job_ready = sem("job1_ready")
        wide_free = [sem(f"wide_free{k}") for k in range(2)]
        xk_ready, minus_ready, shift_ready = sem("xk_ready"), sem("minus1_ready"), sem("shift1_ready")
        values_ready = sem("values_ready")
        score_ready, probs_ready, pv_done = sem("score1_ready"), sem("probs1_ready"), sem("pv1_done")
        o_taken, inverse_ready, normed_ready = sem("o1_taken"), sem("inverse1_ready"), sem("normed1_ready")
        block = ctx.enter_context(nc.Block())

        class Job1:
            def __init__(self, first, k, t):
                n = first + k
                self.bank = n % 2
                self.before = n // 2 + PER_TURN // 2 * t
                self.done = n + 1 + PER_TURN * t

        def whole(run, slot, close):
            slot(0, -1, 0, 0, True, False)

            def batch(b, t, prepare_last):
                for g in range(QUADS):
                    slot(b, g, t, PER_QUAD * (g + 1), prepare_last or g < QUADS - 1, True)
                close(b, t, PER_QUAD * (QUADS + (1 if prepare_last else 0)))

            with run.Fori(0, BATCH - 1) as t:
                batch(t, t, True)
            batch(BATCH - 1, BATCH - 1, False)

        @block.tensor
        def _(pe):
            pe.wait_ge(buffers_clear, 1)

            def run_job(x, job, b, g):
                par = (g + 1) % 2
                out = wide[job.bank]
                nb, ng = (b + 1, 0) if g == QUADS - 1 else (b, g + 1)
                made = QUADS * b + g + 1
                pe.wait_ge(wide_free[job.bank], job.before)

                def spread(c, sel, x, last):
                    o = out[:, c * CHUNK:(c + 1) * CHUNK]
                    for half in range(2):
                        ins = pe.matmul(o, sel[:, (2 * ng + half) * P:(2 * ng + half + 1) * P], x[half][:, ds(nb * SEQ + c * CHUNK, CHUNK)],
                                        start=(half == 0), stop=(half == 1 and last))
                    return ins

                if x[0] == "xq":
                    spread(0, chip.q_sel, chip.q1, True)
                    ins = spread(1, chip.q_sel, chip.q1, True)
                elif x[0] == "xk":
                    spread(0, chip.k_sel, chip.k1, True)
                    ins = spread(1, chip.k_sel, chip.k1, True)
                elif x[0] == "max":
                    _, j, k = x
                    if (j, k) == (0, 0):
                        pe.wait_ge(xk_ready, made + 1)
                    for c in range(2):
                        ins = pe.matmul(out[:, c * CHUNK:(c + 1) * CHUNK], xq[par][32 * j:32 * j + 32, k * P:(k + 1) * P],
                                        xk[par][32 * j:32 * j + 32, c * CHUNK:(c + 1) * CHUNK], start=True, stop=True,
                                        tile_position=(32 * j, 0))
                else:
                    pe.wait_ge(minus_ready, made + 1)
                    for c in range(2):
                        spread(c, chip.q_sel, chip.q1, False)
                        for k in range(4):
                            at = c * CHUNK + k * P
                            ins = pe.matmul(out[:, at:at + P], minus_max[:, 4 * c + k, :], chip.ident16[:], start=False, stop=(k == 3))
                ins.then_inc(job_ready, 1)

            def pv(i, u, g):
                k, c = u // 2, u % 2
                if u < 2:
                    pe.wait_ge(o_taken, 2 * i)
                for j in range(4):
                    pe.wait_ge(probs_ready, UNITS1 * i + 4 * u + j + 1)
                    pe.matmul(o_psum[c][32 * j:32 * j + 32, :], values[g % 2][:, k, j, :], probs[u % 2][j][:],
                              start=(k == 0), stop=(k == SEQ // P - 1), tile_position=(0, 32 * j)).then_inc(pv_done, 1)

            def slot(b, g, t, first, prepare, attend):
                i = QUADS * b + g
                if attend:
                    pe.wait_ge(shift_ready, i + 1)
                    pe.wait_ge(values_ready, i + 1)
                for u in range(STEPS1):
                    k, c = u // 2, u % 2
                    jobs = STEP_JOBS1[u] if prepare else []
                    for j in range(4):
                        if attend:
                            pe.wait_ge(probs_ready, UNITS1 * i + max(4 * u + j - 1, 0))
                            pe.matmul(scores[j % 2][:], xk[g % 2][32 * j:32 * j + 32, k * P:(k + 1) * P],
                                      xq_shift[g % 2][32 * j:32 * j + 32, c * CHUNK:(c + 1) * CHUNK], start=True, stop=True,
                                      tile_position=(32 * j, 0)).then_inc(score_ready, 1)
                        if j % 2 and j // 2 < len(jobs):
                            x = jobs[j // 2]
                            run_job(x, Job1(first, JOBS1[x], t), b, g)
                    if attend and u > 0:
                        pv(i, u - 1, g)
                    for x in jobs[2:]:
                        run_job(x, Job1(first, JOBS1[x], t), b, g)
                if attend:
                    pv(i, STEPS1 - 1, g)

            def close(b, t, first):
                for n, name in enumerate(("place_ctx", "place_sum")):
                    job = Job1(first, n, t)
                    pe.wait_ge(wide_free[job.bank], job.before)
                    pe.wait_ge(o_taken, 2 * QUADS * (b + 1))
                    for c in range(2):
                        for g in range(QUADS):
                            ins = pe.matmul(wide[job.bank][32 * g:32 * g + 32, c * CHUNK:(c + 1) * CHUNK], const(chip, name),
                                            context[g][:, c * CHUNK:(c + 1) * CHUNK], start=True, stop=True, tile_position=(0, 32 * g))
                    ins.then_inc(job_ready, 1)

            whole(pe, slot, close)

        @block.scalar
        def _(act):
            def slot(b, g, t, first, prepare, attend):
                i = QUADS * b + g
                par = (g + 1) % 2
                for u in range(STEPS1):
                    for j in range(4):
                        if not attend:
                            break
                        if u >= 2:
                            act.wait_ge(pv_done, UNITS1 * i + 4 * (u - 2) + j + 1)
                        act.wait_ge(score_ready, UNITS1 * i + 4 * u + j + 1)
                        nc.scalar.activation(probs[u % 2][j][:], scores[j % 2][:], ACT.Exp, scale=SCALE).then_inc(probs_ready, 1)
                    for x in STEP_JOBS1[u] if prepare else []:
                        job = Job1(first, JOBS1[x], t)
                        if x[0] == "max":
                            continue
                        act.wait_ge(job_ready, job.done)
                        src = wide[job.bank][:]
                        if x[0] == "xq":
                            nc.scalar.copy(xq[par][:], src).then_inc(wide_free[job.bank], 1)
                        elif x[0] == "xk":
                            nc.scalar.activation(xk[par][:], src, ACT.Identity, bias=const(chip, "key_pad")).then_inc(wide_free[job.bank], 1)
                            act.wait_ge(wide_free[job.bank], job.before + 1)
                            act.sem_inc(xk_ready, 1)
                        else:
                            nc.scalar.copy(xq_shift[par][:], src).then_inc(wide_free[job.bank], 1)
                            act.wait_ge(wide_free[job.bank], job.before + 1)
                            act.sem_inc(shift_ready, 1)
                if attend:
                    for c in range(2):
                        act.wait_ge(pv_done, UNITS1 * i + 4 * (STEPS1 - 2 + c) + 4)
                        nc.scalar.copy(context[g][:, c * CHUNK:(c + 1) * CHUNK], o_psum[c][:]).then_inc(o_taken, 1)

            def close(b, t, first):
                pass

            whole(act, slot, close)

        @block.gpsimd
        def _(pool):
            for v in range(2):
                ins = nc.gpsimd.memset(values[v][:], 0.0).then_inc(pads_clear, 1)
            pool.wait_ge(pads_clear, 2)
            for v in range(2):
                nc.gpsimd.memset(values[v][:, :, :, DH1:DH1 + 1], WS).then_inc(pads_clear, 1)
            nc.gpsimd.memset(minus_max[:], 0.0).then_inc(pads_clear, 1)
            pool.wait_ge(pads_clear, 5)
            pool.sem_inc(buffers_clear, 1)

            def slot(b, g, t, first, prepare, attend):
                if not prepare:
                    return
                nb, ng = (b + 1, 0) if g == QUADS - 1 else (b, g + 1)
                par = (g + 1) % 2
                pool.wait_ge(job_ready, Job1(first, 0, t).done)
                apart(pool, chip)
                src = chip.v1[:, ds(8 * nb, 8), 32 * ng:32 * ng + 32].rearrange("p k (j d) -> p k j d", j=4)
                nc.gpsimd.tensor_copy(values[par][:, :, :, 0:DH1], src).then_inc(values_ready, 1)

            def close(b, t, first):
                pass

            whole(pool, slot, close)

        @block.vector
        def _(dve):
            dve.wait_ge(buffers_clear, 1)

            def slot(b, g, t, first, prepare, attend):
                if not prepare:
                    return
                made = QUADS * b + g + 1
                for u in range(STEPS1):
                    for x in STEP_JOBS1[u]:
                        if x[0] != "max":
                            continue
                        _, j, k = x
                        job = Job1(first, JOBS1[x], t)
                        dve.wait_ge(job_ready, job.done)
                        nc.vector.tensor_reduce(maxima[:, j, k:k + 1], wide[job.bank][:], AX_X, ALU.max).then_inc(wide_free[job.bank], 1)
                for x in MAX_JOBS[-2:]:
                    job = Job1(first, JOBS1[x], t)
                    dve.wait_ge(wide_free[job.bank], job.before + 1)
                out = minus_max[:].rearrange("p k (j r) -> p j k r", j=4)[:, :, :, 3 * DH1:3 * DH1 + 1]
                nc.vector.tensor_scalar(out, maxima[:].unsqueeze(3), -1.0 / SH, None, ALU.mult).then_inc(minus_ready, 1)

            def close(b, t, first):
                ctx_job, sum_job = Job1(first, 0, t), Job1(first, 1, t)
                dve.wait_ge(job_ready, sum_job.done)
                nc.vector.reciprocal(inverse[:], wide[sum_job.bank][:]).then_inc(wide_free[sum_job.bank], 1)
                dve.wait_ge(wide_free[sum_job.bank], sum_job.before + 1)
                nc.vector.tensor_tensor(normed[:], wide[ctx_job.bank][:], inverse[:], ALU.mult).then_inc(wide_free[ctx_job.bank], 1)
                dve.wait_ge(wide_free[ctx_job.bank], ctx_job.before + 1)
                here = chip.xT[:, ds(b * SEQ, SEQ)]
                nc.vector.scalar_tensor_tensor(here, normed[:], chip.mod[:, 1, GA, ds(b, 1)], here, ALU.mult, ALU.add)

            whole(dve, slot, close)


def load_mlp1(nc, chip, dram):
    with ExitStack() as ctx:
        tiles = HT * (EXPERTS + 1)
        raw = ctx.enter_context(nc.sbuf_tensor("up1_raw", [P, tiles * P], F32))
        loaded, loaded_down, high = (ctx.enter_context(nc.semaphore(x)) for x in ("up1_loaded", "down1_loaded", "up1_high"))
        block = ctx.enter_context(nc.Block())
        up = [chip.up1[:, half, :, :].rearrange("p k m -> p (k m)") for half in range(2)]

        @block.sync
        def _(sp):
            sp.dma_start(raw[:, 0:HID], dram["L1_ffn_Wfc_s"]).then_inc(loaded, 16)
            sp.dma_start(raw[:, HID:].rearrange("c (e h) -> c e h", e=EXPERTS), dram["L1_ffn_Wfc"].rearrange("e c h -> c e h")).then_inc(loaded, 16)
            sp.dma_start(chip.down1[:, 0:HT, :], dram["L1_ffn_Wproj_s"].rearrange("(j p) d -> p j d", p=P)).then_inc(loaded_down, 16)
            sp.dma_start(chip.down1[:, HT:, :], dram["L1_ffn_Wproj"].rearrange("e (j p) d -> p (e j) d", p=P)).then_inc(loaded_down, 16)
            sp.wait_ge(loaded_down, 32)

        @block.scalar
        def _(act):
            act.wait_ge(loaded, 32)
            nc.scalar.mul(up[0], raw[:], WS).then_inc(high, 1)

        @block.vector
        def _(dve):
            dve.wait_ge(high, 1)
            nc.vector.scalar_tensor_tensor(up[1], raw[:], WS, up[0], ALU.mult, ALU.subtract)


def store(nc, chip, out):
    with ExitStack() as ctx:
        def sem(name):
            return ctx.enter_context(nc.semaphore(name))

        turned = [ctx.enter_context(nc.psum_tensor(f"turned{u}", [P, CHUNK], F32)) for u in range(2)]
        rows = [ctx.enter_context(nc.sbuf_tensor(f"out_rows{u}", [P, 4, CH], F32)) for u in range(2)]
        out_turned, out_copied = sem("out_turned"), sem("out_copied")
        out_stored = [sem(f"out_stored{u}") for u in range(2)]
        view = out.rearrange("b (t p) c -> p (b t) c", p=P)
        block = ctx.enter_context(nc.Block())

        @block.tensor
        def _(pe):
            for n in range(NCHUNK):
                if n >= 2:
                    pe.wait_ge(out_copied, n - 1)
                for i in range(4):
                    at = n * CHUNK + i * P
                    ins = pe.transpose(turned[n % 2][:, i * P:(i + 1) * P], chip.xT[:, at:at + P], const(chip, "ident"))
                ins.then_inc(out_turned, 1)

        @block.vector
        def _(dve):
            for n in range(NCHUNK):
                dve.wait_ge(out_turned, n + 1)
                if n >= 2:
                    dve.wait_ge(out_stored[n % 2], 16 * (n // 2))
                nc.vector.tensor_copy(rows[n % 2][:], turned[n % 2][:].rearrange("p (i c) -> p i c", i=4)).then_inc(out_copied, 1)

        @block.sync
        def _(sp):
            for n in range(NCHUNK):
                sp.wait_ge(out_copied, n + 1)
                sp.dma_start(view[:, 4 * n:4 * n + 4, :], rows[n % 2][:]).then_inc(out_stored[n % 2], 16)
            for u in range(2):
                sp.wait_ge(out_stored[u], 16 * NCHUNK // 2)


def clear_semaphores(nc):
    with nc.Block() as block:
        @block.sync
        def _(sp):
            for used in sorted(nc.released_uncleared_semaphores):
                sp.sem_clear(range(used, used + 1))


def program(nc, dram, out, stages=99):
    chip = Chip()
    with ExitStack() as whole:
        chip.apart = whole.enter_context(nc.semaphore("apart"))

        def keep(name, shape, dt, ctx=whole):
            return ctx.enter_context(nc.sbuf_tensor(name, shape, dt))

        chip.xT = keep("xT", [P, TOK], F32)
        chip.h_high = keep("h_high", [P, TOK], F16)
        chip.h_low = keep("h_low", [P, TOK], F16)
        chip.consts = keep("consts_sb", [P, CONST_COLS], F32)
        chip.cols = keep("cols", [P, ROWS], F32)
        chip.bqk = keep("bqk", [P, 2 * HEADS0], F32)
        chip.bqk1 = keep("bqk1", [P, 4], F32)
        chip.bv0 = chip.cols[:, ROW_AT["bv0"][0]:ROW_AT["bv0"][0] + PAIRS]
        chip.mod = keep("mod", [P, 2, 6, BATCH], F32)
        chip.g_bias = keep("g_bias", [P, 3, BATCH], F32)
        chip.ga_scaled = keep("ga_scaled", [P, BATCH], F32)
        chip.mean_ones = keep("mean_ones", [P, P], F32)
        chip.ones = keep("ones", [P, P], F32)
        chip.sum_ones = keep("sum_ones", [P, DH0], F32)
        chip.eps = keep("eps", [P, 1], F32)
        chip.ident16 = keep("ident16", [P, P], F16)
        chip.identb = keep("identb", [P, P], BF16)
        chip.mask_qk = keep("mask_qk", [P, P], BF16)
        chip.mask_kq = keep("mask_kq", [P, P], BF16)
        chip.gate_sel = keep("gate_sel", [3 * EXPERTS, EXPERTS * P], BF16)
        chip.q_sel = keep("q_sel", [P, QUADS * 2 * P], F16)
        chip.k_sel = keep("k_sel", [P, QUADS * 2 * P], F16)
        chip.w_router1 = keep("w_router1", [P, EXPERTS], F32)
        chip.w1_attn_raw = keep("w1_attn_raw", [P, 3, CH], F32)
        chip.b2_rows = keep("b2_rows", [3 * EXPERTS, CH], F32)
        chip.bproj_rows = keep("bproj_rows", [3 * EXPERTS, CH], F32)

        with ExitStack() as layer0:
            chip.w1T = keep("w1T", [P, 2, EXPERTS * HT, P], F16, layer0)
            chip.w2T = keep("w2T", [P, EXPERTS * HT, P], F32, layer0)
            with ExitStack() as att:
                chip.w_qk = keep("w_qk", [P, 2, HEADS0, 2, 2, DH0], F16, att)
                chip.w_v = keep("w_v", [P, 2, HEADS0 * DH0], F16, att)
                chip.w_out = keep("w_out", [P, 2, PAIRS, CH], F16, att)
                with ExitStack() as raw:
                    chip.w_qkv_raw = keep("w_qkv_raw", [P, 3 * HEADS0 * DH0], F32, raw)
                    chip.w_out_raw = keep("w_out_raw", [P, PAIRS, CH], F32, raw)
                    setup(nc, chip, dram)
                layer_norm(nc, chip, "ln1", 0, SA, CA)
                if stages >= 1:
                    attention0(nc, chip)
            if stages >= 2:
                with ExitStack() as mlp:
                    chip.logits = keep("logits0", [P, NTILE, EXPERTS], F32, mlp)
                    chip.gates_b16 = keep("gates0_b16", [3 * EXPERTS, TOK], BF16, mlp)
                    chip.gates_f32 = keep("gates0_f32", [3 * EXPERTS, TOK], F32, mlp)
                    layer_norm(nc, chip, "ln2", 0, SB, CB, bias_of=0, router=chip.cols[:, ROW_AT["gate0"][0]:ROW_AT["gate0"][0] + EXPERTS],
                               logits=chip.logits)
                    gates(nc, chip, 0)
                    experts(nc, chip, 0, chip.w1T, chip.w2T, "b1", chip.b2_rows, 0)
        clear_semaphores(nc)
        with ExitStack() as layer1:
            if stages >= 3:
                layer_norm(nc, chip, "ln3", 1, SA, CA)
                with ExitStack() as att:
                    chip.q1 = [keep(f"q1_{half}", [P, TOK], F16, att) for half in range(2)]
                    chip.k1 = [keep(f"k1_{half}", [P, TOK], F16, att) for half in range(2)]
                    chip.v1 = keep("v1", [P, NTILE, CH], F32, att)
                    project1(nc, chip, dram)
                    attention1(nc, chip)
            if stages >= 4:
                chip.logits = keep("logits1", [P, NTILE, EXPERTS], F32, layer1)
                chip.gates_b16 = keep("gates1_b16", [3 * EXPERTS, TOK], BF16, layer1)
                chip.gates_f32 = keep("gates1_f32", [3 * EXPERTS, TOK], F32, layer1)
                chip.up1 = keep("up1", [P, 2, HT * (EXPERTS + 1), P], F16, layer1)
                chip.down1 = keep("down1", [P, HT * (EXPERTS + 1), P], F32, layer1)
                load_mlp1(nc, chip, dram)
                layer_norm(nc, chip, "ln4", 1, SB, CB, bias_of=1, router=chip.w_router1[:], logits=chip.logits)
                gates(nc, chip, 1)
                experts(nc, chip, 1, chip.up1, chip.down1, "bfc_s", chip.bproj_rows, HT)
        store(nc, chip, out)


INPUTS = ['L0_attn_x', 'L0_attn_w_qkv', 'L0_attn_b_qkv', 'L0_attn_w_out', 'L0_attn_b_out', 'L0_ffn_gate_weight', 'L0_ffn_w1',
          'L0_ffn_b1', 'L0_ffn_w2', 'L0_ffn_b2', 'L0_c', 'L0_wmod', 'L1_attn_Wq', 'L1_attn_bq', 'L1_attn_Wk', 'L1_attn_bk',
          'L1_attn_Wv', 'L1_attn_bv', 'L1_ffn_Wfc_s', 'L1_ffn_bfc_s', 'L1_ffn_Wproj_s', 'L1_ffn_bproj_s', 'L1_ffn_Wr',
          'L1_ffn_Wfc', 'L1_ffn_bfc', 'L1_ffn_Wproj', 'L1_ffn_bproj', 'L1_c', 'L1_wmod']


def kernel(**inputs):
    import concourse.bacc as bacc
    from concourse.bass_utils import run_bass_kernel_spmd

    nc = bacc.Bacc("TRN2", target_bir_lowering=False, num_devices=1)
    arrays, dram = {}, {}
    for name in INPUTS:
        arrays[name] = np.ascontiguousarray(inputs[name])
        dram[name] = nc.dram_tensor(name, arrays[name].shape, mybir.dt.from_np(arrays[name].dtype), kind="ExternalInput").ap()
    arrays["consts"] = constants()
    dram["consts"] = nc.dram_tensor("consts", arrays["consts"].shape, F32, kind="ExternalInput").ap()
    out = nc.dram_tensor("out", (BATCH, SEQ, CH), F32, kind="ExternalOutput").ap()
    program(nc, dram, out)
    result = run_bass_kernel_spmd(nc, [arrays], core_ids=[0])
    return result.results[0]["out"]
```

```python
from contextlib import ExitStack

import numpy as np

import concourse.bass as bass
from concourse import mybir

P = 128
BATCH = 4
SEQ = 1024
CH = 128
TOK = BATCH * SEQ
CHUNK = 512
NCHUNK = TOK // CHUNK
NTILE = TOK // P
HEADS0 = 16
DH0 = 64
PAIRS = HEADS0 // 2
EXPERTS = 8
HID = 512
HT = HID // P
KTH = BATCH * 128 * 6
HEADS1 = 16
DH1 = CH // HEADS1
QUADS = 4
EPS = 1e-5
WS = 16.0
GS = 16.0
SH = 1024.0

F32 = mybir.dt.float32
F16 = mybir.dt.float16
BF16 = mybir.dt.bfloat16
I32 = mybir.dt.int32
ALU = mybir.AluOpType
ACT = mybir.ActivationFunctionType
AX_X = mybir.AxisListType.X
ds = bass.ds

CONST = {}
_at = 0
for _name, _n in (("ident", P), ("mask_qk", P), ("mask_kq", P), ("place_ctx", 32), ("place_sum", 32), ("prefer", EXPERTS),
                  ("key_pad", 1), ("head_rows", 4), ("rot_sign", 1), ("gate_sel", EXPERTS * P), ("q_sel", QUADS * 2 * P),
                  ("k_sel", QUADS * 2 * P), ("cos", SEQ), ("sin", SEQ)):
    CONST[_name] = (_at, _n)
    _at += _n
CONST_COLS = _at

ROW_AT = {}
_at = 0
for _name, _n in (("b_out", 1), ("bq", 1), ("bk", 1), ("bv", 1), ("bq_rot", 1), ("bk_rot", 1), ("c0", BATCH), ("c1", BATCH),
                  ("gate0", EXPERTS), ("bv0", PAIRS), ("b1", EXPERTS * HT), ("bfc_s", HT), ("bfc", EXPERTS * HT),
                  ("bproj_s", 1)):
    ROW_AT[_name] = (_at, _n)
    _at += _n
ROWS = _at

SA, CA, GA, SB, CB, GB = range(6)


def constants():
    c = np.zeros((P, CONST_COLS), np.float32)

    def put(name, a):
        at, n = CONST[name]
        c[:a.shape[0], at:at + n] = a.reshape(a.shape[0], n)

    r = np.arange(P)
    put("ident", np.eye(P, dtype=np.float32))
    far = -1e9 * np.sqrt(DH0) * WS * WS
    put("mask_qk", np.where(r[None, :] > r[:, None], far, 0.0))
    put("mask_kq", np.where(r[:, None] > r[None, :], far, 0.0))
    ctx, tot, pad = np.zeros((P, 32)), np.zeros((P, 32)), np.zeros((P, 1))
    q_sel, k_sel = np.zeros((P, QUADS, 2, P)), np.zeros((P, QUADS, 2, P))
    for j in range(4):
        pad[32 * j + 3 * DH1] = SH
        for d in range(DH1):
            ctx[32 * j + d, DH1 * j + d] = 1
            tot[32 * j + DH1, DH1 * j + d] = 1
            for g in range(QUADS):
                ch = (4 * g + j) * DH1 + d
                for copy, (q_low, k_low) in enumerate(((0, 0), (1, 0), (0, 1))):
                    q_sel[ch, g, q_low, 32 * j + DH1 * copy + d] = 1
                    k_sel[ch, g, k_low, 32 * j + DH1 * copy + d] = 1
    put("place_ctx", ctx)
    put("place_sum", tot)
    put("key_pad", pad)
    put("head_rows", r[:, None] // 32 == np.arange(4)[None, :])
    put("q_sel", q_sel)
    put("k_sel", k_sel)
    put("prefer", np.tile(np.arange(EXPERTS, 0, -1), (P, 1)))
    put("rot_sign", np.where(r % 2 == 0, -1.0, 1.0)[:, None])
    sel = np.zeros((3 * EXPERTS, EXPERTS, P))
    for e in range(EXPERTS):
        sel[e::EXPERTS, e, :] = GS
    put("gate_sel", sel)
    pos = np.arange(SEQ, dtype=np.float32)
    inv = np.power(np.float32(10000.0), np.float32(-2.0) * np.arange(DH1 // 2, dtype=np.float32) / np.float32(DH1)).astype(np.float32)
    ang = (pos[:, None] * inv[None, :]).astype(np.float32)
    put("cos", np.tile(np.repeat(np.cos(ang), 2, axis=-1).T, (HEADS1, 1)))
    put("sin", np.tile(np.repeat(np.sin(ang), 2, axis=-1).T, (HEADS1, 1)))
    return c


class Chip:
    pass


class Link:

    def __init__(self, eng, sem):
        self.eng, self.sem, self.n = eng, sem, 0

    def __call__(self, ins):
        self.n += 1
        ins.then_inc(self.sem, 1)
        self.eng.wait_ge(self.sem, self.n)


def apart(eng, chip):
    eng.sem_inc(chip.apart, 1)


def const(chip, name, rows=P):
    at, n = CONST[name]
    return chip.consts[0:rows, at:at + n]


def col(chip, name, k=0):
    return chip.cols[:, ROW_AT[name][0] + k:ROW_AT[name][0] + k + 1]


def setup(nc, chip, dram):
    with ExitStack() as ctx:
        def sb(name, shape, dt):
            return ctx.enter_context(nc.sbuf_tensor(name, shape, dt))

        def sem(name):
            return ctx.enter_context(nc.semaphore(name))

        bank = [ctx.enter_context(nc.psum_tensor(f"setup_bank{i}", [P, 512], F32)) for i in range(8)]
        x_tok = sb("x_tok", [P, NTILE, CH], F32)
        rows = sb("rows", [P, P], F32)
        dup_rows = sb("dup_rows", [48, P], F32)
        wmod = sb("wmod", [P, 2, 6 * CH], F32)
        w1_raw = sb("w1_raw", [P, EXPERTS * HT, CH], F32)
        w2_raw = sb("w2_raw", [P, EXPERTS, HID], F32)
        silu = sb("silu", [P, 3, 2 * BATCH], F32)
        mag = sb("mag", [P, 2, 2, 2, BATCH], F32)

        loaded_const, loaded_rows = sem("loaded_const"), sem("loaded_rows")
        loaded_x = [sem(f"loaded_x{n}") for n in range(NCHUNK)]
        loaded_wmod, loaded_qkv, loaded_w1, loaded_w2 = sem("loaded_wmod"), sem("loaded_qkv"), sem("loaded_w1"), sem("loaded_w2")
        loaded_small = sem("loaded_small")
        rows_clear, turned_rows, cols_ready = sem("rows_clear"), sem("turned_rows"), sem("cols_ready")
        silu_exp, silu_ready = sem("silu_exp"), sem("silu_ready")
        turned_x, x_by_act, x_by_dve = sem("turned_x"), sem("x_by_act"), sem("x_by_dve")
        mod_done, mod_taken = sem("mod_done"), sem("mod_taken")
        turned_w1, w1_high, w1_low = sem("turned_w1"), sem("w1_high"), sem("w1_low")
        turned_w2, w2_high = sem("turned_w2"), sem("w2_high")
        high_done = sem("high_done")
        dve_chain = sem("setup_dve_chain")
        N_ROW_LOADS = 16

        block = ctx.enter_context(nc.Block())

        @block.sync
        def _(sp):
            sp.wait_ge(rows_clear, 1)
            for h in range(2):
                sp.dma_start(dup_rows[:, h * DH0:(h + 1) * DH0], dram["L0_attn_b_qkv"].rearrange("t h e -> (t h) e")).then_inc(loaded_rows, 16)

            def row(name, src):
                at, n = ROW_AT[name]
                sp.dma_start(rows[at:at + n, :], src).then_inc(loaded_rows, 16)

            vec = "(a b) -> a b"
            row("b_out", dram["L0_attn_b_out"].rearrange(vec, b=CH))
            row("bq", dram["L1_attn_bq"].rearrange(vec, b=CH))
            row("bk", dram["L1_attn_bk"].rearrange(vec, b=CH))
            row("bv", dram["L1_attn_bv"].rearrange(vec, b=CH))
            row("c0", dram["L0_c"])
            row("c1", dram["L1_c"])
            row("gate0", dram["L0_ffn_gate_weight"])
            row("bv0", dram["L0_attn_b_qkv"][2].rearrange("(a b) e -> a (b e)", b=2))
            row("b1", dram["L0_ffn_b1"].rearrange("e (j p) -> (e j) p", p=P))
            row("bfc_s", dram["L1_ffn_bfc_s"].rearrange(vec, b=CH))
            row("bproj_s", dram["L1_ffn_bproj_s"].rearrange(vec, b=CH))
            row("bfc", dram["L1_ffn_bfc"].rearrange("e (j p) -> (e j) p", p=P))
            for name, src in (("bq_rot", "L1_attn_bq"), ("bk_rot", "L1_attn_bk")):
                at = ROW_AT[name][0]
                pairs = dram[src].rearrange("(a i two) -> a i two", a=1, two=2)
                out = rows[at:at + 1, :].rearrange("a (i two) -> a i two", two=2)
                sp.dma_start(out[:, :, 0:1], pairs[:, :, 1:2], allow_slow_non_contiguous=True).then_inc(loaded_rows, 16)
                sp.dma_start(out[:, :, 1:2], pairs[:, :, 0:1], allow_slow_non_contiguous=True).then_inc(loaded_rows, 16)
            sp.dma_start(wmod[:, 0, :], dram["L0_wmod"]).then_inc(loaded_wmod, 16)
            sp.dma_start(wmod[:, 1, :], dram["L1_wmod"]).then_inc(loaded_wmod, 16)
            sp.dma_start(chip.w_qkv_raw[:], dram["L0_attn_w_qkv"].rearrange("d t h e -> d (t h e)")).then_inc(loaded_qkv, 16)
            sp.dma_start(chip.w_out_raw[:], dram["L0_attn_w_out"].rearrange("(p s) e d -> (s e) p d", s=2)).then_inc(loaded_qkv, 16)
            sp.dma_start(w2_raw[:], dram["L0_ffn_w2"].rearrange("e d h -> d e h")).then_inc(loaded_w2, 16)
            sp.dma_start(chip.w_router1[:], dram["L1_ffn_Wr"]).then_inc(loaded_small, 16)
            for k, name in enumerate(("L1_attn_Wq", "L1_attn_Wk", "L1_attn_Wv")):
                sp.dma_start(chip.w1_attn_raw[:, k, :], dram[name]).then_inc(loaded_small, 16)
            for k in range(3):
                sp.dma_start(chip.b2_rows[EXPERTS * k:EXPERTS * (k + 1), :], dram["L0_ffn_b2"]).then_inc(loaded_small, 16)
                sp.dma_start(chip.bproj_rows[EXPERTS * k:EXPERTS * (k + 1), :], dram["L1_ffn_bproj"]).then_inc(loaded_small, 16)
            sp.wait_ge(loaded_small, 16 * 10)

        @block.scalar
        def _(act):
            act.dma_start(chip.consts[:], dram["consts"]).then_inc(loaded_const, 16)
            x_view = dram["L0_attn_x"].rearrange("b (t p) c -> p (b t) c", p=P)
            for n in range(NCHUNK):
                act.dma_start(x_tok[:, 4 * n:4 * n + 4, :], x_view[:, 4 * n:4 * n + 4, :]).then_inc(loaded_x[n], 16)
            act.dma_start(w1_raw[:], dram["L0_ffn_w1"].rearrange("e (j p) d -> p (e j) d", p=P)).then_inc(loaded_w1, 16)
            act.wait_ge(cols_ready, 1)
            c_cols = chip.cols[:, ROW_AT["c0"][0]:ROW_AT["c0"][0] + 2 * BATCH]
            nc.scalar.activation(silu[:, 0, :], c_cols, ACT.Exp, scale=-1.0).then_inc(silu_exp, 1)
            for n in range(1, NCHUNK, 2):
                act.wait_ge(turned_x, n + 1)
                nc.scalar.copy(chip.xT[:, n * CHUNK:(n + 1) * CHUNK], bank[n][:]).then_inc(x_by_act, 1)
            act.wait_ge(loaded_qkv, 32)
            qkv = chip.w_qkv_raw[:].rearrange("c (t h e) -> c t h e", t=3, h=HEADS0)
            for t in range(2):
                for twice in range(2):
                    nc.scalar.mul(chip.w_qk[:, 0, :, t, twice, :], qkv[:, t, :, :], WS).then_inc(high_done, 1)
            nc.scalar.mul(chip.w_v[:, 0, :], chip.w_qkv_raw[:, 2 * HEADS0 * DH0:], WS).then_inc(high_done, 1)
            nc.scalar.mul(chip.w_out[:, 0, :, :], chip.w_out_raw[:], WS).then_inc(high_done, 1)
            for k in range(8):
                act.wait_ge(turned_w1, k + 1)
                nc.scalar.mul(chip.w1T[:, 0, 4 * k:4 * k + 4, :], bank[k][:].rearrange("p (a b) -> p a b", a=4), WS).then_inc(w1_high, 1)
            for k in range(8):
                act.wait_ge(turned_w2, k + 1)
                nc.scalar.mul(chip.w2T[:, 0, 4 * k:4 * k + 4, :], bank[k][:].rearrange("p (a b) -> p a b", a=4), WS).then_inc(w2_high, 1)

        @block.tensor
        def _(pe):
            ident = const(chip, "ident")
            pe.wait_ge(loaded_const, 16)
            pe.wait_ge(loaded_rows, 16 * (2 + 16))
            pe.transpose(bank[7][:, 0:48], dup_rows[:], ident[0:48, 0:48]).then_inc(turned_rows, 1)
            pe.transpose(bank[7][:, 64:64 + ROWS], rows[0:ROWS, :], ident[0:ROWS, 0:ROWS]).then_inc(turned_rows, 1)
            for n in range(NCHUNK):
                pe.wait_ge(loaded_x[n], 16)
                if n == 7:
                    pe.wait_ge(cols_ready, 1)
                for i in range(4):
                    ins = pe.transpose(bank[n][:, i * P:(i + 1) * P], x_tok[:, 4 * n + i, :], ident)
                ins.then_inc(turned_x, 1)
            pe.wait_ge(silu_ready, 1)
            pe.wait_ge(loaded_wmod, 32)
            pe.wait_ge(x_by_dve, 1)
            for layer in range(2):
                for k in range(6):
                    ins = pe.matmul(bank[0][:, (layer * 6 + k) * BATCH:(layer * 6 + k + 1) * BATCH],
                                    wmod[:, layer, k * CH:(k + 1) * CH],
                                    silu[:, 2, layer * BATCH:(layer + 1) * BATCH], start=True, stop=True)
            ins.then_inc(mod_done, 1)
            pe.wait_ge(loaded_w1, 16)
            pe.wait_ge(mod_taken, 1)
            pe.wait_ge(x_by_act, 4)
            pe.wait_ge(x_by_dve, 4)
            for k in range(8):
                for i in range(4):
                    ins = pe.transpose(bank[k][:, i * P:(i + 1) * P], w1_raw[:, 4 * k + i, :], ident)
                ins.then_inc(turned_w1, 1)
            pe.wait_ge(loaded_w2, 16)
            for k in range(8):
                pe.wait_ge(w1_low, k + 1)
                for i in range(4):
                    ins = pe.transpose(bank[k][:, i * P:(i + 1) * P], w2_raw[:, k, i * P:(i + 1) * P], ident)
                ins.then_inc(turned_w2, 1)

        @block.gpsimd
        def _(pool):
            nc.gpsimd.memset(rows[:], 0.0).then_inc(rows_clear, 1)
            nc.gpsimd.memset(chip.mean_ones[:], 1.0 / CH)
            nc.gpsimd.memset(chip.ones[:], 1.0)
            nc.gpsimd.memset(chip.sum_ones[:], WS)
            nc.gpsimd.memset(chip.eps[:], EPS)
            pool.wait_ge(loaded_const, 16)
            nc.gpsimd.tensor_copy(chip.ident16[:], const(chip, "ident"))
            nc.gpsimd.tensor_copy(chip.identb[:], const(chip, "ident"))
            nc.gpsimd.tensor_copy(chip.mask_qk[:], const(chip, "mask_qk"))
            nc.gpsimd.tensor_copy(chip.mask_kq[:], const(chip, "mask_kq"))
            nc.gpsimd.tensor_copy(chip.gate_sel[:], const(chip, "gate_sel", 3 * EXPERTS))
            nc.gpsimd.tensor_copy(chip.q_sel[:], const(chip, "q_sel"))
            nc.gpsimd.tensor_copy(chip.k_sel[:], const(chip, "k_sel"))

        @block.vector
        def _(dve):
            link = Link(dve, dve_chain)
            dve.wait_ge(turned_rows, 2)
            link(nc.vector.tensor_copy(chip.cols[:, 0:ROWS], bank[7][:, 64:64 + ROWS]))
            nc.vector.tensor_scalar(chip.bqk[:], bank[7][:, 0:2 * HEADS0], WS, None, ALU.mult).then_inc(cols_ready, 1)
            dve.wait_ge(silu_exp, 1)
            link(nc.vector.tensor_scalar(silu[:, 1, :], silu[:, 0, :], 1.0, None, ALU.add))
            link(nc.vector.reciprocal(silu[:, 0, :], silu[:, 1, :]))
            c_cols = chip.cols[:, ROW_AT["c0"][0]:ROW_AT["c0"][0] + 2 * BATCH]
            nc.vector.tensor_tensor(silu[:, 2, :], silu[:, 0, :], c_cols, ALU.mult).then_inc(silu_ready, 1)
            for n in range(0, NCHUNK, 2):
                dve.wait_ge(turned_x, n + 1)
                nc.vector.tensor_copy(chip.xT[:, n * CHUNK:(n + 1) * CHUNK], bank[n][:]).then_inc(x_by_dve, 1)
            dve.wait_ge(mod_done, 1)
            mod = chip.mod
            link(nc.vector.tensor_copy(mod[:].rearrange("p l k b -> p (l k b)"), bank[0][:, 0:12 * BATCH]))
            nc.vector.memset(silu[:, 1, 0:1], 0.0).then_inc(mod_taken, 1)
            for k in (CA, CB):
                link(nc.vector.tensor_scalar(mod[:, :, k, :], mod[:, :, k, :], 1.0, None, ALU.add))
            for n, k in enumerate((GA, GB)):
                g = mod[:, :, k, :]
                size, sign = mag[:, 0, n, :, :], mag[:, 1, n, :, :]
                link(nc.vector.scalar_tensor_tensor(size, g, -1.0, g, ALU.mult, ALU.max))
                link(nc.vector.tensor_scalar(size, size, 0.25, None, ALU.max))
                link(nc.vector.tensor_scalar(sign, g, 0.0, 2.0, ALU.is_ge, ALU.mult))
                link(nc.vector.scalar_tensor_tensor(g, sign, -1.0, size, ALU.add, ALU.mult))
            link(nc.vector.tensor_scalar(chip.g_bias[:, 0, :], mod[:, 0, GA, :], col(chip, "b_out"), None, ALU.mult))
            link(nc.vector.tensor_scalar(chip.g_bias[:, 1, :], mod[:, 1, GA, :], col(chip, "bv"), None, ALU.mult))
            link(nc.vector.tensor_scalar(chip.g_bias[:, 2, :], mod[:, 1, GB, :], col(chip, "bproj_s"), None, ALU.mult))
            link(nc.vector.tensor_scalar(chip.ga_scaled[:], mod[:, 0, GA, :], 1.0 / WS, None, ALU.mult))
            link(nc.vector.tensor_scalar(chip.gb_scaled[:], mod[:, :, GB, :], 1.0 / (WS * GS), None, ALU.mult))
            at = ROW_AT["bq"][0]
            link(nc.vector.tensor_scalar(chip.bqk1[:, 0:2], chip.cols[:, at:at + 2], WS, None, ALU.mult))
            at = ROW_AT["bq_rot"][0]
            link(nc.vector.tensor_scalar(chip.bqk1[:, 2:4], chip.cols[:, at:at + 2], const(chip, "rot_sign"), WS, ALU.mult, ALU.mult))
            dve.wait_ge(loaded_qkv, 32)
            qkv = chip.w_qkv_raw[:].rearrange("c (t h e) -> c t h e", t=3, h=HEADS0)
            for t in range(2):
                for twice in range(2):
                    dve.wait_ge(high_done, 2 * t + twice + 1)
                    nc.vector.scalar_tensor_tensor(chip.w_qk[:, 1, :, t, twice, :], qkv[:, t, :, :], WS,
                                                   chip.w_qk[:, 0, :, t, twice, :], ALU.mult, ALU.subtract)
            dve.wait_ge(high_done, 6)
            nc.vector.scalar_tensor_tensor(chip.w_v[:, 1, :], chip.w_qkv_raw[:, 2 * HEADS0 * DH0:], WS, chip.w_v[:, 0, :],
                                           ALU.mult, ALU.subtract)
            nc.vector.scalar_tensor_tensor(chip.w_out[:, 1, :, :], chip.w_out_raw[:], WS, chip.w_out[:, 0, :, :],
                                           ALU.mult, ALU.subtract)
            for k in range(8):
                dve.wait_ge(w1_high, k + 1)
                nc.vector.scalar_tensor_tensor(chip.w1T[:, 1, 4 * k:4 * k + 4, :], bank[k][:].rearrange("p (a b) -> p a b", a=4),
                                               WS, chip.w1T[:, 0, 4 * k:4 * k + 4, :], ALU.mult, ALU.subtract).then_inc(w1_low, 1)
            for k in range(8):
                dve.wait_ge(w2_high, k + 1)
                nc.vector.scalar_tensor_tensor(chip.w2T[:, 1, 4 * k:4 * k + 4, :], bank[k][:].rearrange("p (a b) -> p a b", a=4),
                                               WS, chip.w2T[:, 0, 4 * k:4 * k + 4, :], ALU.mult, ALU.subtract)
            dve.wait_ge(loaded_small, 16 * 10)
            nc.vector.tensor_scalar(chip.b2_rows[:], chip.b2_rows[:], WS * GS, None, ALU.mult)
            nc.vector.tensor_scalar(chip.bproj_rows[:], chip.bproj_rows[:], WS * GS, None, ALU.mult)


def layer_norm(nc, chip, name, layer, shift, scale, bias_of=None, router=None, logits=None):
    W = 4
    with ExitStack() as ctx:
        def sb(what, shape, dt):
            return ctx.enter_context(nc.sbuf_tensor(f"{name}_{what}", shape, dt))

        def sem(what):
            return ctx.enter_context(nc.semaphore(f"{name}_{what}"))

        mean = [ctx.enter_context(nc.psum_tensor(f"{name}_mean{u}", [P, CHUNK], F32)) for u in range(W)]
        var = [ctx.enter_context(nc.psum_tensor(f"{name}_var{u}", [P, CHUNK], F32)) for u in range(W)]
        logit = [mean[u][:, 0:4 * EXPERTS].rearrange("p (i e) -> p i e", i=4) for u in range(W)]
        centred, square, inverse, h32 = ([sb(f"{what}{u}", [P, CHUNK], F32) for u in range(W)]
                                         for what in ("centred", "square", "inverse", "h32"))
        turned = square
        deviation, compact = ([sb(f"{what}{u}", [P, CHUNK // 32], F32) for u in range(W)] for what in ("deviation", "compact"))
        x_whole, mean_ready, centred_ready, square_ready, var_ready, var_turned, deviation_ready = (
            sem(w) for w in ("x_whole", "mean_ready", "centred_ready", "square_ready", "var_ready", "var_turned", "deviation_ready"))
        compact_ready, inverse_ready, normed_ready, h_ready, high_ready, low_ready, logit_ready = (
            sem(w) for w in ("compact_ready", "inverse_ready", "normed_ready", "h_ready", "high_ready", "low_ready", "logit_ready"))
        block = ctx.enter_context(nc.Block())

        def chunk(a, t, u):
            return a[:, ds(t * W * CHUNK + u * CHUNK, CHUNK)]

        @block.tensor
        def _(pe):
            with pe.Fori(0, NCHUNK // W) as t:
                for u in range(W):
                    if bias_of is not None:
                        pe.wait_ge(x_whole, W * t + u + 1)
                    pe.matmul(mean[u][:], chip.mean_ones[:], chunk(chip.xT, t, u), start=True, stop=True).then_inc(mean_ready, 1)
                for u in range(W):
                    pe.wait_ge(square_ready, W * t + u + 1)
                    pe.matmul(var[u][:], chip.mean_ones[:], square[u][:], start=True, stop=True).then_inc(var_ready, 1)
                if router is not None:
                    for u in range(W):
                        pe.wait_ge(h_ready, W * t + u + 1)
                        for i in range(4):
                            ins = pe.matmul(logit[u][:, i, :], h32[u][:, i * P:(i + 1) * P], router, start=True, stop=True)
                        ins.then_inc(logit_ready, 1)

        @block.scalar
        def _(act):
            with act.Fori(0, NCHUNK // W) as t:
                act.wait_ge(deviation_ready, W * t)
                for u in range(W):
                    act.wait_ge(centred_ready, W * t + u + 1)
                    nc.scalar.square(square[u][:], centred[u][:]).then_inc(square_ready, 1)
                for u in range(W):
                    act.wait_ge(var_turned, W * t + u + 1)
                    nc.scalar.activation(deviation[u][:], turned[u][:].rearrange("p (a b) -> p a b", b=32)[:, :, 0], ACT.Sqrt,
                                         bias=chip.eps[:, 0:1]).then_inc(deviation_ready, 1)
                for u in range(W):
                    act.wait_ge(low_ready, W * t)
                    act.wait_ge(normed_ready, W * t + u + 1)
                    apart(act, chip)
                    batch = t * W // 2 + u // 2
                    nc.scalar.activation(h32[u][:], centred[u][:], ACT.Identity, scale=chip.mod[:, layer, scale, ds(batch, 1)],
                                         bias=chip.mod[:, layer, shift, ds(batch, 1)]).then_inc(h_ready, 1)
                for u in range(W):
                    act.wait_ge(h_ready, W * t + u + 1)
                    apart(act, chip)
                    nc.scalar.copy(chunk(chip.h_high, t, u), h32[u][:]).then_inc(high_ready, 1)

        @block.gpsimd
        def _(pool):
            with pool.Fori(0, NCHUNK // W) as t:
                for u in range(W):
                    pool.wait_ge(high_ready, W * t + u + 1)
                    apart(pool, chip)
                    nc.gpsimd.tensor_tensor(chunk(chip.h_low, t, u), h32[u][:], chunk(chip.h_high, t, u), ALU.subtract).then_inc(low_ready, 1)

        @block.vector
        def _(dve):
            with dve.Fori(0, NCHUNK // W) as t:
                for u in range(W):
                    if bias_of is not None:
                        nc.vector.tensor_scalar(chunk(chip.xT, t, u), chunk(chip.xT, t, u),
                                                chip.g_bias[:, bias_of, ds(t * W // 2 + u // 2, 1)], None, ALU.add).then_inc(x_whole, 1)
                dve.wait_ge(h_ready, W * t)
                for u in range(W):
                    dve.wait_ge(mean_ready, W * t + u + 1)
                    nc.vector.tensor_tensor(centred[u][:], chunk(chip.xT, t, u), mean[u][:], ALU.subtract).then_inc(centred_ready, 1)
                for u in range(W):
                    dve.wait_ge(var_ready, W * t + u + 1)
                    nc.vector.transpose(turned[u][:], var[u][:]).then_inc(var_turned, 1)
                for u in range(W):
                    dve.wait_ge(deviation_ready, W * t + u + 1)
                    nc.vector.reciprocal(compact[u][:], deviation[u][:]).then_inc(compact_ready, 1)
                for u in range(W):
                    dve.wait_ge(compact_ready, W * t + u + 1)
                    nc.vector.transpose(inverse[u][:], compact[u][:].unsqueeze(2).broadcast_to([P, CHUNK // 32, 32])).then_inc(inverse_ready, 1)
                for u in range(W):
                    dve.wait_ge(inverse_ready, W * t + u + 1)
                    nc.vector.tensor_tensor(centred[u][:], centred[u][:], inverse[u][:], ALU.mult).then_inc(normed_ready, 1)
                if router is not None:
                    for u in range(W):
                        dve.wait_ge(logit_ready, W * t + u + 1)
                        nc.vector.tensor_copy(logits[:, ds(t * W * 4 + u * 4, 4), :], logit[u])



UNITS = [(j, c) for j in range(SEQ // P) for c in range(2) if P * j < CHUNK * (c + 1)]
NU = len(UNITS)


def unit(u):
    j, c = UNITS[u]
    first = max(P * j, CHUNK * c)
    return j, c, first, CHUNK * (c + 1) - first, first == P * j


STEP_JOBS = [
    [("sum", 0), ("sum", 1), ("q", 0, 0), ("q", 0, 1), ("k", 0, 1), ("k", 0, 0)],
    [("q", 1, 0)],
    [("q", 1, 1)],
    [("k", 1, 1), ("k", 1, 0), ("out", 0), ("out", 1), ("v", 0), ("max", 0, 0, 0)],
    [("max", 0, 1, 0), ("max", 0, 2, 0), ("max", 0, 3, 0), ("max", 0, 4, 0), ("max", 0, 4, 1)],
    [("max", 0, 5, 0), ("max", 0, 7, 0), ("max", 0, 5, 1), ("max", 0, 6, 0)],
    [("max", 0, 6, 1), ("max", 0, 7, 1)],
    [("max", 1, 0, 0), ("max", 1, 2, 0), ("max", 1, 3, 0), ("max", 1, 1, 0)],
    [("shift", 0, 1), ("max", 1, 4, 0), ("max", 1, 4, 1), ("max", 1, 5, 0)],
    [("max", 1, 5, 1), ("max", 1, 7, 0), ("max", 1, 6, 0), ("max", 1, 6, 1), ("max", 1, 7, 1)],
    [("shift", 0, 0)],
    [("shift", 1, 0), ("shift", 1, 1), ("v", 1)],
]
CLOSING = ("sum", "out")


def slot_jobs(close, prepare):
    steps = [[x for x in step if (close if x[0] in CLOSING else prepare)] for step in STEP_JOBS]
    number = {}
    for step in steps:
        for x in step:
            number[x] = len(number)
    return steps, number


ALL_JOBS = len(slot_jobs(True, True)[1])
PREPARE_JOBS = len(slot_jobs(False, True)[1])
HIGHS = 8
BANKS = 4


class Job:

    def __init__(self, first, k, t, per_turn):
        n = first + k
        self.bank = n % BANKS
        self.before = n // BANKS + per_turn // BANKS * t
        self.done = n + 1 + per_turn * t


def attention0(nc, chip):
    SCALE = 1.0 / (float(np.sqrt(DH0)) * WS * WS)
    PER_TURN = 2 * ALL_JOBS
    assert PER_TURN % BANKS == 0
    with ExitStack() as ctx:
        def sb(name, shape, dt):
            return ctx.enter_context(nc.sbuf_tensor(name, shape, dt))

        def sem(name):
            return ctx.enter_context(nc.semaphore(name))

        def two(name, shape, dt):
            return [[sb(f"{name}{v}{s}", shape, dt) for s in range(2)] for v in range(2)]

        q_twice = two("q_twice", [P, SEQ], F16)
        q_low = two("q_low", [96, SEQ], F16)
        k_both = two("k_both", [P, SEQ], F16)
        k_high = two("k_high", [96, SEQ], F16)
        v = two("v", [P, SEQ // P, DH0], F32)
        total = two("total", [P, SEQ], F32)
        probs = two("probs", [P, CHUNK], F32)
        maxima = [sb(f"maxima{s}", [P, 2, 8], F32) for s in range(2)]
        minus_max = [sb(f"minus_max{s}", [P, 8, 32], F16) for s in range(2)]
        turned = [sb(f"sums_turned{c}", [P, CHUNK], F32) for c in range(2)]
        compact = [sb(f"compact{c}", [P, CHUNK // 32], F32) for c in range(2)]
        inverse = [sb(f"inverse{c}", [P, CHUNK], F32) for c in range(2)]
        normed = [sb(f"normed{c}", [P, CHUNK], F32) for c in range(2)]
        o_high = [sb(f"o_high{c}", [P, CHUNK], F16) for c in range(2)]
        o_low = [sb(f"o_low{c}", [P, CHUNK], F16) for c in range(2)]
        scores = [ctx.enter_context(nc.psum_tensor(f"scores{s}", [P, CHUNK], F32)) for s in range(2)]
        spare = [ctx.enter_context(nc.psum_tensor(f"spare{k}", [P, CHUNK], F32)) for k in range(BANKS)]
        o_psum = [ctx.enter_context(nc.psum_tensor(f"o{c}", [P, CHUNK], F32)) for c in range(2)]

        pads_clear, buffers_clear = sem("pads_clear"), sem("buffers_clear")
        job_ready = sem("job_ready")
        bank_free = [sem(f"bank_free{k}") for k in range(BANKS)]
        high_ready = sem("high_ready")
        split_ready = sem("split_ready")
        max_ready = sem("max_ready")
        minus_ready = sem("minus_ready")
        shift_ready = sem("shift_ready")
        score_ready = [sem(f"score_ready{s}") for s in range(2)]
        probs_ready = [sem(f"probs_ready{s}") for s in range(2)]
        pv_done = [sem(f"pv_done{s}") for s in range(2)]
        added = [sem(f"added{s}") for s in range(2)]
        compact_ready = sem("compact_ready")
        inverse_ready, normed_ready = sem("inverse_ready"), sem("normed_ready")
        o_high_ready, o_low_ready = sem("o_high_ready"), sem("o_low_ready")
        block = ctx.enter_context(nc.Block())
        ADDS = NU - 2

        def where(i):
            return i // PAIRS, i % PAIRS

        def weights(half, t, s, pair):
            return chip.w_qk[:, half, ds(2 * pair + s, 1), t, :, :].rearrange("c h w e -> c (h w e)")

        def bias(t, s, pair):
            return chip.bqk[:, ds(t * HEADS0 + 2 * pair + s, 1)]

        def tokens(a, batch, first, n):
            return a[:, ds(batch * SEQ + first, n)]

        def whole(run, slot):
            slot(-1, 1, 0, 0, False, True, False)
            slot(0, 0, 0, PREPARE_JOBS, False, True, True)
            first = 2 * PREPARE_JOBS
            with run.Fori(0, BATCH * PAIRS // 2 - 1) as t:
                slot(2 * t + 1, 1, t, first, True, True, True)
                slot(2 * t + 2, 0, t, first + ALL_JOBS, True, True, True)
            done = first + PER_TURN * (BATCH * PAIRS // 2 - 1)
            closing = ALL_JOBS - PREPARE_JOBS
            slot(BATCH * PAIRS - 1, 1, 0, done, True, False, True)
            slot(BATCH * PAIRS, 0, 0, done + closing, True, False, False)

        @block.tensor
        def _(pe):
            pe.wait_ge(buffers_clear, 1)

            def product(out, high, low, x_high, x_low):
                pe.matmul(out, high, x_high, start=True, stop=False)
                pe.matmul(out, low, x_high, start=False, stop=False)
                return pe.matmul(out, high, x_low, start=False, stop=True)

            def run_job(x, job, i, parity):
                out = spare[job.bank]
                nxt, n_par = i + 1, 1 - parity
                pe.wait_ge(bank_free[job.bank], job.before)
                if x[0] in ("q", "k"):
                    batch, pair = where(nxt)
                    _, s, c = x
                    t = 0 if x[0] == "q" else 1
                    ins = product(out[:], weights(0, t, s, pair), weights(1, t, s, pair),
                                  tokens(chip.h_high, batch, c * CHUNK, CHUNK), tokens(chip.h_low, batch, c * CHUNK, CHUNK))
                elif x[0] == "v":
                    batch, pair = where(nxt)
                    _, s = x
                    wv = [chip.w_v[:, half, ds((2 * pair + s) * DH0, DH0)] for half in range(2)]
                    for k in range(SEQ // P):
                        h_high, h_low = (tokens(h, batch, k * P, P) for h in (chip.h_high, chip.h_low))
                        o = out[:, k * DH0:(k + 1) * DH0]
                        pe.matmul(o, h_high, wv[0], start=True, stop=False)
                        pe.matmul(o, h_high, wv[1], start=False, stop=False)
                        ins = pe.matmul(o, h_low, wv[0], start=False, stop=True)
                elif x[0] == "max":
                    _, s, k, c = x
                    if (k, c) == (0, 0):
                        pe.wait_ge(split_ready, 4 * nxt + 2 * s + 2)
                    n = min(P * (k + 1) - CHUNK * c, CHUNK)
                    diagonal = c == k // 4
                    ins = pe.matmul(out[:, 0:n], q_twice[n_par][s][:, k * P:(k + 1) * P], k_both[n_par][s][:, c * CHUNK:c * CHUNK + n],
                                    start=True, stop=not diagonal)
                    if diagonal:
                        ins = pe.matmul(out[:, n - P:n], chip.identb[:], chip.mask_qk[:], start=False, stop=True)
                elif x[0] == "shift":
                    _, s, c = x
                    pe.wait_ge(minus_ready, 2 * nxt + s + 1)
                    for k in range(4):
                        ins = pe.matmul(out[64:96, k * P:(k + 1) * P], minus_max[s][:, 4 * c + k, :], chip.ident16[:],
                                        start=True, stop=True)
                elif x[0] == "sum":
                    _, c = x
                    for s in range(2):
                        pe.wait_ge(added[s], ADDS * i)
                        ins = pe.matmul(out[64 * s:64 * s + 64, :], chip.sum_ones[:], total[n_par][s][:, c * CHUNK:(c + 1) * CHUNK],
                                        start=True, stop=True)
                else:
                    _, c = x
                    _, pair = where(i - 1)
                    pe.wait_ge(o_low_ready, 2 * (i - 1) + c + 1)
                    wo = [chip.w_out[:, half, ds(pair, 1), :].rearrange("p a c -> p (a c)") for half in range(2)]
                    ins = product(out[:], wo[0], wo[1], o_high[c][:], o_low[c][:])
                ins.then_inc(job_ready, 1)

            def slot(i, parity, t, first, close, prepare, attend):
                steps, number = slot_jobs(close, prepare)
                if attend:
                    pe.wait_ge(shift_ready, i + 1)

                def score(u):
                    j, _, q0, n, diagonal = unit(u)
                    for s in range(2):
                        pe.wait_ge(probs_ready[s], NU * i + u)
                        pe.matmul(scores[s][:, 0:n], k_both[parity][s][:, j * P:(j + 1) * P], q_twice[parity][s][:, q0:q0 + n],
                                  start=True, stop=False)
                        ins = pe.matmul(scores[s][:, 0:n], k_high[parity][s][:, j * P:(j + 1) * P], q_low[parity][s][:, q0:q0 + n],
                                        start=False, stop=not diagonal)
                        if diagonal:
                            ins = pe.matmul(scores[s][:, 0:P], chip.identb[:], chip.mask_kq[:], start=False, stop=True)
                        ins.then_inc(score_ready[s], 1)

                if attend:
                    score(0)
                for u in range(NU):
                    j, c, q0, n, _ = unit(u)
                    for x in steps[u]:
                        run_job(x, Job(first, number[x], t, PER_TURN), i, parity)
                    if attend:
                        if u + 1 < NU:
                            score(u + 1)
                        if close and u < 2:
                            pe.wait_ge(normed_ready, 2 * (i - 1) + u + 1)
                        for s in range(2):
                            pe.wait_ge(probs_ready[s], NU * i + u + 1)
                            p = total[parity][s][:, c * CHUNK:(c + 1) * CHUNK] if u < 2 else probs[u % 2][s][:, 0:n]
                            pe.matmul(o_psum[c][64 * s:64 * s + 64, q0 - c * CHUNK:q0 - c * CHUNK + n], v[parity][s][:, j, :], p,
                                      start=(j == 0), stop=(j == 4 * c + 3)).then_inc(pv_done[s], 1)

            whole(pe, slot)

        @block.scalar
        def _(act):
            def run_job(x, job, i, parity):
                nxt, n_par = i + 1, 1 - parity
                src = spare[job.bank]
                if x[0] in ("q", "k"):
                    _, pair = where(nxt)
                    _, s, c = x
                    t = 0 if x[0] == "q" else 1
                    out = (q_twice if t == 0 else k_both)[n_par][s]
                    act.wait_ge(job_ready, job.done)
                    apart(act, chip)
                    nc.scalar.activation(out[:, c * CHUNK:(c + 1) * CHUNK], src[:], ACT.Identity, bias=bias(t, s, pair))\
                        .then_inc(high_ready, 1)
                elif x[0] == "v":
                    act.wait_ge(job_ready, job.done)
                    nc.scalar.copy(v[n_par][x[1]][:], src[:].rearrange("p (k e) -> p k e", e=DH0)).then_inc(bank_free[job.bank], 1)
                elif x[0] == "shift":
                    _, s, c = x
                    act.wait_ge(job_ready, job.done)
                    nc.scalar.copy(q_low[n_par][s][64:96, c * CHUNK:(c + 1) * CHUNK], src[64:96, :]).then_inc(bank_free[job.bank], 1)
                    if (s, c) == (1, 1):
                        act.wait_ge(bank_free[job.bank], job.before + 1)
                        act.sem_inc(shift_ready, 1)

            def slot(i, parity, t, first, close, prepare, attend):
                steps, number = slot_jobs(close, prepare)
                for u in range(NU):
                    _, c, _, n, _ = unit(u)
                    for s in range(2):
                        if not attend:
                            break
                        if u in (2, 3):
                            act.wait_ge(added[s], ADDS * i)
                        if u >= 4:
                            act.wait_ge(pv_done[s], NU * i + u - 1)
                            act.wait_ge(added[s], ADDS * i + u - 3)
                        act.wait_ge(score_ready[s], NU * i + u + 1)
                        out = total[parity][s][:, c * CHUNK:(c + 1) * CHUNK] if u < 2 else probs[u % 2][s][:, 0:n]
                        nc.scalar.activation(out, scores[s][:, 0:n], ACT.Exp, scale=SCALE).then_inc(probs_ready[s], 1)
                    for x in steps[u]:
                        run_job(x, Job(first, number[x], t, PER_TURN), i, parity)
                    if close and u in (1, 2):
                        c = u - 1
                        _, pair = where(i - 1)
                        act.wait_ge(normed_ready, 2 * (i - 1) + c + 1)
                        apart(act, chip)
                        nc.scalar.activation(o_high[c][:], normed[c][:], ACT.Identity, bias=chip.bv0[:, ds(pair, 1)])\
                            .then_inc(o_high_ready, 1)

            whole(act, slot)

        @block.gpsimd
        def _(pool):
            for par in range(2):
                for s in range(2):
                    nc.gpsimd.memset(q_low[par][s][64:96, :], 0.0)
                    nc.gpsimd.memset(k_high[par][s][64:96, :], 0.0).then_inc(pads_clear, 1)
            pool.wait_ge(pads_clear, 4)
            for par in range(2):
                for s in range(2):
                    nc.gpsimd.memset(k_high[par][s][64:65, :], SH).then_inc(pads_clear, 1)
            pool.wait_ge(pads_clear, 8)
            for s in range(2):
                ins = nc.gpsimd.memset(minus_max[s][:], 0.0)
            ins.then_inc(buffers_clear, 1)

            def slot(i, parity, t, first, close, prepare, attend):
                if not attend:
                    return
                for u in range(2, NU):
                    _, _, q0, n, _ = unit(u)
                    for s in range(2):
                        if u == 2:
                            pool.wait_ge(pv_done[s], NU * i + 2)
                        pool.wait_ge(added[s], ADDS * i + u - 2)
                        pool.wait_ge(probs_ready[s], NU * i + u + 1)
                        acc = total[parity][s][:, q0:q0 + n]
                        nc.gpsimd.tensor_tensor(acc, acc, probs[u % 2][s][:, 0:n], ALU.add).then_inc(added[s], 1)

            whole(pool, slot)

        @block.vector
        def _(dve):
            dve.wait_ge(buffers_clear, 1)

            def run_job(x, job, i, parity, number, jobs_of):
                nxt, n_par = i + 1, 1 - parity
                src = spare[job.bank]
                if x[0] in ("q", "k"):
                    _, pair = where(nxt)
                    _, s, c = x
                    at = slice(c * CHUNK, (c + 1) * CHUNK)
                    t = 0 if x[0] == "q" else 1
                    k = [y for y in number if y[0] in ("q", "k")].index(x)
                    dve.wait_ge(high_ready, HIGHS * nxt + k + 1)
                    if t == 0:
                        nc.vector.scalar_tensor_tensor(q_low[n_par][s][0:64, at], src[0:64, :], chip.bqk[0:64, ds(2 * pair + s, 1)],
                                                       q_twice[n_par][s][0:64, at], ALU.add, ALU.subtract)\
                            .then_inc(bank_free[job.bank], 1)
                    else:
                        low = k_both[n_par][s][64:128, at]
                        nc.vector.scalar_tensor_tensor(low, src[64:128, :], chip.bqk[64:128, ds(HEADS0 + 2 * pair + s, 1)], low,
                                                       ALU.add, ALU.subtract).then_inc(bank_free[job.bank], 1)
                        nc.vector.tensor_copy(k_high[n_par][s][0:64, at], k_both[n_par][s][0:64, at]).then_inc(split_ready, 1)
                elif x[0] == "max":
                    _, s, k, c = x
                    n = min(P * (k + 1) - CHUNK * c, CHUNK)
                    dve.wait_ge(job_ready, job.done)
                    nc.vector.tensor_reduce(maxima[s][:, c, k:k + 1], src[:, 0:n], AX_X, ALU.max).then_inc(bank_free[job.bank], 1)
                    if (k, c) == (7, 1):
                        dve.wait_ge(bank_free[job.bank], job.before + 1)
                        nc.vector.tensor_tensor(maxima[s][:, 0, 4:8], maxima[s][:, 0, 4:8], maxima[s][:, 1, 4:8], ALU.max)\
                            .then_inc(max_ready, 1)
                        dve.wait_ge(max_ready, 2 * nxt + s + 1)
                        nc.vector.tensor_scalar(minus_max[s][:, :, 0:1], maxima[s][:, 0, :].unsqueeze(2), -1.0 / SH, None, ALU.mult)\
                            .then_inc(minus_ready, 1)
                elif x[0] == "sum":
                    _, c = x
                    dve.wait_ge(job_ready, job.done)
                    nc.vector.transpose(turned[c][:], src[:]).then_inc(bank_free[job.bank], 1)
                    if c == 0:
                        return
                    for k in range(2):
                        dve.wait_ge(bank_free[job.bank], job.before + 1)
                        nc.vector.reciprocal(compact[k][:], turned[k][:].rearrange("p (a b) -> p a b", b=32)[:, :, 0])\
                            .then_inc(compact_ready, 1)
                    for k in range(2):
                        dve.wait_ge(compact_ready, 2 * (i - 1) + k + 1)
                        nc.vector.transpose(inverse[k][:], compact[k][:].unsqueeze(2).broadcast_to([P, CHUNK // 32, 32]))\
                            .then_inc(inverse_ready, 1)
                    for k in range(2):
                        dve.wait_ge(inverse_ready, 2 * (i - 1) + k + 1)
                        nc.vector.tensor_tensor(normed[k][:], o_psum[k][:], inverse[k][:], ALU.mult).then_inc(normed_ready, 1)
                elif x[0] == "out":
                    _, c = x
                    batch, _ = where(i - 1)
                    dve.wait_ge(job_ready, job.done)
                    here = tokens(chip.xT, batch, c * CHUNK, CHUNK)
                    nc.vector.scalar_tensor_tensor(here, src[:], chip.ga_scaled[:, ds(batch, 1)], here, ALU.mult, ALU.add)\
                        .then_inc(bank_free[job.bank], 1)

            def slot(i, parity, t, first, close, prepare, attend):
                steps, number = slot_jobs(close, prepare)
                for u in range(NU):
                    for x in steps[u]:
                        run_job(x, Job(first, number[x], t, PER_TURN), i, parity, number, None)
                    if close and u in (1, 2):
                        c = u - 1
                        _, pair = where(i - 1)
                        dve.wait_ge(o_high_ready, 2 * (i - 1) + c + 1)
                        nc.vector.scalar_tensor_tensor(o_low[c][:], normed[c][:], chip.bv0[:, ds(pair, 1)], o_high[c][:],
                                                       ALU.add, ALU.subtract).then_inc(o_low_ready, 1)

            whole(dve, slot)


def gates(nc, chip, layer):
    with ExitStack() as ctx:
        def sb(what, shape, dt):
            return ctx.enter_context(nc.sbuf_tensor(f"gates{layer}_{what}", shape, dt))

        def sem(what):
            return ctx.enter_context(nc.semaphore(f"gates{layer}_{what}"))

        logits = chip.logits
        gate, rest = sb("gate", [P, NTILE, EXPERTS], F32), sb("rest", [P, NTILE, EXPERTS], F32)
        parts = sb("parts", [P, NTILE, 3, EXPERTS], BF16)
        turned = [ctx.enter_context(nc.psum_tensor(f"gates{layer}_turned{k}", [3 * EXPERTS, 8 * P], BF16)) for k in range(4)]
        chain, parts_ready, turned_ready = sem("chain"), sem("parts_ready"), sem("turned_ready")
        if layer == 0:
            below, count, passed = sb("below", [P, NTILE * EXPERTS], F32), sb("count", [P, 1], F32), sb("passed", [P, 1], I32)
            key, bit, trial, flip, bound = (sb(w, [P, 1], I32) for w in ("key", "bit", "trial", "flip", "bound"))
            number = ctx.enter_context(nc.psum_tensor("gates0_number", [P, 1], F32))
            state_ready, trial_ready, flip_ready, bound_ready = (
                sem(w) for w in ("state_ready", "trial_ready", "flip_ready", "bound_ready"))
            counted, summed, passed_ready = sem("counted"), sem("summed"), sem("passed_ready")
        else:
            shifted, powers, ready = sb("shifted", [P, NTILE, EXPERTS], F32), sem("powers"), sem("ready")
            one, first, second = (sb(w, [P, NTILE, EXPERTS], F32) for w in ("one", "first", "second"))
            stat = sb("stat", [P, NTILE], F32)
        block = ctx.enter_context(nc.Block())

        @block.vector
        def _(dve):
            link = Link(dve, chain)
            if layer == 0:
                flat = logits[:].rearrange("p t e -> p (t e)")
                nc.vector.memset(key[:], 0)
                nc.vector.memset(bit[:], -(1 << 31)).then_inc(state_ready, 1)
                with dve.Fori(0, 32) as t:
                    dve.wait_ge(state_ready, t + 1)
                    nc.vector.tensor_tensor(trial[:], key[:], bit[:], ALU.bitwise_or).then_inc(trial_ready, 1)
                    dve.wait_ge(trial_ready, t + 1)
                    nc.vector.tensor_scalar(flip[:], trial[:], 31, 0x7FFFFFFF, ALU.arith_shift_right, ALU.bitwise_and)\
                        .then_inc(flip_ready, 1)
                    dve.wait_ge(flip_ready, t + 1)
                    nc.vector.scalar_tensor_tensor(bound[:], flip[:], -1, trial[:], ALU.bitwise_xor, ALU.bitwise_xor)\
                        .then_inc(bound_ready, 1)
                    dve.wait_ge(bound_ready, t + 1)
                    nc.vector.tensor_scalar(below[:], flat, bound[:].bitcast(F32), 0.0, ALU.is_lt, ALU.add, accum_out=count[:])\
                        .then_inc(counted, 1)
                    dve.wait_ge(summed, t + 1)
                    nc.vector.tensor_scalar(passed[:], number[:], float(KTH - 1), None, ALU.is_le).then_inc(passed_ready, 1)
                    dve.wait_ge(passed_ready, t + 1)
                    apart(dve, chip)
                    nc.vector.copy_predicated(key[:], passed[:], trial[:])
                    nc.vector.tensor_scalar(bit[:], bit[:], 1, None, ALU.logical_shift_right).then_inc(state_ready, 1)
                dve.wait_ge(state_ready, 33)
                link(nc.vector.tensor_scalar(flip[:], key[:], 31, 0x7FFFFFFF, ALU.arith_shift_right, ALU.bitwise_and))
                link(nc.vector.scalar_tensor_tensor(bound[:], flip[:], -1, key[:], ALU.bitwise_xor, ALU.bitwise_xor))
                link(nc.vector.scalar_tensor_tensor(gate[:], logits[:], bound[:].bitcast(F32), logits[:], ALU.is_ge, ALU.mult))
            else:
                def spread(a):
                    return a.unsqueeze(2).broadcast_to([P, NTILE, EXPERTS])

                link(nc.vector.tensor_reduce(stat[:], logits[:], AX_X, ALU.max))
                nc.vector.tensor_tensor(shifted[:], logits[:], spread(stat[:]), ALU.subtract).then_inc(ready, 1)
                dve.wait_ge(powers, 1)
                link(nc.vector.tensor_reduce(stat[:], one[:], AX_X, ALU.add))
                link(nc.vector.reciprocal(stat[:], stat[:]))
                link(nc.vector.tensor_tensor(shifted[:], one[:], spread(stat[:]), ALU.mult))
                at, n = CONST["prefer"]
                prefer = chip.consts[:, at:at + n].unsqueeze(1).broadcast_to([P, NTILE, EXPERTS])
                left = shifted
                for mark in (first, second):
                    link(nc.vector.tensor_reduce(stat[:], left[:], AX_X, ALU.max))
                    link(nc.vector.tensor_tensor(one[:], left[:], spread(stat[:]), ALU.is_equal))
                    link(nc.vector.tensor_tensor(one[:], one[:], prefer, ALU.mult))
                    link(nc.vector.tensor_reduce(stat[:], one[:], AX_X, ALU.max))
                    link(nc.vector.tensor_tensor(mark[:], one[:], spread(stat[:]), ALU.is_equal))
                    if mark is first:
                        link(nc.vector.scalar_tensor_tensor(rest[:], first[:], -2.0, shifted[:], ALU.mult, ALU.add))
                        left = rest
                link(nc.vector.tensor_tensor(one[:], first[:], second[:], ALU.add))
                link(nc.vector.tensor_tensor(one[:], one[:], shifted[:], ALU.mult))
                link(nc.vector.tensor_reduce(stat[:], one[:], AX_X, ALU.add))
                link(nc.vector.reciprocal(stat[:], stat[:]))
                link(nc.vector.tensor_tensor(gate[:], one[:], spread(stat[:]), ALU.mult))
            link(nc.vector.tensor_copy(parts[:, :, 0, :], gate[:]))
            link(nc.vector.tensor_tensor(rest[:], gate[:], parts[:, :, 0, :], ALU.subtract))
            link(nc.vector.tensor_copy(parts[:, :, 1, :], rest[:]))
            nc.vector.tensor_tensor(parts[:, :, 2, :], rest[:], parts[:, :, 1, :], ALU.subtract).then_inc(parts_ready, 1)
            for k in range(4):
                dve.wait_ge(turned_ready, k + 1)
                nc.vector.tensor_copy(chip.gates_f32[:, k * SEQ:(k + 1) * SEQ], turned[k][:])
                ins = nc.vector.tensor_copy(chip.gates_b16[:, k * SEQ:(k + 1) * SEQ], turned[k][:])
            link(ins)

        @block.scalar
        def _(act):
            if layer == 1:
                act.wait_ge(ready, 1)
                nc.scalar.activation(one[:], shifted[:], ACT.Exp).then_inc(powers, 1)

        @block.tensor
        def _(pe):
            if layer == 0:
                with pe.Fori(0, 32) as t:
                    pe.wait_ge(counted, t + 1)
                    pe.matmul(number[:], chip.ones[:], count[:], start=True, stop=True).then_inc(summed, 1)
            pe.wait_ge(parts_ready, 1)
            for k in range(4):
                for i in range(8):
                    ins = pe.transpose(turned[k][:, i * P:(i + 1) * P], parts[:, 8 * k + i, :, :].rearrange("p a e -> p (a e)"), chip.identb[:])
                ins.then_inc(turned_ready, 1)


def experts(nc, chip, layer, w_up, w_down, bias_name, bias_rows, ungated):
    TILES = EXPERTS * HT + ungated
    RING = 4
    AHEAD = RING
    with ExitStack() as ctx:
        def sem(what):
            return ctx.enter_context(nc.semaphore(f"experts{layer}_{what}"))

        hidden = [ctx.enter_context(nc.psum_tensor(f"hidden{layer}_{k}", [P, CHUNK], F32)) for k in range(RING)]
        gate = [ctx.enter_context(nc.psum_tensor(f"gate{layer}_{k}", [P, CHUNK], F32)) for k in range(2)]
        y = ctx.enter_context(nc.psum_tensor(f"y{layer}", [P, CHUNK], F32))
        active = [ctx.enter_context(nc.sbuf_tensor(f"active{layer}_{k}", [P, CHUNK], F32)) for k in range(RING)]
        weighed = [ctx.enter_context(nc.sbuf_tensor(f"weighed{layer}_{k}", [P, CHUNK], F32)) for k in range(RING)]
        high = [ctx.enter_context(nc.sbuf_tensor(f"weighed_high{layer}_{k}", [P, CHUNK], F16)) for k in range(RING)]
        low = [ctx.enter_context(nc.sbuf_tensor(f"weighed_low{layer}_{k}", [P, CHUNK], F16)) for k in range(RING)]
        up_ready, gate_ready, active_ready, weighed_ready = sem("up_ready"), sem("gate_ready"), sem("active_ready"), sem("weighed_ready")
        high_ready, low_ready = sem("high_ready"), sem("low_ready")
        down_done, y_ready, y_taken = sem("down_done"), sem("y_ready"), sem("y_taken")
        x_biased = sem("x_biased")
        block = ctx.enter_context(nc.Block())

        @block.tensor
        def _(pe):
            with pe.Fori(0, NCHUNK) as n:
                h_high, h_low = (h[:, ds(n * CHUNK, CHUNK)] for h in (chip.h_high, chip.h_low))

                def up(k):
                    if k >= RING:
                        pe.wait_ge(active_ready, n * TILES + k - RING + 1)
                    pe.matmul(hidden[k % RING][:], w_up[:, 0, k, :], h_high, start=True, stop=False)
                    pe.matmul(hidden[k % RING][:], w_up[:, 1, k, :], h_high, start=False, stop=False)
                    pe.matmul(hidden[k % RING][:], w_up[:, 0, k, :], h_low, start=False, stop=True).then_inc(up_ready, 1)

                def spread_gate(e):
                    if e >= 2:
                        pe.wait_ge(weighed_ready, n * TILES + ungated + HT * (e - 1))
                    apart(pe, chip)
                    pe.matmul(gate[e % 2][:], chip.gate_sel[:, e * P:(e + 1) * P], chip.gates_b16[:, ds(n * CHUNK, CHUNK)],
                              start=True, stop=True).then_inc(gate_ready, 1)

                for k in range(AHEAD):
                    up(k)
                spread_gate(0)
                for k in range(TILES):
                    if k + AHEAD < TILES:
                        up(k + AHEAD)
                    ahead = k + AHEAD - ungated
                    if ahead >= HT and ahead % HT == 0 and ahead // HT < EXPERTS:
                        spread_gate(ahead // HT)
                    if k == 0:
                        pe.wait_ge(y_taken, n)
                    pe.wait_ge(high_ready, n * TILES + k + 1)
                    pe.matmul(y[:], w_down[:, 0, k, :], high[k % RING][:], start=(k == 0), stop=False)
                    pe.matmul(y[:], w_down[:, 1, k, :], high[k % RING][:], start=False, stop=False)
                    pe.wait_ge(low_ready, n * TILES + k + 1)
                    pe.matmul(y[:], w_down[:, 0, k, :], low[k % RING][:], start=False, stop=False).then_inc(down_done, 1)
                pe.matmul(y[:], bias_rows[:], chip.gates_f32[:, ds(n * CHUNK, CHUNK)], start=False, stop=True).then_inc(y_ready, 1)

        @block.scalar
        def _(act):
            with act.Fori(0, NCHUNK) as n:
                def split(k):
                    if k >= RING:
                        act.wait_ge(down_done, n * TILES + k - RING + 1)
                    act.wait_ge(weighed_ready, n * TILES + k + 1)
                    nc.scalar.copy(high[k % RING][:], weighed[k % RING][:]).then_inc(high_ready, 1)

                for k in range(TILES):
                    if k >= RING:
                        act.wait_ge(weighed_ready, n * TILES + k - RING + 1)
                    act.wait_ge(up_ready, n * TILES + k + 1)
                    nc.scalar.activation(active[k % RING][:], hidden[k % RING][:], ACT.Gelu_apprx_tanh, bias=col(chip, bias_name, k),
                                         scale=1.0 / WS).then_inc(active_ready, 1)
                    if k >= 1:
                        split(k - 1)
                split(TILES - 1)

        @block.gpsimd
        def _(pool):
            with pool.Fori(0, NCHUNK) as n:
                for k in range(TILES):
                    pool.wait_ge(high_ready, n * TILES + k + 1)
                    nc.gpsimd.tensor_tensor(low[k % RING][:], weighed[k % RING][:], high[k % RING][:], ALU.subtract).then_inc(low_ready, 1)

        @block.vector
        def _(dve):
            with dve.Fori(0, NCHUNK) as n:
                here = chip.xT[:, ds(n * CHUNK, CHUNK)]
                if layer == 1:
                    nc.vector.tensor_scalar(here, here, chip.g_bias[:, 2, ds(n // 2, 1)], None, ALU.add).then_inc(x_biased, 1)
                for k in range(TILES):
                    e = (k - ungated) // HT
                    if k >= ungated and (k - ungated) % HT == 0:
                        dve.wait_ge(gate_ready, n * EXPERTS + e + 1)
                    if k >= RING:
                        dve.wait_ge(low_ready, n * TILES + k - RING + 1)
                    dve.wait_ge(active_ready, n * TILES + k + 1)
                    if k < ungated:
                        nc.vector.tensor_scalar(weighed[k % RING][:], active[k % RING][:], GS, None, ALU.mult).then_inc(weighed_ready, 1)
                    else:
                        nc.vector.tensor_tensor(weighed[k % RING][:], active[k % RING][:], gate[e % 2][:], ALU.mult).then_inc(weighed_ready, 1)
                dve.wait_ge(y_ready, n + 1)
                if layer == 1:
                    dve.wait_ge(x_biased, n + 1)
                nc.vector.scalar_tensor_tensor(here, y[:], chip.gb_scaled[:, layer, ds(n // 2, 1)], here, ALU.mult, ALU.add)\
                    .then_inc(y_taken, 1)


def project1(nc, chip, dram):
    with ExitStack() as ctx:
        def sb(name, shape, dt):
            return ctx.enter_context(nc.sbuf_tensor(name, shape, dt))

        def sem(name):
            return ctx.enter_context(nc.semaphore(name))

        Q, K, V, QR, KR = range(5)
        raw = sb("w1_attn", [P, 5, CH], F32)
        w = sb("w1_attn_split", [P, 2, 5, CH], F16)
        straight = [[sb(f"straight{x}{u}", [P, CHUNK], F32) for u in range(2)] for x in range(2)]
        turned = [[sb(f"rope_turned{x}{u}", [P, CHUNK], F32) for u in range(2)] for x in range(2)]
        psum = [ctx.enter_context(nc.psum_tensor(f"project{k}", [P, CHUNK], F32)) for k in range(8)]
        chain, split_ready, project_ready, value_taken = sem("project_chain"), sem("project_split"), sem("project_ready"), sem("value_taken")
        straight_ready, turned_ready, rotated, high_ready = sem("straight_ready"), sem("turned1_ready"), sem("rotated"), sem("high1_ready")
        block = ctx.enter_context(nc.Block())
        highs = (chip.q1[0], chip.k1[0])
        lows = (chip.q1[1], chip.k1[1])

        @block.tensor
        def _(pe):
            pe.wait_ge(split_ready, 1)
            with pe.Fori(0, BATCH) as t:
                for u in range(2):
                    at = ds(t * SEQ + u * CHUNK, CHUNK)
                    for x in range(2):
                        for part, k in enumerate(((Q, QR), (K, KR))[x]):
                            out = psum[4 * u + 2 * x + part][:]
                            pe.wait_ge(rotated, 4 * t)
                            pe.matmul(out, w[:, 0, k, :], chip.h_high[:, at], start=True, stop=False)
                            pe.matmul(out, w[:, 1, k, :], chip.h_high[:, at], start=False, stop=False)
                            pe.matmul(out, w[:, 0, k, :], chip.h_low[:, at], start=False, stop=True).then_inc(project_ready, 1)

        @block.scalar
        def _(act):
            with act.Fori(0, BATCH) as t:
                for u in range(2):
                    for x in range(2):
                        act.wait_ge(rotated, 4 * t + 2 * u + x + 1)
                        apart(act, chip)
                        nc.scalar.copy(highs[x][:, ds(t * SEQ + u * CHUNK, CHUNK)], straight[x][u][:]).then_inc(high_ready, 1)

        @block.vector
        def _(dve):
            link = Link(dve, chain)
            link(nc.vector.tensor_copy(raw[:, 0:3, :], chip.w1_attn_raw[:]))
            for x in range(2):
                src = raw[:, x, :].rearrange("c (i two) -> c i two", two=2)
                dst = raw[:, QR + x, :].rearrange("c (i two) -> c i two", two=2)
                link(nc.vector.tensor_scalar(dst[:, :, 0:1], src[:, :, 1:2], -1.0, None, ALU.mult))
                link(nc.vector.tensor_copy(dst[:, :, 1:2], src[:, :, 0:1]))
            link(nc.vector.tensor_scalar(w[:, 0, :, :], raw[:], WS, None, ALU.mult))
            nc.vector.scalar_tensor_tensor(w[:, 1, :, :], raw[:], WS, w[:, 0, :, :], ALU.mult, ALU.subtract).then_inc(split_ready, 1)
            with dve.Fori(0, BATCH) as t:
                for u in range(2):
                    at = CONST["cos"][0] + u * CHUNK
                    cos = chip.consts[:, at:at + CHUNK]
                    at = CONST["sin"][0] + u * CHUNK
                    sin = chip.consts[:, at:at + CHUNK]
                    for x in range(2):
                        dve.wait_ge(project_ready, 8 * t + 4 * u + 2 * x + 1)
                        nc.vector.scalar_tensor_tensor(straight[x][u][:], psum[4 * u + 2 * x][:], chip.bqk1[:, x:x + 1], cos, ALU.add, ALU.mult)\
                            .then_inc(straight_ready, 1)
                        dve.wait_ge(project_ready, 8 * t + 4 * u + 2 * x + 2)
                        nc.vector.scalar_tensor_tensor(turned[x][u][:], psum[4 * u + 2 * x + 1][:], chip.bqk1[:, 2 + x:3 + x], sin, ALU.add, ALU.mult)\
                            .then_inc(turned_ready, 1)
                    for x in range(2):
                        dve.wait_ge(turned_ready, 4 * t + 2 * u + x + 1)
                        dve.wait_ge(straight_ready, 4 * t + 2 * u + x + 1)
                        nc.vector.tensor_tensor(straight[x][u][:], straight[x][u][:], turned[x][u][:], ALU.add).then_inc(rotated, 1)
                    for x in range(2):
                        dve.wait_ge(high_ready, 4 * t + 2 * u + x + 1)
                        chunk = ds(t * SEQ + u * CHUNK, CHUNK)
                        nc.vector.tensor_tensor(lows[x][:, chunk], straight[x][u][:], highs[x][:, chunk], ALU.subtract)

    with ExitStack() as ctx:
        psum = [ctx.enter_context(nc.psum_tensor(f"value_rows{k}", [P, CHUNK], F32)) for k in range(2)]
        w = ctx.enter_context(nc.sbuf_tensor("wv1_split", [P, 2, CH], F16))
        v_split, v_ready, v_taken = (ctx.enter_context(nc.semaphore(x)) for x in ("v_split", "v_ready", "v_taken"))
        block = ctx.enter_context(nc.Block())

        @block.tensor
        def _(pe):
            pe.wait_ge(v_split, 2)
            for n in range(NCHUNK):
                if n >= 2:
                    pe.wait_ge(v_taken, n - 1)
                for i in range(4):
                    out = psum[n % 2][:, i * P:(i + 1) * P]
                    at = n * CHUNK + i * P
                    pe.matmul(out, chip.h_high[:, at:at + P], w[:, 0, :], start=True, stop=False)
                    pe.matmul(out, chip.h_high[:, at:at + P], w[:, 1, :], start=False, stop=False)
                    ins = pe.matmul(out, chip.h_low[:, at:at + P], w[:, 0, :], start=False, stop=True)
                ins.then_inc(v_ready, 1)

        @block.scalar
        def _(act):
            for n in range(NCHUNK):
                act.wait_ge(v_ready, n + 1)
                nc.scalar.copy(chip.v1[:, 4 * n:4 * n + 4, :], psum[n % 2][:].rearrange("p (a b) -> p a b", a=4)).then_inc(v_taken, 1)

        @block.vector
        def _(dve):
            nc.vector.tensor_scalar(w[:, 0, :], chip.w1_attn_raw[:, 2, :], WS, None, ALU.mult).then_inc(v_split, 1)
            dve.wait_ge(v_split, 1)
            nc.vector.scalar_tensor_tensor(w[:, 1, :], chip.w1_attn_raw[:, 2, :], WS, w[:, 0, :], ALU.mult, ALU.subtract).then_inc(v_split, 1)


STEPS1 = 2 * (SEQ // P)
MAX_JOBS = [("max", j, k) for j in range(4) for k in range(SEQ // P)]
SHIFT_STEP, SPREAD_STEP, MASK_STEP, CLOSE_STEPS = 0, 4, 6, (9, 12)


def slot_jobs1(shift, maxima, spread, close):
    steps = [[] for _ in range(STEPS1)]
    for n, x in enumerate(MAX_JOBS if maxima else []):
        steps[n * STEPS1 // len(MAX_JOBS)].append(x)
    if shift:
        steps[SHIFT_STEP].append(("shift",))
    if spread:
        steps[SPREAD_STEP].append(("xq",))
        steps[SPREAD_STEP + 1].append(("xk",))
    if close:
        for c, u in enumerate(CLOSE_STEPS):
            steps[u].append(("close", c))
    number = {}
    for step in steps:
        for x in step:
            number[x] = len(number)
    return steps, number


PER_QUAD = len(slot_jobs1(True, True, True, False)[1])
CLOSE_JOBS = len(CLOSE_STEPS)


def attention1(nc, chip):
    SCALE = 1.0 / (float(np.sqrt(DH1)) * WS * WS)
    PER_TURN = QUADS * PER_QUAD + CLOSE_JOBS
    UNITS1 = 4 * STEPS1
    assert PER_TURN % 2 == 0
    with ExitStack() as ctx:
        def sb(name, shape, dt):
            return ctx.enter_context(nc.sbuf_tensor(name, shape, dt))

        def sem(name):
            return ctx.enter_context(nc.semaphore(name))

        xq = [sb(f"xq{g}", [P, SEQ], F16) for g in range(QUADS)]
        xq_shift = [sb(f"xq_shift{v}", [P, SEQ], F16) for v in range(2)]
        xk = [sb(f"xk{v}", [P, SEQ], F16) for v in range(2)]
        xk_head = [[sb(f"xk{g}_head{j}", [P, SEQ], F16) for j in range(4)] for g in range(2)]
        xk_head += [[h[:, j * SEQ:(j + 1) * SEQ] for j in range(4)] for h in (chip.h_high, chip.h_low)]
        values = [sb(f"values{v}", [P, SEQ // P, 4, 32], F32) for v in range(2)]
        probs = [[sb(f"probs1_{v}{j}", [P, CHUNK], F32) for j in range(4)] for v in range(2)]
        context = [sb(f"context{g}", [P, SEQ], F32) for g in range(QUADS)]
        maxima = sb("quad_maxima", [P, 4, SEQ // P], F32)
        minus_max = sb("quad_minus_max", [P, SEQ // P, P], F16)
        turned, inverse, normed = ([sb(f"batch_{what}{c}", [P, CHUNK], F32) for c in range(2)] for what in ("turned", "inverse", "normed"))
        compact = [sb(f"batch_compact{c}", [P, CHUNK // 32, 32 // DH1], F32) for c in range(2)]
        wide = [ctx.enter_context(nc.psum_tensor(f"wide{k}", [P, SEQ], F32)) for k in range(2)]
        scores = [ctx.enter_context(nc.psum_tensor(f"scores1_{k}", [P, CHUNK], F32)) for k in range(2)]
        o_psum = [ctx.enter_context(nc.psum_tensor(f"o1_{c}", [P, CHUNK], F32)) for c in range(2)]

        pads_clear, buffers_clear = sem("pads1_clear"), sem("buffers1_clear")
        job_ready = sem("job1_ready")
        wide_free = [sem(f"wide_free{k}") for k in range(2)]
        xk_ready, minus_ready, shift_ready = sem("xk_ready"), sem("minus1_ready"), sem("shift1_ready")
        values_ready = sem("values_ready")
        score_ready, probs_ready, pv_done = sem("score1_ready"), sem("probs1_ready"), sem("pv1_done")
        sums_turned = sem("sums1_turned")
        o_taken, compact_ready, inverse_ready = sem("o1_taken"), sem("compact1_ready"), sem("inverse1_ready")
        block = ctx.enter_context(nc.Block())

        class Job1:
            def __init__(self, first, k, t):
                n = first + k
                self.bank = n % 2
                self.before = n // 2 + PER_TURN // 2 * t
                self.done = n + 1 + PER_TURN * t

        def after(b, g, n):
            return b + (g + n) // QUADS, (g + n) % QUADS

        def whole(run, slot):
            first = 0

            def next_slot(b, g, t, has, attend=True):
                nonlocal first
                slot(b, g, t, first, has, attend)
                first += len(slot_jobs1(*has)[1])

            next_slot(0, -3, 0, (False, False, True, False), False)
            next_slot(0, -2, 0, (False, True, True, False), False)
            next_slot(0, -1, 0, (True, True, True, False), False)
            next_slot(0, 0, 0, (True, True, True, False))
            with run.Fori(0, BATCH - 1) as t:
                for g in range(1, QUADS):
                    next_slot(t, g, t, (True, True, True, False))
                next_slot(t + 1, 0, t, (True, True, True, True))
            first += PER_TURN * (BATCH - 2)
            for g in range(1, QUADS):
                next_slot(BATCH - 1, g, 0, (g + 1 < QUADS, g + 2 < QUADS, g + 3 < QUADS, False))
            next_slot(BATCH, 0, 0, (False, False, False, True), False)

        @block.tensor
        def _(pe):
            pe.wait_ge(buffers_clear, 1)

            def run_job(x, job, b, g):
                out = wide[job.bank]
                nb, ng = after(b, g, {"shift": 1, "max": 2, "xq": 3, "xk": 3, "close": 0}[x[0]])
                pe.wait_ge(wide_free[job.bank], job.before)

                def spread(c, sel, x, last):
                    o = out[:, c * CHUNK:(c + 1) * CHUNK]
                    for half in range(2):
                        ins = pe.matmul(o, sel[:, (2 * ng + half) * P:(2 * ng + half + 1) * P], x[half][:, ds(nb * SEQ + c * CHUNK, CHUNK)],
                                        start=(half == 0), stop=(half == 1 and last))
                    return ins

                if x[0] == "xq":
                    spread(0, chip.q_sel, chip.q1, True)
                    ins = spread(1, chip.q_sel, chip.q1, True)
                elif x[0] == "xk":
                    spread(0, chip.k_sel, chip.k1, True)
                    ins = spread(1, chip.k_sel, chip.k1, True)
                elif x[0] == "max":
                    _, j, k = x
                    if k == 0:
                        pe.wait_ge(xk_ready, 4 * (QUADS * b + g + 2) + j + 1)
                    for c in range(2):
                        ins = pe.matmul(out[:, c * CHUNK:(c + 1) * CHUNK], xq[ng][:, k * P:(k + 1) * P],
                                        xk_head[ng][j][:, c * CHUNK:(c + 1) * CHUNK], start=True, stop=True)
                elif x[0] == "close":
                    c = x[1]
                    pe.wait_ge(o_taken, 2 * QUADS * b)
                    for n, name in enumerate(("place_ctx", "place_sum")):
                        for q in range(QUADS):
                            ins = pe.matmul(out[32 * q:32 * q + 32, n * CHUNK:(n + 1) * CHUNK], const(chip, name),
                                            context[q][:, c * CHUNK:(c + 1) * CHUNK], start=True, stop=True, tile_position=(0, 32 * q))
                else:
                    pe.wait_ge(minus_ready, QUADS * b + g + 2)
                    for c in range(2):
                        spread(c, chip.q_sel, chip.q1, False)
                        for k in range(4):
                            at = c * CHUNK + k * P
                            ins = pe.matmul(out[:, at:at + P], minus_max[:, 4 * c + k, :], chip.ident16[:], start=False, stop=(k == 3))
                ins.then_inc(job_ready, 1)

            def pv(i, u, g):
                k, c = u // 2, u % 2
                if u < 2:
                    pe.wait_ge(o_taken, 2 * i)
                for j in range(4):
                    pe.wait_ge(probs_ready, UNITS1 * i + 4 * u + j + 1)
                    pe.matmul(o_psum[c][32 * j:32 * j + 32, :], values[g % 2][:, k, j, :], probs[u % 2][j][:],
                              start=(k == 0), stop=(k == SEQ // P - 1), tile_position=(0, 32 * j)).then_inc(pv_done, 1)

            def slot(b, g, t, first, has, attend):
                i = QUADS * b + g
                steps, number = slot_jobs1(*has)

                def jobs(some):
                    for x in some:
                        run_job(x, Job1(first, number[x], t), b, g)

                if attend:
                    pe.wait_ge(shift_ready, i + 1)
                    pe.wait_ge(values_ready, i + 1)
                for u in range(STEPS1):
                    k, c = u // 2, u % 2
                    for j in range(4 if attend else 0):
                        pe.wait_ge(probs_ready, UNITS1 * i + max(4 * u + j - 1, 0))
                        pe.matmul(scores[j % 2][:], xk_head[g][j][:, k * P:(k + 1) * P],
                                  xq_shift[g % 2][:, c * CHUNK:(c + 1) * CHUNK], start=True, stop=True).then_inc(score_ready, 1)
                        if j == 0:
                            jobs(steps[u][0:1])
                        elif j == 1:
                            jobs(steps[u][1:-1])
                        elif j == 2 and u > 0:
                            pv(i, u - 1, g)
                    jobs(steps[u][1:][-1:] if attend else steps[u])
                if attend:
                    pv(i, STEPS1 - 1, g)

            whole(pe, slot)

        @block.scalar
        def _(act):
            def slot(b, g, t, first, has, attend):
                i = QUADS * b + g
                steps, number = slot_jobs1(*has)
                for u in range(STEPS1):
                    for j in range(4 if attend else 0):
                        if u >= 2:
                            act.wait_ge(pv_done, UNITS1 * i + 4 * (u - 2) + j + 1)
                        act.wait_ge(score_ready, UNITS1 * i + 4 * u + j + 1)
                        nc.scalar.activation(probs[u % 2][j][:], scores[j % 2][:], ACT.Exp, scale=SCALE).then_inc(probs_ready, 1)
                    for x in steps[u]:
                        job = Job1(first, number[x], t)
                        if x[0] in ("max", "close"):
                            continue
                        act.wait_ge(job_ready, job.done)
                        src = wide[job.bank][:]
                        if x[0] == "xq":
                            nc.scalar.copy(xq[(g + 3) % QUADS][:], src).then_inc(wide_free[job.bank], 1)
                        elif x[0] == "xk":
                            nc.scalar.activation(xk[(g + 1) % 2][:], src, ACT.Identity, bias=const(chip, "key_pad")).then_inc(wide_free[job.bank], 1)
                        else:
                            nc.scalar.copy(xq_shift[(g + 1) % 2][:], src).then_inc(wide_free[job.bank], 1)
                            act.wait_ge(wide_free[job.bank], job.before + 1)
                            act.sem_inc(shift_ready, 1)
                if attend:
                    for c in range(2):
                        act.wait_ge(pv_done, UNITS1 * i + 4 * (STEPS1 - 2 + c) + 4)
                        nc.scalar.copy(context[g][:, c * CHUNK:(c + 1) * CHUNK], o_psum[c][:]).then_inc(o_taken, 1)

            whole(act, slot)

        @block.gpsimd
        def _(pool):
            for v in range(2):
                ins = nc.gpsimd.memset(values[v][:], 0.0).then_inc(pads_clear, 1)
            pool.wait_ge(pads_clear, 2)
            for v in range(2):
                nc.gpsimd.memset(values[v][:, :, :, DH1:DH1 + 1], WS).then_inc(pads_clear, 1)
            nc.gpsimd.memset(minus_max[:], 0.0).then_inc(pads_clear, 1)
            pool.wait_ge(pads_clear, 5)
            pool.sem_inc(buffers_clear, 1)

            def slot(b, g, t, first, has, attend):
                if not has[0]:
                    return
                nb, ng = after(b, g, 1)
                par = (g + 1) % 2
                pool.wait_ge(job_ready, Job1(first, 0, t).done)
                apart(pool, chip)
                src = chip.v1[:, ds(8 * nb, 8), 32 * ng:32 * ng + 32].rearrange("p k (j d) -> p k j d", j=4)
                nc.gpsimd.tensor_copy(values[par][:, :, :, 0:DH1], src).then_inc(values_ready, 1)

            whole(pool, slot)

        @block.vector
        def _(dve):
            dve.wait_ge(buffers_clear, 1)

            def close(b, c, job):
                n = 2 * (b - 1) + c + 1
                out, sums = (wide[job.bank][:, k * CHUNK:(k + 1) * CHUNK] for k in range(2))
                dve.wait_ge(job_ready, job.done)
                nc.vector.transpose(turned[c][:], sums).then_inc(sums_turned, 1)
                dve.wait_ge(sums_turned, n)
                nc.vector.reciprocal(compact[c][:], turned[c][:].rearrange("p (a j d) -> p a j d", j=32 // DH1, d=DH1)[:, :, :, 0])\
                    .then_inc(compact_ready, 1)
                dve.wait_ge(compact_ready, n)
                nc.vector.transpose(inverse[c][:].rearrange("p (a j d) -> p a j d", j=32 // DH1, d=DH1),
                                    compact[c][:].unsqueeze(3).broadcast_to([P, CHUNK // 32, 32 // DH1, DH1])).then_inc(inverse_ready, 1)
                dve.wait_ge(inverse_ready, n)
                nc.vector.tensor_tensor(normed[c][:], out, inverse[c][:], ALU.mult).then_inc(wide_free[job.bank], 1)
                dve.wait_ge(wide_free[job.bank], job.before + 1)
                here = chip.xT[:, ds((b - 1) * SEQ + c * CHUNK, CHUNK)]
                nc.vector.scalar_tensor_tensor(here, normed[c][:], chip.mod[:, 1, GA, ds(b - 1, 1)], here, ALU.mult, ALU.add)

            def slot(b, g, t, first, has, attend):
                steps, number = slot_jobs1(*has)
                if has[1]:
                    dve.wait_ge(minus_ready, QUADS * b + g + 2)
                for u in range(STEPS1):
                    if has[2] and u == MASK_STEP:
                        job = Job1(first, number[("xk",)], t)
                        dve.wait_ge(wide_free[job.bank], job.before + 1)
                        for j in range(4):
                            nc.vector.tensor_scalar(xk_head[(g + 3) % QUADS][j][:], xk[(g + 1) % 2][:], const(chip, "head_rows")[:, j:j + 1], None,
                                                    ALU.mult).then_inc(xk_ready, 1)
                    for x in steps[u]:
                        if x[0] == "close":
                            close(b, x[1], Job1(first, number[x], t))
                        if x[0] != "max":
                            continue
                        _, j, k = x
                        job = Job1(first, number[x], t)
                        dve.wait_ge(job_ready, job.done)
                        nc.vector.tensor_reduce(maxima[:, j, k:k + 1], wide[job.bank][:], AX_X, ALU.max).then_inc(wide_free[job.bank], 1)
                if not has[1]:
                    return
                for x in MAX_JOBS[-2:]:
                    job = Job1(first, number[x], t)
                    dve.wait_ge(wide_free[job.bank], job.before + 1)
                out = minus_max[:].rearrange("p k (j r) -> p j k r", j=4)[:, :, :, 3 * DH1:3 * DH1 + 1]
                nc.vector.tensor_scalar(out, maxima[:].unsqueeze(3), -1.0 / SH, None, ALU.mult).then_inc(minus_ready, 1)

            whole(dve, slot)


def load_mlp1(nc, chip, dram):
    with ExitStack() as ctx:
        tiles = HT * (EXPERTS + 1)
        PIECES = 3
        size = tiles // PIECES
        raw = [ctx.enter_context(nc.sbuf_tensor(f"{name}_raw", [P, tiles, P], F32)) for name in ("up1", "down1")]
        up_loaded, down_loaded, high = (ctx.enter_context(nc.semaphore(x)) for x in ("up1_loaded", "down1_loaded", "mlp1_high"))
        block = ctx.enter_context(nc.Block())
        pieces = [(split[:, :, k * size:(k + 1) * size, :], raw[which][:, k * size:(k + 1) * size, :])
                  for which, split in enumerate((chip.up1, chip.down1)) for k in range(PIECES)]

        @block.sync
        def _(sp):
            up = raw[0][:].rearrange("p k m -> p (k m)")
            sp.dma_start(up[:, 0:HID], dram["L1_ffn_Wfc_s"]).then_inc(up_loaded, 16)
            sp.dma_start(up[:, HID:].rearrange("c (e h) -> c e h", e=EXPERTS), dram["L1_ffn_Wfc"].rearrange("e c h -> c e h")).then_inc(up_loaded, 16)
            sp.dma_start(raw[1][:, 0:HT, :], dram["L1_ffn_Wproj_s"].rearrange("(j p) d -> p j d", p=P)).then_inc(down_loaded, 16)
            sp.dma_start(raw[1][:, HT:, :], dram["L1_ffn_Wproj"].rearrange("e (j p) d -> p (e j) d", p=P)).then_inc(down_loaded, 16)

        @block.scalar
        def _(act):
            for k, (split, src) in enumerate(pieces):
                if k == 0:
                    act.wait_ge(up_loaded, 32)
                if k == PIECES:
                    act.wait_ge(down_loaded, 32)
                nc.scalar.mul(split[:, 0], src, WS).then_inc(high, 1)

        @block.vector
        def _(dve):
            for k, (split, src) in enumerate(pieces):
                dve.wait_ge(high, k + 1)
                nc.vector.scalar_tensor_tensor(split[:, 1], src, WS, split[:, 0], ALU.mult, ALU.subtract)


def store(nc, chip, out):
    with ExitStack() as ctx:
        def sem(name):
            return ctx.enter_context(nc.semaphore(name))

        turned = [ctx.enter_context(nc.psum_tensor(f"turned{u}", [P, CHUNK], F32)) for u in range(2)]
        rows = [ctx.enter_context(nc.sbuf_tensor(f"out_rows{u}", [P, 4, CH], F32)) for u in range(2)]
        out_turned, out_copied = sem("out_turned"), sem("out_copied")
        out_stored = [sem(f"out_stored{u}") for u in range(2)]
        view = out.rearrange("b (t p) c -> p (b t) c", p=P)
        block = ctx.enter_context(nc.Block())

        @block.tensor
        def _(pe):
            for n in range(NCHUNK):
                if n >= 2:
                    pe.wait_ge(out_copied, n - 1)
                for i in range(4):
                    at = n * CHUNK + i * P
                    ins = pe.transpose(turned[n % 2][:, i * P:(i + 1) * P], chip.xT[:, at:at + P], const(chip, "ident"))
                ins.then_inc(out_turned, 1)

        @block.vector
        def _(dve):
            for n in range(NCHUNK):
                dve.wait_ge(out_turned, n + 1)
                if n >= 2:
                    dve.wait_ge(out_stored[n % 2], 16 * (n // 2))
                nc.vector.tensor_copy(rows[n % 2][:], turned[n % 2][:].rearrange("p (i c) -> p i c", i=4)).then_inc(out_copied, 1)

        @block.sync
        def _(sp):
            for n in range(NCHUNK):
                sp.wait_ge(out_copied, n + 1)
                sp.dma_start(view[:, 4 * n:4 * n + 4, :], rows[n % 2][:]).then_inc(out_stored[n % 2], 16)
            for u in range(2):
                sp.wait_ge(out_stored[u], 16 * NCHUNK // 2)


def clear_semaphores(nc):
    with nc.Block() as block:
        @block.sync
        def _(sp):
            for used in sorted(nc.released_uncleared_semaphores):
                sp.sem_clear(range(used, used + 1))


def program(nc, dram, out, stages=99):
    chip = Chip()
    with ExitStack() as whole:
        chip.apart = whole.enter_context(nc.semaphore("apart"))

        def keep(name, shape, dt, ctx=whole):
            return ctx.enter_context(nc.sbuf_tensor(name, shape, dt))

        chip.xT = keep("xT", [P, TOK], F32)
        chip.h_high = keep("h_high", [P, TOK], F16)
        chip.h_low = keep("h_low", [P, TOK], F16)
        chip.consts = keep("consts_sb", [P, CONST_COLS], F32)
        chip.cols = keep("cols", [P, ROWS], F32)
        chip.bqk = keep("bqk", [P, 2 * HEADS0], F32)
        chip.bqk1 = keep("bqk1", [P, 4], F32)
        chip.bv0 = chip.cols[:, ROW_AT["bv0"][0]:ROW_AT["bv0"][0] + PAIRS]
        chip.mod = keep("mod", [P, 2, 6, BATCH], F32)
        chip.g_bias = keep("g_bias", [P, 3, BATCH], F32)
        chip.ga_scaled = keep("ga_scaled", [P, BATCH], F32)
        chip.gb_scaled = keep("gb_scaled", [P, 2, BATCH], F32)
        chip.mean_ones = keep("mean_ones", [P, P], F32)
        chip.ones = keep("ones", [P, P], F32)
        chip.sum_ones = keep("sum_ones", [P, DH0], F32)
        chip.eps = keep("eps", [P, 1], F32)
        chip.ident16 = keep("ident16", [P, P], F16)
        chip.identb = keep("identb", [P, P], BF16)
        chip.mask_qk = keep("mask_qk", [P, P], BF16)
        chip.mask_kq = keep("mask_kq", [P, P], BF16)
        chip.gate_sel = keep("gate_sel", [3 * EXPERTS, EXPERTS * P], BF16)
        chip.q_sel = keep("q_sel", [P, QUADS * 2 * P], F16)
        chip.k_sel = keep("k_sel", [P, QUADS * 2 * P], F16)
        chip.w_router1 = keep("w_router1", [P, EXPERTS], F32)
        chip.w1_attn_raw = keep("w1_attn_raw", [P, 3, CH], F32)
        chip.b2_rows = keep("b2_rows", [3 * EXPERTS, CH], F32)
        chip.bproj_rows = keep("bproj_rows", [3 * EXPERTS, CH], F32)

        with ExitStack() as layer0:
            chip.w1T = keep("w1T", [P, 2, EXPERTS * HT, P], F16, layer0)
            chip.w2T = keep("w2T", [P, 2, EXPERTS * HT, P], F16, layer0)
            with ExitStack() as att:
                chip.w_qk = keep("w_qk", [P, 2, HEADS0, 2, 2, DH0], F16, att)
                chip.w_v = keep("w_v", [P, 2, HEADS0 * DH0], F16, att)
                chip.w_out = keep("w_out", [P, 2, PAIRS, CH], F16, att)
                with ExitStack() as raw:
                    chip.w_qkv_raw = keep("w_qkv_raw", [P, 3 * HEADS0 * DH0], F32, raw)
                    chip.w_out_raw = keep("w_out_raw", [P, PAIRS, CH], F32, raw)
                    setup(nc, chip, dram)
                layer_norm(nc, chip, "ln1", 0, SA, CA)
                if stages >= 1:
                    attention0(nc, chip)
            if stages >= 2:
                with ExitStack() as mlp:
                    chip.logits = keep("logits0", [P, NTILE, EXPERTS], F32, mlp)
                    chip.gates_b16 = keep("gates0_b16", [3 * EXPERTS, TOK], BF16, mlp)
                    chip.gates_f32 = keep("gates0_f32", [3 * EXPERTS, TOK], F32, mlp)
                    layer_norm(nc, chip, "ln2", 0, SB, CB, bias_of=0, router=chip.cols[:, ROW_AT["gate0"][0]:ROW_AT["gate0"][0] + EXPERTS],
                               logits=chip.logits)
                    gates(nc, chip, 0)
                    experts(nc, chip, 0, chip.w1T, chip.w2T, "b1", chip.b2_rows, 0)
        clear_semaphores(nc)
        with ExitStack() as layer1:
            if stages >= 3:
                layer_norm(nc, chip, "ln3", 1, SA, CA)
                with ExitStack() as att:
                    chip.q1 = [keep(f"q1_{half}", [P, TOK], F16, att) for half in range(2)]
                    chip.k1 = [keep(f"k1_{half}", [P, TOK], F16, att) for half in range(2)]
                    chip.v1 = keep("v1", [P, NTILE, CH], F32, att)
                    project1(nc, chip, dram)
                    attention1(nc, chip)
            if stages >= 4:
                chip.logits = keep("logits1", [P, NTILE, EXPERTS], F32, layer1)
                chip.gates_b16 = keep("gates1_b16", [3 * EXPERTS, TOK], BF16, layer1)
                chip.gates_f32 = keep("gates1_f32", [3 * EXPERTS, TOK], F32, layer1)
                chip.up1 = keep("up1", [P, 2, HT * (EXPERTS + 1), P], F16, layer1)
                chip.down1 = keep("down1", [P, 2, HT * (EXPERTS + 1), P], F16, layer1)
                load_mlp1(nc, chip, dram)
                layer_norm(nc, chip, "ln4", 1, SB, CB, bias_of=1, router=chip.w_router1[:], logits=chip.logits)
                gates(nc, chip, 1)
                experts(nc, chip, 1, chip.up1, chip.down1, "bfc_s", chip.bproj_rows, HT)
        store(nc, chip, out)


INPUTS = ['L0_attn_x', 'L0_attn_w_qkv', 'L0_attn_b_qkv', 'L0_attn_w_out', 'L0_attn_b_out', 'L0_ffn_gate_weight', 'L0_ffn_w1',
          'L0_ffn_b1', 'L0_ffn_w2', 'L0_ffn_b2', 'L0_c', 'L0_wmod', 'L1_attn_Wq', 'L1_attn_bq', 'L1_attn_Wk', 'L1_attn_bk',
          'L1_attn_Wv', 'L1_attn_bv', 'L1_ffn_Wfc_s', 'L1_ffn_bfc_s', 'L1_ffn_Wproj_s', 'L1_ffn_bproj_s', 'L1_ffn_Wr',
          'L1_ffn_Wfc', 'L1_ffn_bfc', 'L1_ffn_Wproj', 'L1_ffn_bproj', 'L1_c', 'L1_wmod']


def kernel(**inputs):
    import concourse.bacc as bacc
    from concourse.bass_utils import run_bass_kernel_spmd

    nc = bacc.Bacc("TRN2", target_bir_lowering=False, num_devices=1)
    arrays, dram = {}, {}
    for name in INPUTS:
        arrays[name] = np.ascontiguousarray(inputs[name])
        dram[name] = nc.dram_tensor(name, arrays[name].shape, mybir.dt.from_np(arrays[name].dtype), kind="ExternalInput").ap()
    arrays["consts"] = constants()
    dram["consts"] = nc.dram_tensor("consts", arrays["consts"].shape, F32, kind="ExternalInput").ap()
    out = nc.dram_tensor("out", (BATCH, SEQ, CH), F32, kind="ExternalOutput").ap()
    program(nc, dram, out)
    result = run_bass_kernel_spmd(nc, [arrays], core_ids=[0])
    return result.results[0]["out"]
```

```python
from contextlib import ExitStack

import numpy as np

import concourse.bass as bass
from concourse import mybir

P = 128
BATCH = 4
SEQ = 1024
CH = 128
TOK = BATCH * SEQ
CHUNK = 512
NCHUNK = TOK // CHUNK
NTILE = TOK // P
HEADS0 = 16
DH0 = 64
PAIRS = HEADS0 // 2
EXPERTS = 8
HID = 512
HT = HID // P
KTH = BATCH * 128 * 6
HEADS1 = 16
DH1 = CH // HEADS1
QUADS = 4
EPS = 1e-5
WS = 16.0
GS = 16.0
SH = 1024.0

F32 = mybir.dt.float32
F16 = mybir.dt.float16
BF16 = mybir.dt.bfloat16
I32 = mybir.dt.int32
ALU = mybir.AluOpType
ACT = mybir.ActivationFunctionType
AX_X = mybir.AxisListType.X
ds = bass.ds

CONST = {}
_at = 0
for _name, _n in (("ident", P), ("mask_qk", P), ("mask_kq", P), ("place_ctx", 32), ("place_sum", 32), ("prefer", EXPERTS),
                  ("key_pad", 1), ("head_rows", 4), ("rot_sign", 1), ("gate_sel", EXPERTS * P), ("q_sel", QUADS * 2 * P),
                  ("k_sel", QUADS * 2 * P), ("cos", SEQ), ("sin", SEQ)):
    CONST[_name] = (_at, _n)
    _at += _n
CONST_COLS = _at
TABLES_AT = CONST["gate_sel"][0]

ROW_AT = {}
_at = 0
for _name, _n in (("b_out", 1), ("bq", 1), ("bk", 1), ("bv", 1), ("bq_rot", 1), ("bk_rot", 1), ("c0", BATCH), ("c1", BATCH),
                  ("gate0", EXPERTS), ("bv0", PAIRS), ("b1", EXPERTS * HT), ("bfc_s", HT), ("bfc", EXPERTS * HT),
                  ("bproj_s", 1)):
    ROW_AT[_name] = (_at, _n)
    _at += _n
ROWS = _at

SA, CA, GA, SB, CB, GB = range(6)


def constants():
    c = np.zeros((P, CONST_COLS), np.float32)

    def put(name, a):
        at, n = CONST[name]
        c[:a.shape[0], at:at + n] = a.reshape(a.shape[0], n)

    r = np.arange(P)
    put("ident", np.eye(P, dtype=np.float32))
    far = -1e9 * np.sqrt(DH0) * WS * WS
    put("mask_qk", np.where(r[None, :] > r[:, None], far, 0.0))
    put("mask_kq", np.where(r[:, None] > r[None, :], far, 0.0))
    ctx, tot, pad = np.zeros((P, 32)), np.zeros((P, 32)), np.zeros((P, 1))
    q_sel, k_sel = np.zeros((P, QUADS, 2, P)), np.zeros((P, QUADS, 2, P))
    for j in range(4):
        pad[32 * j + 3 * DH1] = SH
        for d in range(DH1):
            ctx[32 * j + d, DH1 * j + d] = 1
            tot[32 * j + DH1, DH1 * j + d] = 1
            for g in range(QUADS):
                ch = (4 * g + j) * DH1 + d
                for copy, (q_low, k_low) in enumerate(((0, 0), (1, 0), (0, 1))):
                    q_sel[ch, g, q_low, 32 * j + DH1 * copy + d] = 1
                    k_sel[ch, g, k_low, 32 * j + DH1 * copy + d] = 1
    put("place_ctx", ctx)
    put("place_sum", tot)
    put("key_pad", pad)
    put("head_rows", r[:, None] // 32 == np.arange(4)[None, :])
    put("q_sel", q_sel)
    put("k_sel", k_sel)
    put("prefer", np.tile(np.arange(EXPERTS, 0, -1), (P, 1)))
    put("rot_sign", np.where(r % 2 == 0, -1.0, 1.0)[:, None])
    sel = np.zeros((3 * EXPERTS, EXPERTS, P))
    for e in range(EXPERTS):
        sel[e::EXPERTS, e, :] = GS
    put("gate_sel", sel)
    pos = np.arange(SEQ, dtype=np.float32)
    inv = np.power(np.float32(10000.0), np.float32(-2.0) * np.arange(DH1 // 2, dtype=np.float32) / np.float32(DH1)).astype(np.float32)
    ang = (pos[:, None] * inv[None, :]).astype(np.float32)
    put("cos", np.tile(np.repeat(np.cos(ang), 2, axis=-1).T, (HEADS1, 1)))
    put("sin", np.tile(np.repeat(np.sin(ang), 2, axis=-1).T, (HEADS1, 1)))
    return c


class Chip:
    pass


class Link:

    def __init__(self, eng, sem):
        self.eng, self.sem, self.n = eng, sem, 0

    def __call__(self, ins):
        self.n += 1
        ins.then_inc(self.sem, 1)
        self.eng.wait_ge(self.sem, self.n)


def apart(eng, chip):
    eng.sem_inc(chip.apart, 1)


def const(chip, name, rows=P):
    at, n = CONST[name]
    return chip.consts[0:rows, at:at + n]


def col(chip, name, k=0):
    return chip.cols[:, ROW_AT[name][0] + k:ROW_AT[name][0] + k + 1]


def setup(nc, chip, dram):
    with ExitStack() as ctx:
        def sb(name, shape, dt):
            return ctx.enter_context(nc.sbuf_tensor(name, shape, dt))

        def sem(name):
            return ctx.enter_context(nc.semaphore(name))

        bank = [ctx.enter_context(nc.psum_tensor(f"setup_bank{i}", [P, 512], F32)) for i in range(8)]
        x_tok = sb("x_tok", [P, NTILE, CH], F32)
        rows = sb("rows", [P, P], F32)
        dup_rows = sb("dup_rows", [48, P], F32)
        wmod = sb("wmod", [P, 2, 6 * CH], F32)
        w1_raw = sb("w1_attn", [P, 5, CH], F32)
        silu = sb("silu", [P, 3, 2 * BATCH], F32)
        mag = sb("mag", [P, 2, 2, 2, BATCH], F32)

        loaded_const, loaded_rows = sem("loaded_const"), sem("loaded_rows")
        loaded_x = [sem(f"loaded_x{n}") for n in range(NCHUNK)]
        loaded_wmod, loaded_qkv, loaded_tables = sem("loaded_wmod"), sem("loaded_qkv"), sem("loaded_tables")
        loaded_small = sem("loaded_small")
        rows_clear, turned_rows, cols_ready = sem("rows_clear"), sem("turned_rows"), sem("cols_ready")
        silu_exp, silu_ready = sem("silu_exp"), sem("silu_ready")
        turned_x, x_by_act, x_by_dve = sem("turned_x"), sem("x_by_act"), sem("x_by_dve")
        mod_done, mod_taken = sem("mod_done"), sem("mod_taken")
        high_done = sem("high_done")
        dve_chain = sem("setup_dve_chain")
        N_ROW_LOADS = 16

        block = ctx.enter_context(nc.Block())

        @block.sync
        def _(sp):
            sp.wait_ge(rows_clear, 1)
            for h in range(2):
                sp.dma_start(dup_rows[:, h * DH0:(h + 1) * DH0], dram["L0_attn_b_qkv"].rearrange("t h e -> (t h) e")).then_inc(loaded_rows, 16)

            def row(name, src):
                at, n = ROW_AT[name]
                sp.dma_start(rows[at:at + n, :], src).then_inc(loaded_rows, 16)

            vec = "(a b) -> a b"
            row("b_out", dram["L0_attn_b_out"].rearrange(vec, b=CH))
            row("bq", dram["L1_attn_bq"].rearrange(vec, b=CH))
            row("bk", dram["L1_attn_bk"].rearrange(vec, b=CH))
            row("bv", dram["L1_attn_bv"].rearrange(vec, b=CH))
            row("c0", dram["L0_c"])
            row("c1", dram["L1_c"])
            row("gate0", dram["L0_ffn_gate_weight"])
            row("bv0", dram["L0_attn_b_qkv"][2].rearrange("(a b) e -> a (b e)", b=2))
            row("b1", dram["L0_ffn_b1"].rearrange("e (j p) -> (e j) p", p=P))
            row("bfc_s", dram["L1_ffn_bfc_s"].rearrange(vec, b=CH))
            row("bproj_s", dram["L1_ffn_bproj_s"].rearrange(vec, b=CH))
            row("bfc", dram["L1_ffn_bfc"].rearrange("e (j p) -> (e j) p", p=P))
            for name, src in (("bq_rot", "L1_attn_bq"), ("bk_rot", "L1_attn_bk")):
                at = ROW_AT[name][0]
                pairs = dram[src].rearrange("(a i two) -> a i two", a=1, two=2)
                out = rows[at:at + 1, :].rearrange("a (i two) -> a i two", two=2)
                sp.dma_start(out[:, :, 0:1], pairs[:, :, 1:2], allow_slow_non_contiguous=True).then_inc(loaded_rows, 16)
                sp.dma_start(out[:, :, 1:2], pairs[:, :, 0:1], allow_slow_non_contiguous=True).then_inc(loaded_rows, 16)
            sp.dma_start(wmod[:, 0, :], dram["L0_wmod"]).then_inc(loaded_wmod, 16)
            sp.dma_start(wmod[:, 1, :], dram["L1_wmod"]).then_inc(loaded_wmod, 16)
            sp.dma_start(chip.w_qkv_raw[:], dram["L0_attn_w_qkv"].rearrange("d t h e -> d (t h e)")).then_inc(loaded_qkv, 16)
            sp.dma_start(chip.w_out_raw[:], dram["L0_attn_w_out"].rearrange("(p s) e d -> (s e) p d", s=2)).then_inc(loaded_qkv, 16)
            sp.dma_start(chip.w_router1[:], dram["L1_ffn_Wr"]).then_inc(loaded_small, 16)
            for k, name in enumerate(("L1_attn_Wq", "L1_attn_Wk", "L1_attn_Wv")):
                sp.dma_start(chip.w1_attn_raw[:, k, :], dram[name]).then_inc(loaded_small, 16)
            for k in range(3):
                sp.dma_start(chip.b2_rows[EXPERTS * k:EXPERTS * (k + 1), :], dram["L0_ffn_b2"]).then_inc(loaded_small, 16)
                sp.dma_start(chip.bproj_rows[EXPERTS * k:EXPERTS * (k + 1), :], dram["L1_ffn_bproj"]).then_inc(loaded_small, 16)
            sp.dma_start(chip.w_raw[:, EXPERTS * HT:, :], dram["L0_ffn_w2"].rearrange("e d (j h) -> d e j h", h=P)).then_inc(chip.mlp0_loaded, 16)
            sp.wait_ge(loaded_small, 16 * 10)

        @block.scalar
        def _(act):
            act.dma_start(chip.consts[:, 0:TABLES_AT], dram["consts"][:, 0:TABLES_AT]).then_inc(loaded_const, 16)
            x_view = dram["L0_attn_x"].rearrange("b (t p) c -> p (b t) c", p=P)
            for n in range(NCHUNK):
                act.dma_start(x_tok[:, 4 * n:4 * n + 4, :], x_view[:, 4 * n:4 * n + 4, :]).then_inc(loaded_x[n], 16)
            act.dma_start(chip.consts[:, TABLES_AT:], dram["consts"][:, TABLES_AT:]).then_inc(loaded_tables, 16)
            act.dma_start(chip.w_raw[:, 0:EXPERTS * HT, :], dram["L0_ffn_w1"].rearrange("e (j p) d -> p (e j) d", p=P)).then_inc(chip.mlp0_loaded, 16)
            act.wait_ge(cols_ready, 1)
            c_cols = chip.cols[:, ROW_AT["c0"][0]:ROW_AT["c0"][0] + 2 * BATCH]
            nc.scalar.activation(silu[:, 0, :], c_cols, ACT.Exp, scale=-1.0).then_inc(silu_exp, 1)
            for n in range(1, NCHUNK, 2):
                act.wait_ge(turned_x, n + 1)
                nc.scalar.copy(chip.xT[:, n * CHUNK:(n + 1) * CHUNK], bank[n][:]).then_inc(x_by_act, 1)
            act.wait_ge(loaded_qkv, 32)
            qkv = chip.w_qkv_raw[:].rearrange("c (t h e) -> c t h e", t=3, h=HEADS0)
            for t in range(2):
                for twice in range(2):
                    nc.scalar.mul(chip.w_qk[:, 0, :, t, twice, :], qkv[:, t, :, :], WS).then_inc(high_done, 1)
            nc.scalar.mul(chip.w_v[:, 0, :], chip.w_qkv_raw[:, 2 * HEADS0 * DH0:], WS).then_inc(high_done, 1)
            nc.scalar.mul(chip.w_out[:, 0, :, :], chip.w_out_raw[:], WS).then_inc(high_done, 1)

        @block.tensor
        def _(pe):
            ident = const(chip, "ident")
            pe.wait_ge(loaded_const, 16)
            pe.wait_ge(loaded_rows, 16 * (2 + 16))
            pe.transpose(bank[7][:, 0:48], dup_rows[:], ident[0:48, 0:48]).then_inc(turned_rows, 1)
            pe.transpose(bank[7][:, 64:64 + ROWS], rows[0:ROWS, :], ident[0:ROWS, 0:ROWS]).then_inc(turned_rows, 1)
            for n in range(NCHUNK):
                pe.wait_ge(loaded_x[n], 16)
                if n == 7:
                    pe.wait_ge(cols_ready, 1)
                for i in range(4):
                    ins = pe.transpose(bank[n][:, i * P:(i + 1) * P], x_tok[:, 4 * n + i, :], ident)
                ins.then_inc(turned_x, 1)
            pe.wait_ge(silu_ready, 1)
            pe.wait_ge(loaded_wmod, 32)
            pe.wait_ge(x_by_dve, 1)
            for layer in range(2):
                for k in range(6):
                    ins = pe.matmul(bank[0][:, (layer * 6 + k) * BATCH:(layer * 6 + k + 1) * BATCH],
                                    wmod[:, layer, k * CH:(k + 1) * CH],
                                    silu[:, 2, layer * BATCH:(layer + 1) * BATCH], start=True, stop=True)
            ins.then_inc(mod_done, 1)

        @block.gpsimd
        def _(pool):
            nc.gpsimd.memset(rows[:], 0.0).then_inc(rows_clear, 1)
            nc.gpsimd.memset(chip.mean_ones[:], 1.0 / CH)
            nc.gpsimd.memset(chip.ones[:], 1.0)
            nc.gpsimd.memset(chip.sum_ones[:], WS)
            nc.gpsimd.memset(chip.eps[:], EPS)
            pool.wait_ge(loaded_const, 16)
            nc.gpsimd.tensor_copy(chip.ident16[:], const(chip, "ident"))
            nc.gpsimd.tensor_copy(chip.identb[:], const(chip, "ident"))
            nc.gpsimd.tensor_copy(chip.mask_qk[:], const(chip, "mask_qk"))
            nc.gpsimd.tensor_copy(chip.mask_kq[:], const(chip, "mask_kq"))
            pool.wait_ge(loaded_tables, 16)
            nc.gpsimd.tensor_copy(chip.gate_sel[:], const(chip, "gate_sel", 3 * EXPERTS))
            nc.gpsimd.tensor_copy(chip.q_sel[:], const(chip, "q_sel"))
            nc.gpsimd.tensor_copy(chip.k_sel[:], const(chip, "k_sel"))

        @block.vector
        def _(dve):
            link = Link(dve, dve_chain)
            dve.wait_ge(turned_rows, 2)
            link(nc.vector.tensor_copy(chip.cols[:, 0:ROWS], bank[7][:, 64:64 + ROWS]))
            nc.vector.tensor_scalar(chip.bqk[:], bank[7][:, 0:2 * HEADS0], WS, None, ALU.mult).then_inc(cols_ready, 1)
            dve.wait_ge(silu_exp, 1)
            link(nc.vector.tensor_scalar(silu[:, 1, :], silu[:, 0, :], 1.0, None, ALU.add))
            link(nc.vector.reciprocal(silu[:, 0, :], silu[:, 1, :]))
            c_cols = chip.cols[:, ROW_AT["c0"][0]:ROW_AT["c0"][0] + 2 * BATCH]
            nc.vector.tensor_tensor(silu[:, 2, :], silu[:, 0, :], c_cols, ALU.mult).then_inc(silu_ready, 1)
            for n in range(0, NCHUNK, 2):
                dve.wait_ge(turned_x, n + 1)
                nc.vector.tensor_copy(chip.xT[:, n * CHUNK:(n + 1) * CHUNK], bank[n][:]).then_inc(x_by_dve, 1)
            dve.wait_ge(mod_done, 1)
            mod = chip.mod
            link(nc.vector.tensor_copy(mod[:].rearrange("p l k b -> p (l k b)"), bank[0][:, 0:12 * BATCH]))
            nc.vector.memset(silu[:, 1, 0:1], 0.0).then_inc(mod_taken, 1)
            for k in (CA, CB):
                link(nc.vector.tensor_scalar(mod[:, :, k, :], mod[:, :, k, :], 1.0, None, ALU.add))
            for n, k in enumerate((GA, GB)):
                g = mod[:, :, k, :]
                size, sign = mag[:, 0, n, :, :], mag[:, 1, n, :, :]
                link(nc.vector.scalar_tensor_tensor(size, g, -1.0, g, ALU.mult, ALU.max))
                link(nc.vector.tensor_scalar(size, size, 0.25, None, ALU.max))
                link(nc.vector.tensor_scalar(sign, g, 0.0, 2.0, ALU.is_ge, ALU.mult))
                link(nc.vector.scalar_tensor_tensor(g, sign, -1.0, size, ALU.add, ALU.mult))
            link(nc.vector.tensor_scalar(chip.g_bias[:, 0, :], mod[:, 0, GA, :], col(chip, "b_out"), None, ALU.mult))
            link(nc.vector.tensor_scalar(chip.g_bias[:, 1, :], mod[:, 1, GA, :], col(chip, "bv"), None, ALU.mult))
            link(nc.vector.tensor_scalar(chip.g_bias[:, 2, :], mod[:, 1, GB, :], col(chip, "bproj_s"), None, ALU.mult))
            link(nc.vector.tensor_scalar(chip.ga_scaled[:], mod[:, 0, GA, :], 1.0 / WS, None, ALU.mult))
            link(nc.vector.tensor_scalar(chip.gb_scaled[:], mod[:, :, GB, :], 1.0 / (WS * GS), None, ALU.mult))
            at = ROW_AT["bq"][0]
            link(nc.vector.tensor_scalar(chip.bqk1[:, 0:2], chip.cols[:, at:at + 2], WS, None, ALU.mult))
            at = ROW_AT["bq_rot"][0]
            link(nc.vector.tensor_scalar(chip.bqk1[:, 2:4], chip.cols[:, at:at + 2], const(chip, "rot_sign"), WS, ALU.mult, ALU.mult))
            dve.wait_ge(loaded_qkv, 32)
            qkv = chip.w_qkv_raw[:].rearrange("c (t h e) -> c t h e", t=3, h=HEADS0)
            for t in range(2):
                for twice in range(2):
                    dve.wait_ge(high_done, 2 * t + twice + 1)
                    nc.vector.scalar_tensor_tensor(chip.w_qk[:, 1, :, t, twice, :], qkv[:, t, :, :], WS,
                                                   chip.w_qk[:, 0, :, t, twice, :], ALU.mult, ALU.subtract)
            dve.wait_ge(high_done, 6)
            nc.vector.scalar_tensor_tensor(chip.w_v[:, 1, :], chip.w_qkv_raw[:, 2 * HEADS0 * DH0:], WS, chip.w_v[:, 0, :],
                                           ALU.mult, ALU.subtract)
            nc.vector.scalar_tensor_tensor(chip.w_out[:, 1, :, :], chip.w_out_raw[:], WS, chip.w_out[:, 0, :, :],
                                           ALU.mult, ALU.subtract)
            dve.wait_ge(loaded_small, 16 * 10)
            link(nc.vector.tensor_copy(w1_raw[:, 0:3, :], chip.w1_attn_raw[:]))
            for x in range(2):
                src = w1_raw[:, x, :].rearrange("c (i two) -> c i two", two=2)
                dst = w1_raw[:, 3 + x, :].rearrange("c (i two) -> c i two", two=2)
                link(nc.vector.tensor_scalar(dst[:, :, 0:1], src[:, :, 1:2], -1.0, None, ALU.mult))
                link(nc.vector.tensor_copy(dst[:, :, 1:2], src[:, :, 0:1]))
            link(nc.vector.tensor_scalar(chip.w1_attn[:, 0, :, :], w1_raw[:], WS, None, ALU.mult))
            nc.vector.scalar_tensor_tensor(chip.w1_attn[:, 1, :, :], w1_raw[:], WS, chip.w1_attn[:, 0, :, :], ALU.mult, ALU.subtract)
            nc.vector.tensor_scalar(chip.b2_rows[:], chip.b2_rows[:], WS * GS, None, ALU.mult)
            nc.vector.tensor_scalar(chip.bproj_rows[:], chip.bproj_rows[:], WS * GS, None, ALU.mult)


def layer_norm(nc, chip, name, layer, shift, scale, bias_of=None, router=None, logits=None):
    W = NCHUNK
    with ExitStack() as ctx:
        def sb(what, shape, dt):
            return ctx.enter_context(nc.sbuf_tensor(f"{name}_{what}", shape, dt))

        def sem(what):
            return ctx.enter_context(nc.semaphore(f"{name}_{what}"))

        mean = [ctx.enter_context(nc.psum_tensor(f"{name}_mean{u}", [P, CHUNK], F32)) for u in range(W)]
        var = mean
        logit = [mean[u][:, 0:4 * EXPERTS].rearrange("p (i e) -> p i e", i=4) for u in range(W)]
        centred, square = ([sb(f"{what}{u}", [P, CHUNK], F32) for u in range(W)] for what in ("centred", "square"))
        turned = inverse = h32 = square
        deviation, compact = ([sb(f"{what}{u}", [P, CHUNK // 32], F32) for u in range(W)] for what in ("deviation", "compact"))
        x_whole, mean_ready, centred_ready, square_ready, var_ready, var_turned, deviation_ready = (
            sem(w) for w in ("x_whole", "mean_ready", "centred_ready", "square_ready", "var_ready", "var_turned", "deviation_ready"))
        compact_ready, inverse_ready, normed_ready, h_ready, high_ready, logit_ready = (
            sem(w) for w in ("compact_ready", "inverse_ready", "normed_ready", "h_ready", "high_ready", "logit_ready"))
        block = ctx.enter_context(nc.Block())

        def chunk(a, u):
            return a[:, u * CHUNK:(u + 1) * CHUNK]

        @block.tensor
        def _(pe):
            for u in range(W):
                if bias_of is not None:
                    pe.wait_ge(x_whole, u + 1)
                pe.matmul(mean[u][:], chip.mean_ones[:], chunk(chip.xT, u), start=True, stop=True).then_inc(mean_ready, 1)
            for u in range(W):
                pe.wait_ge(square_ready, u + 1)
                pe.matmul(var[u][:], chip.mean_ones[:], square[u][:], start=True, stop=True).then_inc(var_ready, 1)
            if router is not None:
                for u in range(W):
                    pe.wait_ge(h_ready, u + 1)
                    for i in range(4):
                        ins = pe.matmul(logit[u][:, i, :], h32[u][:, i * P:(i + 1) * P], router, start=True, stop=True)
                    ins.then_inc(logit_ready, 1)

        @block.scalar
        def _(act):
            def high(u):
                act.wait_ge(h_ready, u + 1)
                nc.scalar.copy(chunk(chip.h_high, u), h32[u][:]).then_inc(high_ready, 1)

            for u in range(W):
                act.wait_ge(centred_ready, u + 1)
                nc.scalar.square(square[u][:], centred[u][:]).then_inc(square_ready, 1)
            for u in range(W):
                act.wait_ge(var_turned, u + 1)
                nc.scalar.activation(deviation[u][:], turned[u][:].rearrange("p (a b) -> p a b", b=32)[:, :, 0], ACT.Sqrt,
                                     bias=chip.eps[:, 0:1]).then_inc(deviation_ready, 1)
            for u in range(W):
                act.wait_ge(normed_ready, u + 1)
                batch = u // 2
                nc.scalar.activation(h32[u][:], centred[u][:], ACT.Identity, scale=chip.mod[:, layer, scale, batch:batch + 1],
                                     bias=chip.mod[:, layer, shift, batch:batch + 1]).then_inc(h_ready, 1)
                if u >= 1:
                    high(u - 1)
            high(W - 1)

        @block.gpsimd
        def _(pool):
            for u in range(0, W, 2):
                pool.wait_ge(high_ready, u + 1)
                nc.gpsimd.tensor_tensor(chunk(chip.h_low, u), h32[u][:], chunk(chip.h_high, u), ALU.subtract)

        @block.vector
        def _(dve):
            for u in range(W):
                if bias_of is not None:
                    nc.vector.tensor_scalar(chunk(chip.xT, u), chunk(chip.xT, u),
                                            chip.g_bias[:, bias_of, u // 2:u // 2 + 1], None, ALU.add).then_inc(x_whole, 1)
            for u in range(W):
                dve.wait_ge(mean_ready, u + 1)
                nc.vector.tensor_tensor(centred[u][:], chunk(chip.xT, u), mean[u][:], ALU.subtract).then_inc(centred_ready, 1)
            for u in range(W):
                dve.wait_ge(var_ready, u + 1)
                nc.vector.transpose(turned[u][:], var[u][:]).then_inc(var_turned, 1)
            for u in range(W):
                dve.wait_ge(deviation_ready, u + 1)
                nc.vector.reciprocal(compact[u][:], deviation[u][:]).then_inc(compact_ready, 1)
            for u in range(W):
                dve.wait_ge(compact_ready, u + 1)
                nc.vector.transpose(inverse[u][:], compact[u][:].unsqueeze(2).broadcast_to([P, CHUNK // 32, 32])).then_inc(inverse_ready, 1)
            for u in range(W):
                dve.wait_ge(inverse_ready, u + 1)
                nc.vector.tensor_tensor(centred[u][:], centred[u][:], inverse[u][:], ALU.mult).then_inc(normed_ready, 1)
            if router is not None:
                for u in range(W):
                    dve.wait_ge(logit_ready, u + 1)
                    nc.vector.tensor_copy(logits[:, 4 * u:4 * u + 4, :], logit[u])
            for u in range(1, W, 2):
                dve.wait_ge(high_ready, u + 1)
                nc.vector.tensor_tensor(chunk(chip.h_low, u), h32[u][:], chunk(chip.h_high, u), ALU.subtract)



UNITS = [(j, c) for j in range(SEQ // P) for c in range(2) if P * j < CHUNK * (c + 1)]
NU = len(UNITS)


def unit(u):
    j, c = UNITS[u]
    first = max(P * j, CHUNK * c)
    return j, c, first, CHUNK * (c + 1) - first, first == P * j


STEP_JOBS = [
    [("sum", 0), ("sum", 1), ("q", 0, 0), ("q", 0, 1), ("k", 0, 1), ("k", 0, 0)],
    [("q", 1, 0)],
    [("q", 1, 1)],
    [("k", 1, 1), ("k", 1, 0), ("out", 0), ("out", 1), ("v", 0), ("max", 0, 0, 0)],
    [("max", 0, 1, 0), ("max", 0, 2, 0), ("max", 0, 3, 0), ("max", 0, 4, 0), ("max", 0, 4, 1)],
    [("max", 0, 5, 0), ("max", 0, 7, 0), ("max", 0, 5, 1), ("max", 0, 6, 0)],
    [("max", 0, 6, 1), ("max", 0, 7, 1)],
    [("max", 1, 0, 0), ("max", 1, 2, 0), ("max", 1, 3, 0), ("max", 1, 1, 0)],
    [("shift", 0, 1), ("max", 1, 4, 0), ("max", 1, 4, 1), ("max", 1, 5, 0)],
    [("max", 1, 5, 1), ("max", 1, 7, 0), ("max", 1, 6, 0), ("max", 1, 6, 1), ("max", 1, 7, 1)],
    [("shift", 0, 0)],
    [("shift", 1, 0), ("shift", 1, 1), ("v", 1)],
]
CLOSING = ("sum", "out")


def slot_jobs(close, prepare):
    steps = [[x for x in step if (close if x[0] in CLOSING else prepare)] for step in STEP_JOBS]
    number = {}
    for step in steps:
        for x in step:
            number[x] = len(number)
    return steps, number


ALL_JOBS = len(slot_jobs(True, True)[1])
PREPARE_JOBS = len(slot_jobs(False, True)[1])
HIGHS = 8
BANKS = 4


class Job:

    def __init__(self, first, k, t, per_turn):
        n = first + k
        self.bank = n % BANKS
        self.before = n // BANKS + per_turn // BANKS * t
        self.done = n + 1 + per_turn * t


def attention0(nc, chip):
    SCALE = 1.0 / (float(np.sqrt(DH0)) * WS * WS)
    PER_TURN = 2 * ALL_JOBS
    assert PER_TURN % BANKS == 0
    with ExitStack() as ctx:
        def sb(name, shape, dt):
            return ctx.enter_context(nc.sbuf_tensor(name, shape, dt))

        def sem(name):
            return ctx.enter_context(nc.semaphore(name))

        def two(name, shape, dt):
            return [[sb(f"{name}{v}{s}", shape, dt) for s in range(2)] for v in range(2)]

        q_twice = two("q_twice", [P, SEQ], F16)
        q_low = two("q_low", [96, SEQ], F16)
        k_both = two("k_both", [P, SEQ], F16)
        k_high = two("k_high", [96, SEQ], F16)
        v = two("v", [P, SEQ // P, DH0], F32)
        total = two("total", [P, SEQ], F32)
        probs = two("probs", [P, CHUNK], F32)
        maxima = [sb(f"maxima{s}", [P, 2, 8], F32) for s in range(2)]
        minus_max = [sb(f"minus_max{s}", [P, 8, 32], F16) for s in range(2)]
        turned = [sb(f"sums_turned{c}", [P, CHUNK], F32) for c in range(2)]
        compact = [sb(f"compact{c}", [P, CHUNK // 32], F32) for c in range(2)]
        inverse = [sb(f"inverse{c}", [P, CHUNK], F32) for c in range(2)]
        normed = [sb(f"normed{c}", [P, CHUNK], F32) for c in range(2)]
        o_high = [sb(f"o_high{c}", [P, CHUNK], F16) for c in range(2)]
        o_low = [sb(f"o_low{c}", [P, CHUNK], F16) for c in range(2)]
        scores = [ctx.enter_context(nc.psum_tensor(f"scores{s}", [P, CHUNK], F32)) for s in range(2)]
        spare = [ctx.enter_context(nc.psum_tensor(f"spare{k}", [P, CHUNK], F32)) for k in range(BANKS)]
        o_psum = [ctx.enter_context(nc.psum_tensor(f"o{c}", [P, CHUNK], F32)) for c in range(2)]

        pads_clear, buffers_clear = sem("pads_clear"), sem("buffers_clear")
        job_ready = sem("job_ready")
        bank_free = [sem(f"bank_free{k}") for k in range(BANKS)]
        high_ready = sem("high_ready")
        split_ready = sem("split_ready")
        max_ready = sem("max_ready")
        minus_ready = sem("minus_ready")
        shift_ready = sem("shift_ready")
        score_ready = [sem(f"score_ready{s}") for s in range(2)]
        probs_ready = [sem(f"probs_ready{s}") for s in range(2)]
        pv_done = [sem(f"pv_done{s}") for s in range(2)]
        added = [sem(f"added{s}") for s in range(2)]
        compact_ready = sem("compact_ready")
        inverse_ready, normed_ready = sem("inverse_ready"), sem("normed_ready")
        o_high_ready, o_low_ready = sem("o_high_ready"), sem("o_low_ready")
        block = ctx.enter_context(nc.Block())
        ADDS = NU - 2

        def where(i):
            return i // PAIRS, i % PAIRS

        def weights(half, t, s, pair):
            return chip.w_qk[:, half, ds(2 * pair + s, 1), t, :, :].rearrange("c h w e -> c (h w e)")

        def bias(t, s, pair):
            return chip.bqk[:, ds(t * HEADS0 + 2 * pair + s, 1)]

        def tokens(a, batch, first, n):
            return a[:, ds(batch * SEQ + first, n)]

        def whole(run, slot):
            slot(-1, 1, 0, 0, False, True, False)
            slot(0, 0, 0, PREPARE_JOBS, False, True, True)
            first = 2 * PREPARE_JOBS
            with run.Fori(0, BATCH * PAIRS // 2 - 1) as t:
                slot(2 * t + 1, 1, t, first, True, True, True)
                slot(2 * t + 2, 0, t, first + ALL_JOBS, True, True, True)
            done = first + PER_TURN * (BATCH * PAIRS // 2 - 1)
            closing = ALL_JOBS - PREPARE_JOBS
            slot(BATCH * PAIRS - 1, 1, 0, done, True, False, True)
            slot(BATCH * PAIRS, 0, 0, done + closing, True, False, False)

        @block.tensor
        def _(pe):
            def product(out, high, low, x_high, x_low):
                pe.matmul(out, high, x_high, start=True, stop=False)
                pe.matmul(out, low, x_high, start=False, stop=False)
                return pe.matmul(out, high, x_low, start=False, stop=True)

            def run_job(x, job, i, parity):
                out = spare[job.bank]
                nxt, n_par = i + 1, 1 - parity
                pe.wait_ge(bank_free[job.bank], job.before)
                if x[0] in ("q", "k"):
                    batch, pair = where(nxt)
                    _, s, c = x
                    t = 0 if x[0] == "q" else 1
                    ins = product(out[:], weights(0, t, s, pair), weights(1, t, s, pair),
                                  tokens(chip.h_high, batch, c * CHUNK, CHUNK), tokens(chip.h_low, batch, c * CHUNK, CHUNK))
                elif x[0] == "v":
                    batch, pair = where(nxt)
                    _, s = x
                    wv = [chip.w_v[:, half, ds((2 * pair + s) * DH0, DH0)] for half in range(2)]
                    for k in range(SEQ // P):
                        h_high, h_low = (tokens(h, batch, k * P, P) for h in (chip.h_high, chip.h_low))
                        o = out[:, k * DH0:(k + 1) * DH0]
                        pe.matmul(o, h_high, wv[0], start=True, stop=False)
                        pe.matmul(o, h_high, wv[1], start=False, stop=False)
                        ins = pe.matmul(o, h_low, wv[0], start=False, stop=True)
                elif x[0] == "max":
                    _, s, k, c = x
                    if (k, c) == (0, 0):
                        pe.wait_ge(split_ready, 4 * nxt + 2 * s + 2)
                    n = min(P * (k + 1) - CHUNK * c, CHUNK)
                    diagonal = c == k // 4
                    ins = pe.matmul(out[:, 0:n], q_twice[n_par][s][:, k * P:(k + 1) * P], k_both[n_par][s][:, c * CHUNK:c * CHUNK + n],
                                    start=True, stop=not diagonal)
                    if diagonal:
                        ins = pe.matmul(out[:, n - P:n], chip.identb[:], chip.mask_qk[:], start=False, stop=True)
                elif x[0] == "shift":
                    _, s, c = x
                    pe.wait_ge(buffers_clear, 1)
                    pe.wait_ge(minus_ready, 2 * nxt + s + 1)
                    for k in range(4):
                        ins = pe.matmul(out[64:96, k * P:(k + 1) * P], minus_max[s][:, 4 * c + k, :], chip.ident16[:],
                                        start=True, stop=True)
                elif x[0] == "sum":
                    _, c = x
                    for s in range(2):
                        pe.wait_ge(added[s], ADDS * i)
                        ins = pe.matmul(out[64 * s:64 * s + 64, :], chip.sum_ones[:], total[n_par][s][:, c * CHUNK:(c + 1) * CHUNK],
                                        start=True, stop=True)
                else:
                    _, c = x
                    _, pair = where(i - 1)
                    pe.wait_ge(o_low_ready, 2 * (i - 1) + c + 1)
                    wo = [chip.w_out[:, half, ds(pair, 1), :].rearrange("p a c -> p (a c)") for half in range(2)]
                    ins = product(out[:], wo[0], wo[1], o_high[c][:], o_low[c][:])
                ins.then_inc(job_ready, 1)

            def slot(i, parity, t, first, close, prepare, attend):
                steps, number = slot_jobs(close, prepare)
                if attend:
                    pe.wait_ge(shift_ready, i + 1)

                def score(u):
                    j, _, q0, n, diagonal = unit(u)
                    for s in range(2):
                        pe.wait_ge(probs_ready[s], NU * i + u)
                        pe.matmul(scores[s][:, 0:n], k_both[parity][s][:, j * P:(j + 1) * P], q_twice[parity][s][:, q0:q0 + n],
                                  start=True, stop=False)
                        ins = pe.matmul(scores[s][:, 0:n], k_high[parity][s][:, j * P:(j + 1) * P], q_low[parity][s][:, q0:q0 + n],
                                        start=False, stop=not diagonal)
                        if diagonal:
                            ins = pe.matmul(scores[s][:, 0:P], chip.identb[:], chip.mask_kq[:], start=False, stop=True)
                        ins.then_inc(score_ready[s], 1)

                if attend:
                    score(0)
                for u in range(NU):
                    j, c, q0, n, _ = unit(u)
                    for x in steps[u]:
                        run_job(x, Job(first, number[x], t, PER_TURN), i, parity)
                    if attend:
                        if u + 1 < NU:
                            score(u + 1)
                        if close and u < 2:
                            pe.wait_ge(normed_ready, 2 * (i - 1) + u + 1)
                        for s in range(2):
                            pe.wait_ge(probs_ready[s], NU * i + u + 1)
                            p = total[parity][s][:, c * CHUNK:(c + 1) * CHUNK] if u < 2 else probs[u % 2][s][:, 0:n]
                            pe.matmul(o_psum[c][64 * s:64 * s + 64, q0 - c * CHUNK:q0 - c * CHUNK + n], v[parity][s][:, j, :], p,
                                      start=(j == 0), stop=(j == 4 * c + 3)).then_inc(pv_done[s], 1)

            whole(pe, slot)

        @block.scalar
        def _(act):
            def run_job(x, job, i, parity):
                nxt, n_par = i + 1, 1 - parity
                src = spare[job.bank]
                if x[0] in ("q", "k"):
                    _, pair = where(nxt)
                    _, s, c = x
                    t = 0 if x[0] == "q" else 1
                    out = (q_twice if t == 0 else k_both)[n_par][s]
                    act.wait_ge(job_ready, job.done)
                    apart(act, chip)
                    nc.scalar.activation(out[:, c * CHUNK:(c + 1) * CHUNK], src[:], ACT.Identity, bias=bias(t, s, pair))\
                        .then_inc(high_ready, 1)
                elif x[0] == "v":
                    act.wait_ge(job_ready, job.done)
                    nc.scalar.copy(v[n_par][x[1]][:], src[:].rearrange("p (k e) -> p k e", e=DH0)).then_inc(bank_free[job.bank], 1)
                elif x[0] == "shift":
                    _, s, c = x
                    act.wait_ge(job_ready, job.done)
                    nc.scalar.copy(q_low[n_par][s][64:96, c * CHUNK:(c + 1) * CHUNK], src[64:96, :]).then_inc(bank_free[job.bank], 1)
                    if (s, c) == (1, 1):
                        act.wait_ge(bank_free[job.bank], job.before + 1)
                        act.sem_inc(shift_ready, 1)

            def slot(i, parity, t, first, close, prepare, attend):
                steps, number = slot_jobs(close, prepare)
                for u in range(NU):
                    _, c, _, n, _ = unit(u)
                    for s in range(2):
                        if not attend:
                            break
                        if u in (2, 3):
                            act.wait_ge(added[s], ADDS * i)
                        if u >= 4:
                            act.wait_ge(pv_done[s], NU * i + u - 1)
                            act.wait_ge(added[s], ADDS * i + u - 3)
                        act.wait_ge(score_ready[s], NU * i + u + 1)
                        out = total[parity][s][:, c * CHUNK:(c + 1) * CHUNK] if u < 2 else probs[u % 2][s][:, 0:n]
                        nc.scalar.activation(out, scores[s][:, 0:n], ACT.Exp, scale=SCALE).then_inc(probs_ready[s], 1)
                    for x in steps[u]:
                        run_job(x, Job(first, number[x], t, PER_TURN), i, parity)
                    if close and u in (1, 2):
                        c = u - 1
                        _, pair = where(i - 1)
                        act.wait_ge(normed_ready, 2 * (i - 1) + c + 1)
                        apart(act, chip)
                        nc.scalar.activation(o_high[c][:], normed[c][:], ACT.Identity, bias=chip.bv0[:, ds(pair, 1)])\
                            .then_inc(o_high_ready, 1)

            whole(act, slot)

        @block.gpsimd
        def _(pool):
            for par in range(2):
                for s in range(2):
                    nc.gpsimd.memset(q_low[par][s][64:96, :], 0.0)
                    nc.gpsimd.memset(k_high[par][s][64:96, :], 0.0).then_inc(pads_clear, 1)
            pool.wait_ge(pads_clear, 4)
            for par in range(2):
                for s in range(2):
                    nc.gpsimd.memset(k_high[par][s][64:65, :], SH).then_inc(pads_clear, 1)
            pool.wait_ge(pads_clear, 8)
            for s in range(2):
                ins = nc.gpsimd.memset(minus_max[s][:], 0.0)
            ins.then_inc(buffers_clear, 1)

            def slot(i, parity, t, first, close, prepare, attend):
                if not attend:
                    return
                for u in range(2, NU):
                    _, _, q0, n, _ = unit(u)
                    for s in range(2):
                        if u == 2:
                            pool.wait_ge(pv_done[s], NU * i + 2)
                        pool.wait_ge(added[s], ADDS * i + u - 2)
                        pool.wait_ge(probs_ready[s], NU * i + u + 1)
                        acc = total[parity][s][:, q0:q0 + n]
                        nc.gpsimd.tensor_tensor(acc, acc, probs[u % 2][s][:, 0:n], ALU.add).then_inc(added[s], 1)

            whole(pool, slot)

        @block.vector
        def _(dve):
            def run_job(x, job, i, parity, number):
                nxt, n_par = i + 1, 1 - parity
                src = spare[job.bank]
                if x[0] in ("q", "k"):
                    _, pair = where(nxt)
                    _, s, c = x
                    at = slice(c * CHUNK, (c + 1) * CHUNK)
                    t = 0 if x[0] == "q" else 1
                    k = [y for y in number if y[0] in ("q", "k")].index(x)
                    dve.wait_ge(high_ready, HIGHS * nxt + k + 1)
                    if t == 0:
                        nc.vector.scalar_tensor_tensor(q_low[n_par][s][0:64, at], src[0:64, :], chip.bqk[0:64, ds(2 * pair + s, 1)],
                                                       q_twice[n_par][s][0:64, at], ALU.add, ALU.subtract)\
                            .then_inc(bank_free[job.bank], 1)
                    else:
                        low = k_both[n_par][s][64:128, at]
                        nc.vector.scalar_tensor_tensor(low, src[64:128, :], chip.bqk[64:128, ds(HEADS0 + 2 * pair + s, 1)], low,
                                                       ALU.add, ALU.subtract).then_inc(bank_free[job.bank], 1)
                        nc.vector.tensor_copy(k_high[n_par][s][0:64, at], k_both[n_par][s][0:64, at]).then_inc(split_ready, 1)
                elif x[0] == "max":
                    _, s, k, c = x
                    n = min(P * (k + 1) - CHUNK * c, CHUNK)
                    dve.wait_ge(job_ready, job.done)
                    nc.vector.tensor_reduce(maxima[s][:, c, k:k + 1], src[:, 0:n], AX_X, ALU.max).then_inc(bank_free[job.bank], 1)
                    if (k, c) == (7, 1):
                        dve.wait_ge(bank_free[job.bank], job.before + 1)
                        nc.vector.tensor_tensor(maxima[s][:, 0, 4:8], maxima[s][:, 0, 4:8], maxima[s][:, 1, 4:8], ALU.max)\
                            .then_inc(max_ready, 1)
                        dve.wait_ge(max_ready, 2 * nxt + s + 1)
                        dve.wait_ge(buffers_clear, 1)
                        nc.vector.tensor_scalar(minus_max[s][:, :, 0:1], maxima[s][:, 0, :].unsqueeze(2), -1.0 / SH, None, ALU.mult)\
                            .then_inc(minus_ready, 1)
                elif x[0] == "sum":
                    _, c = x
                    dve.wait_ge(job_ready, job.done)
                    nc.vector.transpose(turned[c][:], src[:]).then_inc(bank_free[job.bank], 1)
                    if c == 0:
                        return
                    for k in range(2):
                        dve.wait_ge(bank_free[job.bank], job.before + 1)
                        nc.vector.reciprocal(compact[k][:], turned[k][:].rearrange("p (a b) -> p a b", b=32)[:, :, 0])\
                            .then_inc(compact_ready, 1)
                    for k in range(2):
                        dve.wait_ge(compact_ready, 2 * (i - 1) + k + 1)
                        nc.vector.transpose(inverse[k][:], compact[k][:].unsqueeze(2).broadcast_to([P, CHUNK // 32, 32]))\
                            .then_inc(inverse_ready, 1)
                    for k in range(2):
                        dve.wait_ge(inverse_ready, 2 * (i - 1) + k + 1)
                        nc.vector.tensor_tensor(normed[k][:], o_psum[k][:], inverse[k][:], ALU.mult).then_inc(normed_ready, 1)
                elif x[0] == "out":
                    _, c = x
                    batch, _ = where(i - 1)
                    dve.wait_ge(job_ready, job.done)
                    here = tokens(chip.xT, batch, c * CHUNK, CHUNK)
                    nc.vector.scalar_tensor_tensor(here, src[:], chip.ga_scaled[:, ds(batch, 1)], here, ALU.mult, ALU.add)\
                        .then_inc(bank_free[job.bank], 1)

            def slot(i, parity, t, first, close, prepare, attend):
                steps, number = slot_jobs(close, prepare)
                for u in range(NU):
                    for x in steps[u]:
                        run_job(x, Job(first, number[x], t, PER_TURN), i, parity, number)
                    if close and u in (1, 2):
                        c = u - 1
                        _, pair = where(i - 1)
                        dve.wait_ge(o_high_ready, 2 * (i - 1) + c + 1)
                        nc.vector.scalar_tensor_tensor(o_low[c][:], normed[c][:], chip.bv0[:, ds(pair, 1)], o_high[c][:],
                                                       ALU.add, ALU.subtract).then_inc(o_low_ready, 1)

            whole(dve, slot)


def gates(nc, chip, layer):
    with ExitStack() as ctx:
        def sb(what, shape, dt):
            return ctx.enter_context(nc.sbuf_tensor(f"gates{layer}_{what}", shape, dt))

        def sem(what):
            return ctx.enter_context(nc.semaphore(f"gates{layer}_{what}"))

        logits = chip.logits
        gate, rest = sb("gate", [P, NTILE, EXPERTS], F32), sb("rest", [P, NTILE, EXPERTS], F32)
        parts = sb("parts", [P, NTILE, 3, EXPERTS], BF16)
        turned = [ctx.enter_context(nc.psum_tensor(f"gates{layer}_turned{k}", [3 * EXPERTS, 8 * P], BF16)) for k in range(4)]
        chain, parts_ready, turned_ready = sem("chain"), sem("parts_ready"), sem("turned_ready")
        if layer == 0:
            TRIALS, ROUNDS = 3, 16
            w_high, w_low = (chip.w12T[:, half] for half in range(2))
            w_bank = ctx.enter_context(nc.psum_tensor("gates0_w_bank", [P, CHUNK], F32))
            w_scaled = sb("w_scaled", [P, CHUNK], F32)
            w_turned, w_high_ready, w_scaled_ready, w_low_ready = (sem(w) for w in ("w_turned", "w_high_ready", "w_scaled_ready", "w_low_ready"))
            below, count, passed = sb("below", [P, TRIALS, NTILE * EXPERTS], F32), sb("count", [P, TRIALS], F32), sb("passed", [P, TRIALS], I32)
            bits, trial, flip, bound = (sb(w, [P, TRIALS], I32) for w in ("bits", "trial", "flip", "bound"))
            key = sb("key", [P, 1], I32)
            number = ctx.enter_context(nc.psum_tensor("gates0_number", [P, TRIALS], F32))
            state_ready, trial_ready, flip_ready, bound_ready = (
                sem(w) for w in ("state_ready", "trial_ready", "flip_ready", "bound_ready"))
            counted, summed, passed_ready, key_ready = sem("counted"), sem("summed"), sem("passed_ready"), sem("key_ready")
        else:
            shifted, powers, ready = sb("shifted", [P, NTILE, EXPERTS], F32), sem("powers"), sem("ready")
            one, first, second = (sb(w, [P, NTILE, EXPERTS], F32) for w in ("one", "first", "second"))
            stat = sb("stat", [P, NTILE], F32)
            w_high_ready = sem("w_high_ready")
            weights = ((chip.up1, chip.mlp1_raw[0]), (chip.down1, chip.mlp1_raw[1]))
        block = ctx.enter_context(nc.Block())

        @block.vector
        def _(dve):
            link = Link(dve, chain)
            if layer == 0:
                flat = logits[:].rearrange("p t e -> p (t e)")
                nc.vector.memset(key[:], 0)
                for j, top in enumerate((1 << 30, -(1 << 31), -(1 << 30))):
                    ins = nc.vector.memset(bits[:, j:j + 1], top)
                ins.then_inc(state_ready, 1)
                with dve.Fori(0, ROUNDS) as t:
                    dve.wait_ge(state_ready, t + 1)
                    nc.vector.tensor_tensor(trial[:], key[:].broadcast_to([P, TRIALS]), bits[:], ALU.bitwise_or).then_inc(trial_ready, 1)
                    dve.wait_ge(trial_ready, t + 1)
                    nc.vector.tensor_scalar(flip[:], trial[:], 31, 0x7FFFFFFF, ALU.arith_shift_right, ALU.bitwise_and)\
                        .then_inc(flip_ready, 1)
                    dve.wait_ge(flip_ready, t + 1)
                    nc.vector.scalar_tensor_tensor(bound[:], flip[:], -1, trial[:], ALU.bitwise_xor, ALU.bitwise_xor)\
                        .then_inc(bound_ready, 1)
                    dve.wait_ge(bound_ready, t + 1)
                    for j in range(TRIALS):
                        nc.vector.tensor_scalar(below[:, j, :], flat, bound[:, j:j + 1].bitcast(F32), 0.0, ALU.is_lt, ALU.add,
                                                accum_out=count[:, j:j + 1]).then_inc(counted, 1)
                    dve.wait_ge(summed, t + 1)
                    nc.vector.tensor_scalar(passed[:], number[:], float(KTH - 1), None, ALU.is_le).then_inc(passed_ready, 1)
                    dve.wait_ge(passed_ready, t + 1)
                    for j in range(TRIALS):
                        if j:
                            dve.wait_ge(key_ready, TRIALS * t + j)
                        apart(dve, chip)
                        nc.vector.copy_predicated(key[:], passed[:, j:j + 1], trial[:, j:j + 1]).then_inc(key_ready, 1)
                    nc.vector.tensor_scalar(bits[:], bits[:], 2, None, ALU.logical_shift_right).then_inc(state_ready, 1)
                dve.wait_ge(state_ready, ROUNDS + 1)
                link(nc.vector.tensor_scalar(flip[:, 0:1], key[:], 31, 0x7FFFFFFF, ALU.arith_shift_right, ALU.bitwise_and))
                link(nc.vector.scalar_tensor_tensor(bound[:, 0:1], flip[:, 0:1], -1, key[:], ALU.bitwise_xor, ALU.bitwise_xor))
                link(nc.vector.scalar_tensor_tensor(gate[:], logits[:], bound[:, 0:1].bitcast(F32), logits[:], ALU.is_ge, ALU.mult))
            else:
                def spread(a):
                    return a.unsqueeze(2).broadcast_to([P, NTILE, EXPERTS])

                link(nc.vector.tensor_reduce(stat[:], logits[:], AX_X, ALU.max))
                nc.vector.tensor_tensor(shifted[:], logits[:], spread(stat[:]), ALU.subtract).then_inc(ready, 1)
                dve.wait_ge(powers, 1)
                link(nc.vector.tensor_reduce(stat[:], one[:], AX_X, ALU.add))
                link(nc.vector.reciprocal(stat[:], stat[:]))
                link(nc.vector.tensor_tensor(shifted[:], one[:], spread(stat[:]), ALU.mult))
                at, n = CONST["prefer"]
                prefer = chip.consts[:, at:at + n].unsqueeze(1).broadcast_to([P, NTILE, EXPERTS])
                left = shifted
                for mark in (first, second):
                    link(nc.vector.tensor_reduce(stat[:], left[:], AX_X, ALU.max))
                    link(nc.vector.tensor_tensor(one[:], left[:], spread(stat[:]), ALU.is_equal))
                    link(nc.vector.tensor_tensor(one[:], one[:], prefer, ALU.mult))
                    link(nc.vector.tensor_reduce(stat[:], one[:], AX_X, ALU.max))
                    link(nc.vector.tensor_tensor(mark[:], one[:], spread(stat[:]), ALU.is_equal))
                    if mark is first:
                        link(nc.vector.scalar_tensor_tensor(rest[:], first[:], -2.0, shifted[:], ALU.mult, ALU.add))
                        left = rest
                link(nc.vector.tensor_tensor(one[:], first[:], second[:], ALU.add))
                link(nc.vector.tensor_tensor(one[:], one[:], shifted[:], ALU.mult))
                link(nc.vector.tensor_reduce(stat[:], one[:], AX_X, ALU.add))
                link(nc.vector.reciprocal(stat[:], stat[:]))
                link(nc.vector.tensor_tensor(gate[:], one[:], spread(stat[:]), ALU.mult))
            link(nc.vector.tensor_copy(parts[:, :, 0, :], gate[:]))
            link(nc.vector.tensor_tensor(rest[:], gate[:], parts[:, :, 0, :], ALU.subtract))
            link(nc.vector.tensor_copy(parts[:, :, 1, :], rest[:]))
            nc.vector.tensor_tensor(parts[:, :, 2, :], rest[:], parts[:, :, 1, :], ALU.subtract).then_inc(parts_ready, 1)
            if layer == 1:
                for k, (split, raw) in enumerate(weights):
                    dve.wait_ge(w_high_ready, k + 1)
                    nc.vector.scalar_tensor_tensor(split[:, 1], raw[:], WS, split[:, 0], ALU.mult, ALU.subtract)
            for k in range(4):
                dve.wait_ge(turned_ready, k + 1)
                nc.vector.tensor_copy(chip.gates_f32[:, k * SEQ:(k + 1) * SEQ], turned[k][:])
                ins = nc.vector.tensor_copy(chip.gates_b16[:, k * SEQ:(k + 1) * SEQ], turned[k][:])
            link(ins)

        @block.gpsimd
        def _(pool):
            if layer == 0:
                with pool.Fori(0, ROUNDS) as t:
                    pool.wait_ge(w_scaled_ready, t + 1)
                    apart(pool, chip)
                    nc.gpsimd.tensor_tensor(w_low[:, ds(4 * t, 4), :].rearrange("p a b -> p (a b)"), w_scaled[:],
                                            w_high[:, ds(4 * t, 4), :].rearrange("p a b -> p (a b)"), ALU.subtract).then_inc(w_low_ready, 1)

        @block.scalar
        def _(act):
            if layer == 0:
                with act.Fori(0, ROUNDS) as t:
                    act.wait_ge(w_turned, t + 1)
                    apart(act, chip)
                    nc.scalar.mul(w_high[:, ds(4 * t, 4), :].rearrange("p a b -> p (a b)"), w_bank[:], WS).then_inc(w_high_ready, 1)
                    act.wait_ge(w_low_ready, t)
                    act.wait_ge(w_high_ready, t + 1)
                    nc.scalar.mul(w_scaled[:], w_bank[:], WS).then_inc(w_scaled_ready, 1)
            if layer == 1:
                act.wait_ge(ready, 1)
                nc.scalar.activation(one[:], shifted[:], ACT.Exp).then_inc(powers, 1)
                act.wait_ge(chip.mlp1_loaded, 64)
                for split, raw in weights:
                    nc.scalar.mul(split[:, 0], raw[:], WS).then_inc(w_high_ready, 1)

        @block.tensor
        def _(pe):
            if layer == 0:
                pe.wait_ge(chip.mlp0_loaded, 32)
                for t in range(ROUNDS):
                    pe.wait_ge(counted, TRIALS * t + TRIALS)
                    pe.matmul(number[:], chip.ones[:], count[:], start=True, stop=True).then_inc(summed, 1)
                    pe.wait_ge(w_scaled_ready, t)
                    for i in range(4):
                        ins = pe.transpose(w_bank[:, i * P:(i + 1) * P], chip.w_raw[:, 4 * t + i, :], const(chip, "ident"))
                    ins.then_inc(w_turned, 1)
            pe.wait_ge(parts_ready, 1)
            for k in range(4):
                for i in range(8):
                    ins = pe.transpose(turned[k][:, i * P:(i + 1) * P], parts[:, 8 * k + i, :, :].rearrange("p a e -> p (a e)"), chip.identb[:])
                ins.then_inc(turned_ready, 1)


def experts(nc, chip, layer, w_up, w_down, bias_name, bias_rows, ungated):
    TILES = EXPERTS * HT + ungated
    RING = 4
    AHEAD = RING
    with ExitStack() as ctx:
        def sem(what):
            return ctx.enter_context(nc.semaphore(f"experts{layer}_{what}"))

        hidden = [ctx.enter_context(nc.psum_tensor(f"hidden{layer}_{k}", [P, CHUNK], F32)) for k in range(RING)]
        gate = [ctx.enter_context(nc.psum_tensor(f"gate{layer}_{k}", [P, CHUNK], F32)) for k in range(2)]
        ys = [ctx.enter_context(nc.psum_tensor(f"y{layer}_{k}", [P, CHUNK], F32)) for k in range(2)]
        active = [ctx.enter_context(nc.sbuf_tensor(f"active{layer}_{k}", [P, CHUNK], F32)) for k in range(RING)]
        weighed = [ctx.enter_context(nc.sbuf_tensor(f"weighed{layer}_{k}", [P, CHUNK], F32)) for k in range(RING)]
        high = [ctx.enter_context(nc.sbuf_tensor(f"weighed_high{layer}_{k}", [P, CHUNK], F16)) for k in range(RING)]
        low = [ctx.enter_context(nc.sbuf_tensor(f"weighed_low{layer}_{k}", [P, CHUNK], F16)) for k in range(RING)]
        up_ready, gate_ready, active_ready, weighed_ready = sem("up_ready"), sem("gate_ready"), sem("active_ready"), sem("weighed_ready")
        high_ready, low_ready = sem("high_ready"), sem("low_ready")
        down_done, y_ready, y_taken = sem("down_done"), sem("y_ready"), sem("y_taken")
        x_biased = sem("x_biased")
        block = ctx.enter_context(nc.Block())

        def whole(run, chunk):
            chunk(0, 0, True, False)
            with run.Fori(0, NCHUNK // 2 - 1) as t:
                chunk(2 * t + 1, 1, False, False)
                chunk(2 * t + 2, 0, False, False)
            chunk(NCHUNK - 1, 1, False, True)

        @block.tensor
        def _(pe):
            def up(n, k, first):
                if k >= RING or not first:
                    pe.wait_ge(active_ready, n * TILES + k - RING + 1)
                h_high, h_low = (h[:, ds(n * CHUNK, CHUNK)] for h in (chip.h_high, chip.h_low))
                apart(pe, chip)
                pe.matmul(hidden[k % RING][:], w_up[:, 0, k, :], h_high, start=True, stop=False)
                pe.matmul(hidden[k % RING][:], w_up[:, 1, k, :], h_high, start=False, stop=False)
                pe.matmul(hidden[k % RING][:], w_up[:, 0, k, :], h_low, start=False, stop=True).then_inc(up_ready, 1)

            def spread_gate(n, e, first):
                if e >= 2 or not first:
                    pe.wait_ge(weighed_ready, n * TILES + (ungated + HT * (e - 1) if e >= 2 else HT * (e - 1)))
                apart(pe, chip)
                pe.matmul(gate[e % 2][:], chip.gate_sel[:, e * P:(e + 1) * P], chip.gates_b16[:, ds(n * CHUNK, CHUNK)],
                          start=True, stop=True).then_inc(gate_ready, 1)

            def chunk(n, parity, first, last):
                y = ys[parity]
                if first:
                    for k in range(AHEAD):
                        up(n, k, True)
                    spread_gate(n, 0, True)
                for k in range(TILES):
                    if k + AHEAD < TILES:
                        up(n, k + AHEAD, first)
                    elif not last:
                        up(n + 1, k + AHEAD - TILES, False)
                    ahead = k + AHEAD - ungated
                    if ahead >= HT and ahead % HT == 0 and ahead // HT < EXPERTS:
                        spread_gate(n, ahead // HT, first)
                    if k == TILES - 1 and not last:
                        spread_gate(n + 1, 0, False)
                    if k == 0 and not first:
                        pe.wait_ge(y_taken, n - 1)
                    pe.wait_ge(high_ready, n * TILES + k + 1)
                    pe.matmul(y[:], w_down[:, 0, k, :], high[k % RING][:], start=(k == 0), stop=False)
                    pe.matmul(y[:], w_down[:, 1, k, :], high[k % RING][:], start=False, stop=False)
                    pe.wait_ge(low_ready, n * TILES + k + 1)
                    pe.matmul(y[:], w_down[:, 0, k, :], low[k % RING][:], start=False, stop=False).then_inc(down_done, 1)
                pe.matmul(y[:], bias_rows[:], chip.gates_f32[:, ds(n * CHUNK, CHUNK)], start=False, stop=True).then_inc(y_ready, 1)

            whole(pe, chunk)

        @block.scalar
        def _(act):
            def split(n, k, first):
                if k >= RING or not first:
                    act.wait_ge(down_done, n * TILES + k - RING + 1)
                act.wait_ge(weighed_ready, n * TILES + k + 1)
                nc.scalar.copy(high[k % RING][:], weighed[k % RING][:]).then_inc(high_ready, 1)

            def chunk(n, parity, first, last):
                for k in range(TILES):
                    if k >= RING or not first:
                        act.wait_ge(weighed_ready, n * TILES + k - RING + 1)
                    act.wait_ge(up_ready, n * TILES + k + 1)
                    nc.scalar.activation(active[k % RING][:], hidden[k % RING][:], ACT.Gelu_apprx_tanh, bias=col(chip, bias_name, k),
                                         scale=1.0 / WS).then_inc(active_ready, 1)
                    if k >= 1:
                        split(n, k - 1, first)
                    elif not first:
                        split(n - 1, TILES - 1, False)
                if last:
                    split(n, TILES - 1, False)

            whole(act, chunk)

        @block.gpsimd
        def _(pool):
            def chunk(n, parity, first, last):
                for k in range(TILES):
                    pool.wait_ge(high_ready, n * TILES + k + 1)
                    nc.gpsimd.tensor_tensor(low[k % RING][:], weighed[k % RING][:], high[k % RING][:], ALU.subtract).then_inc(low_ready, 1)

            whole(pool, chunk)

        @block.vector
        def _(dve):
            def add(n, parity):
                here = chip.xT[:, ds(n * CHUNK, CHUNK)]
                if layer == 1:
                    nc.vector.tensor_scalar(here, here, chip.g_bias[:, 2, ds(n // 2, 1)], None, ALU.add).then_inc(x_biased, 1)
                    dve.wait_ge(x_biased, n + 1)
                dve.wait_ge(y_ready, n + 1)
                apart(dve, chip)
                nc.vector.scalar_tensor_tensor(here, ys[parity][:], chip.gb_scaled[:, layer, ds(n // 2, 1)], here, ALU.mult, ALU.add)\
                    .then_inc(y_taken, 1)

            def chunk(n, parity, first, last):
                for k in range(TILES):
                    e = (k - ungated) // HT
                    if k >= ungated and (k - ungated) % HT == 0:
                        dve.wait_ge(gate_ready, n * EXPERTS + e + 1)
                    if k >= RING or not first:
                        dve.wait_ge(low_ready, n * TILES + k - RING + 1)
                    dve.wait_ge(active_ready, n * TILES + k + 1)
                    if k < ungated:
                        nc.vector.tensor_scalar(weighed[k % RING][:], active[k % RING][:], GS, None, ALU.mult).then_inc(weighed_ready, 1)
                    else:
                        nc.vector.tensor_tensor(weighed[k % RING][:], active[k % RING][:], gate[e % 2][:], ALU.mult).then_inc(weighed_ready, 1)
                    if k == RING - 1 and not first:
                        add(n - 1, 1 - parity)
                if last:
                    add(n, parity)

            whole(dve, chunk)


def project1(nc, chip):
    with ExitStack() as ctx:
        def sb(name, shape, dt):
            return ctx.enter_context(nc.sbuf_tensor(name, shape, dt))

        def sem(name):
            return ctx.enter_context(nc.semaphore(name))

        Q, K, V, QR, KR = range(5)
        w = chip.w1_attn
        straight = [[sb(f"straight{x}{u}", [P, CHUNK], F32) for u in range(2)] for x in range(2)]
        turned = [[sb(f"rope_turned{x}{u}", [P, CHUNK], F32) for u in range(2)] for x in range(2)]
        psum = [ctx.enter_context(nc.psum_tensor(f"project{k}", [P, CHUNK], F32)) for k in range(4)]
        value_rows = [ctx.enter_context(nc.psum_tensor(f"value_rows{k}", [P, CHUNK], F32)) for k in range(2)]
        project_ready = sem("project_ready")
        value_ready, value_taken = sem("value_ready"), sem("value_taken")
        straight_ready, turned_ready, rotated, high_ready = sem("straight_ready"), sem("turned1_ready"), sem("rotated"), sem("high1_ready")
        block = ctx.enter_context(nc.Block())
        highs = (chip.q1[0], chip.k1[0])
        lows = (chip.q1[1], chip.k1[1])

        @block.tensor
        def _(pe):
            with pe.Fori(0, BATCH) as t:
                for u in range(2):
                    at = ds(t * SEQ + u * CHUNK, CHUNK)
                    for x in range(2):
                        for part, k in enumerate(((Q, QR), (K, KR))[x]):
                            out = psum[2 * x + part][:]
                            pe.wait_ge(turned_ready, 4 * t + 2 * u + x + 1)
                            apart(pe, chip)
                            pe.matmul(out, w[:, 0, k, :], chip.h_high[:, at], start=True, stop=False)
                            pe.matmul(out, w[:, 1, k, :], chip.h_high[:, at], start=False, stop=False)
                            pe.matmul(out, w[:, 0, k, :], chip.h_low[:, at], start=False, stop=True).then_inc(project_ready, 1)
                    pe.wait_ge(value_taken, 2 * t)
                    apart(pe, chip)
                    for i in range(4):
                        out = value_rows[u][:, i * P:(i + 1) * P]
                        at = ds(t * SEQ + u * CHUNK + i * P, P)
                        pe.matmul(out, chip.h_high[:, at], w[:, 0, V, :], start=True, stop=False)
                        pe.matmul(out, chip.h_high[:, at], w[:, 1, V, :], start=False, stop=False)
                        ins = pe.matmul(out, chip.h_low[:, at], w[:, 0, V, :], start=False, stop=True)
                    ins.then_inc(value_ready, 1)

        @block.scalar
        def _(act):
            with act.Fori(0, BATCH) as t:
                for u in range(2):
                    for x in range(2):
                        act.wait_ge(rotated, 4 * t + 2 * u + x + 1)
                        apart(act, chip)
                        nc.scalar.copy(highs[x][:, ds(t * SEQ + u * CHUNK, CHUNK)], straight[x][u][:]).then_inc(high_ready, 1)
                    act.wait_ge(value_ready, 2 * t + u + 1)
                    apart(act, chip)
                    nc.scalar.copy(chip.v1[:, ds(8 * t + 4 * u, 4), :], value_rows[u][:].rearrange("p (a b) -> p a b", a=4)).then_inc(value_taken, 1)

        @block.vector
        def _(dve):
            dve.sem_inc(turned_ready, 2)
            with dve.Fori(0, BATCH) as t:
                for u in range(2):
                    at = CONST["cos"][0] + u * CHUNK
                    cos = chip.consts[:, at:at + CHUNK]
                    at = CONST["sin"][0] + u * CHUNK
                    sin = chip.consts[:, at:at + CHUNK]
                    for x in range(2):
                        dve.wait_ge(project_ready, 8 * t + 4 * u + 2 * x + 1)
                        nc.vector.scalar_tensor_tensor(straight[x][u][:], psum[2 * x][:], chip.bqk1[:, x:x + 1], cos, ALU.add, ALU.mult)\
                            .then_inc(straight_ready, 1)
                        dve.wait_ge(project_ready, 8 * t + 4 * u + 2 * x + 2)
                        nc.vector.scalar_tensor_tensor(turned[x][u][:], psum[2 * x + 1][:], chip.bqk1[:, 2 + x:3 + x], sin, ALU.add, ALU.mult)\
                            .then_inc(turned_ready, 1)
                    for x in range(2):
                        dve.wait_ge(turned_ready, 2 + 4 * t + 2 * u + x + 1)
                        dve.wait_ge(straight_ready, 4 * t + 2 * u + x + 1)
                        nc.vector.tensor_tensor(straight[x][u][:], straight[x][u][:], turned[x][u][:], ALU.add).then_inc(rotated, 1)
                    for x in range(2):
                        dve.wait_ge(high_ready, 4 * t + 2 * u + x + 1)
                        chunk = ds(t * SEQ + u * CHUNK, CHUNK)
                        nc.vector.tensor_tensor(lows[x][:, chunk], straight[x][u][:], highs[x][:, chunk], ALU.subtract)


STEPS1 = 2 * (SEQ // P)
MAX_JOBS = [("max", j, k) for j in range(4) for k in range(SEQ // P)]
SHIFT_STEP, SPREAD_STEP, MASK_STEP, CLOSE_STEPS = 0, 4, 8, (10, 13)


def slot_jobs1(shift, maxima, spread, close):
    steps = [[] for _ in range(STEPS1)]
    for n, x in enumerate(MAX_JOBS if maxima else []):
        steps[n * STEPS1 // len(MAX_JOBS)].append(x)
    if shift:
        steps[SHIFT_STEP].append(("shift",))
    if spread:
        steps[SPREAD_STEP].append(("xq",))
        steps[SPREAD_STEP + 1].append(("xk",))
    if close:
        for c, u in enumerate(CLOSE_STEPS):
            steps[u].append(("close", c))
    number = {}
    for step in steps:
        for x in step:
            number[x] = len(number)
    return steps, number


PER_QUAD = len(slot_jobs1(True, True, True, False)[1])
CLOSE_JOBS = len(CLOSE_STEPS)


def attention1(nc, chip):
    SCALE = 1.0 / (float(np.sqrt(DH1)) * WS * WS)
    PER_TURN = QUADS * PER_QUAD + CLOSE_JOBS
    UNITS1 = 4 * STEPS1
    assert PER_TURN % 2 == 0
    with ExitStack() as ctx:
        def sb(name, shape, dt):
            return ctx.enter_context(nc.sbuf_tensor(name, shape, dt))

        def sem(name):
            return ctx.enter_context(nc.semaphore(name))

        xq = [sb(f"xq{g}", [P, SEQ], F16) for g in range(QUADS)]
        xq_shift = [sb(f"xq_shift{v}", [P, SEQ], F16) for v in range(2)]
        xk = [sb(f"xk{v}", [P, SEQ], F16) for v in range(2)]
        xk_head = [[sb(f"xk{g}_head{j}", [P, SEQ], F16) for j in range(4)] for g in range(2)]
        xk_head += [[h[:, j * SEQ:(j + 1) * SEQ] for j in range(4)] for h in (chip.h_high, chip.h_low)]
        values = [sb(f"values{v}", [P, SEQ // P, 4, 32], F32) for v in range(2)]
        probs = [[sb(f"probs1_{v}{j}", [P, CHUNK], F32) for j in range(4)] for v in range(2)]
        context = [sb(f"context{g}", [P, SEQ], F32) for g in range(QUADS)]
        maxima = sb("quad_maxima", [P, 4, SEQ // P], F32)
        minus_max = sb("quad_minus_max", [P, SEQ // P, P], F16)
        turned, inverse, normed = ([sb(f"batch_{what}{c}", [P, CHUNK], F32) for c in range(2)] for what in ("turned", "inverse", "normed"))
        compact = [sb(f"batch_compact{c}", [P, CHUNK // 32, 32 // DH1], F32) for c in range(2)]
        wide = [ctx.enter_context(nc.psum_tensor(f"wide{k}", [P, SEQ], F32)) for k in range(2)]
        scores = [ctx.enter_context(nc.psum_tensor(f"scores1_{k}", [P, CHUNK], F32)) for k in range(2)]
        o_psum = [ctx.enter_context(nc.psum_tensor(f"o1_{c}", [P, CHUNK], F32)) for c in range(2)]

        pads_clear, buffers_clear = sem("pads1_clear"), sem("buffers1_clear")
        job_ready = sem("job1_ready")
        wide_free = [sem(f"wide_free{k}") for k in range(2)]
        xk_ready, minus_ready, shift_ready = sem("xk_ready"), sem("minus1_ready"), sem("shift1_ready")
        values_ready = sem("values_ready")
        score_ready, probs_ready, pv_done = sem("score1_ready"), sem("probs1_ready"), sem("pv1_done")
        sums_turned = sem("sums1_turned")
        o_taken, compact_ready, inverse_ready = sem("o1_taken"), sem("compact1_ready"), sem("inverse1_ready")
        block = ctx.enter_context(nc.Block())

        class Job1:
            def __init__(self, first, k, t):
                n = first + k
                self.bank = n % 2
                self.before = n // 2 + PER_TURN // 2 * t
                self.done = n + 1 + PER_TURN * t

        def after(b, g, n):
            return b + (g + n) // QUADS, (g + n) % QUADS

        def whole(run, slot):
            first = 0

            def next_slot(b, g, t, has, attend=True):
                nonlocal first
                slot(b, g, t, first, has, attend)
                first += len(slot_jobs1(*has)[1])

            next_slot(0, -3, 0, (False, False, True, False), False)
            next_slot(0, -2, 0, (False, True, True, False), False)
            next_slot(0, -1, 0, (True, True, True, False), False)
            next_slot(0, 0, 0, (True, True, True, False))
            with run.Fori(0, BATCH - 1) as t:
                for g in range(1, QUADS):
                    next_slot(t, g, t, (True, True, True, False))
                next_slot(t + 1, 0, t, (True, True, True, True))
            first += PER_TURN * (BATCH - 2)
            for g in range(1, QUADS):
                next_slot(BATCH - 1, g, 0, (g + 1 < QUADS, g + 2 < QUADS, g + 3 < QUADS, False))
            next_slot(BATCH, 0, 0, (False, False, False, True), False)

        @block.tensor
        def _(pe):
            pe.wait_ge(buffers_clear, 1)

            def run_job(x, job, b, g):
                out = wide[job.bank]
                nb, ng = after(b, g, {"shift": 1, "max": 2, "xq": 3, "xk": 3, "close": 0}[x[0]])
                pe.wait_ge(wide_free[job.bank], job.before)

                def spread(c, sel, x, last):
                    o = out[:, c * CHUNK:(c + 1) * CHUNK]
                    for half in range(2):
                        ins = pe.matmul(o, sel[:, (2 * ng + half) * P:(2 * ng + half + 1) * P], x[half][:, ds(nb * SEQ + c * CHUNK, CHUNK)],
                                        start=(half == 0), stop=(half == 1 and last))
                    return ins

                if x[0] == "xq":
                    spread(0, chip.q_sel, chip.q1, True)
                    ins = spread(1, chip.q_sel, chip.q1, True)
                elif x[0] == "xk":
                    spread(0, chip.k_sel, chip.k1, True)
                    ins = spread(1, chip.k_sel, chip.k1, True)
                elif x[0] == "max":
                    _, j, k = x
                    if k == 0:
                        pe.wait_ge(xk_ready, 4 * (QUADS * b + g + 2) + j + 1)
                    for c in range(2):
                        ins = pe.matmul(out[:, c * CHUNK:(c + 1) * CHUNK], xq[ng][:, k * P:(k + 1) * P],
                                        xk_head[ng][j][:, c * CHUNK:(c + 1) * CHUNK], start=True, stop=True)
                elif x[0] == "close":
                    c = x[1]
                    pe.wait_ge(o_taken, 2 * QUADS * b)
                    for n, name in enumerate(("place_ctx", "place_sum")):
                        for q in range(QUADS):
                            ins = pe.matmul(out[32 * q:32 * q + 32, n * CHUNK:(n + 1) * CHUNK], const(chip, name),
                                            context[q][:, c * CHUNK:(c + 1) * CHUNK], start=True, stop=True, tile_position=(0, 32 * q))
                else:
                    pe.wait_ge(minus_ready, QUADS * b + g + 2)
                    for c in range(2):
                        spread(c, chip.q_sel, chip.q1, False)
                        for k in range(4):
                            at = c * CHUNK + k * P
                            ins = pe.matmul(out[:, at:at + P], minus_max[:, 4 * c + k, :], chip.ident16[:], start=False, stop=(k == 3))
                ins.then_inc(job_ready, 1)

            def pv(i, u, g):
                k, c = u // 2, u % 2
                if u < 2:
                    pe.wait_ge(o_taken, 2 * i)
                for j in range(4):
                    pe.wait_ge(probs_ready, UNITS1 * i + 4 * u + j + 1)
                    pe.matmul(o_psum[c][32 * j:32 * j + 32, :], values[g % 2][:, k, j, :], probs[u % 2][j][:],
                              start=(k == 0), stop=(k == SEQ // P - 1), tile_position=(0, 32 * j)).then_inc(pv_done, 1)

            def slot(b, g, t, first, has, attend):
                i = QUADS * b + g
                steps, number = slot_jobs1(*has)

                def jobs(some):
                    for x in some:
                        run_job(x, Job1(first, number[x], t), b, g)

                if attend:
                    pe.wait_ge(shift_ready, i + 1)
                    pe.wait_ge(values_ready, i + 1)
                for u in range(STEPS1):
                    k, c = u // 2, u % 2
                    for j in range(4 if attend else 0):
                        pe.wait_ge(probs_ready, UNITS1 * i + max(4 * u + j - 1, 0))
                        pe.matmul(scores[j % 2][:], xk_head[g][j][:, k * P:(k + 1) * P],
                                  xq_shift[g % 2][:, c * CHUNK:(c + 1) * CHUNK], start=True, stop=True).then_inc(score_ready, 1)
                        if j == 0:
                            jobs(steps[u][0:1])
                        elif j == 2:
                            jobs(steps[u][1:-1])
                        elif j == 1 and u > 0:
                            pv(i, u - 1, g)
                    jobs(steps[u][1:][-1:] if attend else steps[u])
                if attend:
                    pv(i, STEPS1 - 1, g)

            whole(pe, slot)

        @block.scalar
        def _(act):
            def slot(b, g, t, first, has, attend):
                i = QUADS * b + g
                steps, number = slot_jobs1(*has)
                for u in range(STEPS1):
                    for j in range(4 if attend else 0):
                        if u >= 2:
                            act.wait_ge(pv_done, UNITS1 * i + 4 * (u - 2) + j + 1)
                        act.wait_ge(score_ready, UNITS1 * i + 4 * u + j + 1)
                        nc.scalar.activation(probs[u % 2][j][:], scores[j % 2][:], ACT.Exp, scale=SCALE).then_inc(probs_ready, 1)
                    for x in steps[u]:
                        job = Job1(first, number[x], t)
                        if x[0] in ("max", "close"):
                            continue
                        act.wait_ge(job_ready, job.done)
                        src = wide[job.bank][:]
                        if x[0] == "xq":
                            nc.scalar.copy(xq[(g + 3) % QUADS][:], src).then_inc(wide_free[job.bank], 1)
                        elif x[0] == "xk":
                            nc.scalar.activation(xk[(g + 1) % 2][:], src, ACT.Identity, bias=const(chip, "key_pad")).then_inc(wide_free[job.bank], 1)
                        else:
                            nc.scalar.copy(xq_shift[(g + 1) % 2][:], src).then_inc(wide_free[job.bank], 1)
                            act.wait_ge(wide_free[job.bank], job.before + 1)
                            act.sem_inc(shift_ready, 1)
                if attend:
                    for c in range(2):
                        act.wait_ge(pv_done, UNITS1 * i + 4 * (STEPS1 - 2 + c) + 4)
                        nc.scalar.copy(context[g][:, c * CHUNK:(c + 1) * CHUNK], o_psum[c][:]).then_inc(o_taken, 1)

            whole(act, slot)

        @block.gpsimd
        def _(pool):
            for v in range(2):
                ins = nc.gpsimd.memset(values[v][:], 0.0).then_inc(pads_clear, 1)
            pool.wait_ge(pads_clear, 2)
            for v in range(2):
                nc.gpsimd.memset(values[v][:, :, :, DH1:DH1 + 1], WS).then_inc(pads_clear, 1)
            nc.gpsimd.memset(minus_max[:], 0.0).then_inc(pads_clear, 1)
            pool.wait_ge(pads_clear, 5)
            pool.sem_inc(buffers_clear, 1)

            def slot(b, g, t, first, has, attend):
                if not has[0]:
                    return
                nb, ng = after(b, g, 1)
                par = (g + 1) % 2
                pool.wait_ge(job_ready, Job1(first, 0, t).done)
                apart(pool, chip)
                src = chip.v1[:, ds(8 * nb, 8), 32 * ng:32 * ng + 32].rearrange("p k (j d) -> p k j d", j=4)
                nc.gpsimd.tensor_copy(values[par][:, :, :, 0:DH1], src).then_inc(values_ready, 1)

            whole(pool, slot)

        @block.vector
        def _(dve):
            dve.wait_ge(buffers_clear, 1)

            def close(b, c, job):
                n = 2 * (b - 1) + c + 1
                out, sums = (wide[job.bank][:, k * CHUNK:(k + 1) * CHUNK] for k in range(2))
                dve.wait_ge(job_ready, job.done)
                nc.vector.transpose(turned[c][:], sums).then_inc(sums_turned, 1)
                dve.wait_ge(sums_turned, n)
                nc.vector.reciprocal(compact[c][:], turned[c][:].rearrange("p (a j d) -> p a j d", j=32 // DH1, d=DH1)[:, :, :, 0])\
                    .then_inc(compact_ready, 1)
                dve.wait_ge(compact_ready, n)
                nc.vector.transpose(inverse[c][:].rearrange("p (a j d) -> p a j d", j=32 // DH1, d=DH1),
                                    compact[c][:].unsqueeze(3).broadcast_to([P, CHUNK // 32, 32 // DH1, DH1])).then_inc(inverse_ready, 1)
                dve.wait_ge(inverse_ready, n)
                nc.vector.tensor_tensor(normed[c][:], out, inverse[c][:], ALU.mult).then_inc(wide_free[job.bank], 1)
                dve.wait_ge(wide_free[job.bank], job.before + 1)
                here = chip.xT[:, ds((b - 1) * SEQ + c * CHUNK, CHUNK)]
                nc.vector.scalar_tensor_tensor(here, normed[c][:], chip.mod[:, 1, GA, ds(b - 1, 1)], here, ALU.mult, ALU.add)

            def slot(b, g, t, first, has, attend):
                steps, number = slot_jobs1(*has)
                if has[1]:
                    dve.wait_ge(minus_ready, QUADS * b + g + 2)
                for u in range(STEPS1):
                    if has[2] and u == MASK_STEP:
                        job = Job1(first, number[("xk",)], t)
                        dve.wait_ge(wide_free[job.bank], job.before + 1)
                        for j in range(4):
                            nc.vector.tensor_scalar(xk_head[(g + 3) % QUADS][j][:], xk[(g + 1) % 2][:], const(chip, "head_rows")[:, j:j + 1], None,
                                                    ALU.mult).then_inc(xk_ready, 1)
                    for x in steps[u]:
                        if x[0] == "close":
                            close(b, x[1], Job1(first, number[x], t))
                        if x[0] != "max":
                            continue
                        _, j, k = x
                        job = Job1(first, number[x], t)
                        dve.wait_ge(job_ready, job.done)
                        nc.vector.tensor_reduce(maxima[:, j, k:k + 1], wide[job.bank][:], AX_X, ALU.max).then_inc(wide_free[job.bank], 1)
                if not has[1]:
                    return
                for x in MAX_JOBS[-2:]:
                    job = Job1(first, number[x], t)
                    dve.wait_ge(wide_free[job.bank], job.before + 1)
                out = minus_max[:].rearrange("p k (j r) -> p j k r", j=4)[:, :, :, 3 * DH1:3 * DH1 + 1]
                nc.vector.tensor_scalar(out, maxima[:].unsqueeze(3), -1.0 / SH, None, ALU.mult).then_inc(minus_ready, 1)

            whole(dve, slot)


def load_mlp1(nc, chip, dram):
    with nc.Block() as block:
        @block.sync
        def _(sp):
            up, down = chip.mlp1_raw
            up = up[:].rearrange("p k m -> p (k m)")
            sp.dma_start(up[:, 0:HID], dram["L1_ffn_Wfc_s"]).then_inc(chip.mlp1_loaded, 16)
            sp.dma_start(up[:, HID:].rearrange("c (e h) -> c e h", e=EXPERTS), dram["L1_ffn_Wfc"].rearrange("e c h -> c e h"))\
                .then_inc(chip.mlp1_loaded, 16)
            sp.dma_start(down[:, 0:HT, :], dram["L1_ffn_Wproj_s"].rearrange("(j p) d -> p j d", p=P)).then_inc(chip.mlp1_loaded, 16)
            sp.dma_start(down[:, HT:, :], dram["L1_ffn_Wproj"].rearrange("e (j p) d -> p (e j) d", p=P)).then_inc(chip.mlp1_loaded, 16)


def store(nc, chip, out):
    with ExitStack() as ctx:
        def sem(name):
            return ctx.enter_context(nc.semaphore(name))

        turned = [ctx.enter_context(nc.psum_tensor(f"turned{u}", [P, CHUNK], F32)) for u in range(2)]
        rows = [ctx.enter_context(nc.sbuf_tensor(f"out_rows{u}", [P, 4, CH], F32)) for u in range(2)]
        out_turned, out_copied = sem("out_turned"), sem("out_copied")
        out_stored = [sem(f"out_stored{u}") for u in range(2)]
        view = out.rearrange("b (t p) c -> p (b t) c", p=P)
        block = ctx.enter_context(nc.Block())

        @block.tensor
        def _(pe):
            for n in range(NCHUNK):
                if n >= 2:
                    pe.wait_ge(out_copied, n - 1)
                for i in range(4):
                    at = n * CHUNK + i * P
                    ins = pe.transpose(turned[n % 2][:, i * P:(i + 1) * P], chip.xT[:, at:at + P], const(chip, "ident"))
                ins.then_inc(out_turned, 1)

        @block.vector
        def _(dve):
            for n in range(NCHUNK):
                dve.wait_ge(out_turned, n + 1)
                if n >= 2:
                    dve.wait_ge(out_stored[n % 2], 16 * (n // 2))
                nc.vector.tensor_copy(rows[n % 2][:], turned[n % 2][:].rearrange("p (i c) -> p i c", i=4)).then_inc(out_copied, 1)

        @block.sync
        def _(sp):
            for n in range(NCHUNK):
                sp.wait_ge(out_copied, n + 1)
                sp.dma_start(view[:, 4 * n:4 * n + 4, :], rows[n % 2][:]).then_inc(out_stored[n % 2], 16)
            for u in range(2):
                sp.wait_ge(out_stored[u], 16 * NCHUNK // 2)


def clear_semaphores(nc):
    with nc.Block() as block:
        @block.sync
        def _(sp):
            for used in sorted(nc.released_uncleared_semaphores):
                sp.sem_clear(range(used, used + 1))


def program(nc, dram, out):
    chip = Chip()
    with ExitStack() as whole:
        chip.apart = whole.enter_context(nc.semaphore("apart"))

        def keep(name, shape, dt, ctx=whole):
            return ctx.enter_context(nc.sbuf_tensor(name, shape, dt))

        chip.xT = keep("xT", [P, TOK], F32)
        chip.h_high = keep("h_high", [P, TOK], F16)
        chip.h_low = keep("h_low", [P, TOK], F16)
        chip.consts = keep("consts_sb", [P, CONST_COLS], F32)
        chip.cols = keep("cols", [P, ROWS], F32)
        chip.bqk = keep("bqk", [P, 2 * HEADS0], F32)
        chip.bqk1 = keep("bqk1", [P, 4], F32)
        chip.bv0 = chip.cols[:, ROW_AT["bv0"][0]:ROW_AT["bv0"][0] + PAIRS]
        chip.mod = keep("mod", [P, 2, 6, BATCH], F32)
        chip.g_bias = keep("g_bias", [P, 3, BATCH], F32)
        chip.ga_scaled = keep("ga_scaled", [P, BATCH], F32)
        chip.gb_scaled = keep("gb_scaled", [P, 2, BATCH], F32)
        chip.mean_ones = keep("mean_ones", [P, P], F32)
        chip.ones = keep("ones", [P, P], F32)
        chip.sum_ones = keep("sum_ones", [P, DH0], F32)
        chip.eps = keep("eps", [P, 1], F32)
        chip.ident16 = keep("ident16", [P, P], F16)
        chip.identb = keep("identb", [P, P], BF16)
        chip.mask_qk = keep("mask_qk", [P, P], BF16)
        chip.mask_kq = keep("mask_kq", [P, P], BF16)
        chip.gate_sel = keep("gate_sel", [3 * EXPERTS, EXPERTS * P], BF16)
        chip.q_sel = keep("q_sel", [P, QUADS * 2 * P], F16)
        chip.k_sel = keep("k_sel", [P, QUADS * 2 * P], F16)
        chip.w_router1 = keep("w_router1", [P, EXPERTS], F32)
        chip.w1_attn = keep("w1_attn_split", [P, 2, 5, CH], F16)
        chip.w1_attn_raw = keep("w1_attn_raw", [P, 3, CH], F32)
        chip.b2_rows = keep("b2_rows", [3 * EXPERTS, CH], F32)
        chip.bproj_rows = keep("bproj_rows", [3 * EXPERTS, CH], F32)

        with ExitStack() as layer0:
            chip.w_raw = keep("w_raw", [P, 2 * EXPERTS * HT, P], F32, layer0)
            chip.mlp0_loaded = layer0.enter_context(nc.semaphore("mlp0_loaded"))
            with ExitStack() as att:
                chip.w_qk = keep("w_qk", [P, 2, HEADS0, 2, 2, DH0], F16, att)
                chip.w_v = keep("w_v", [P, 2, HEADS0 * DH0], F16, att)
                chip.w_out = keep("w_out", [P, 2, PAIRS, CH], F16, att)
                with ExitStack() as raw:
                    chip.w_qkv_raw = keep("w_qkv_raw", [P, 3 * HEADS0 * DH0], F32, raw)
                    chip.w_out_raw = keep("w_out_raw", [P, PAIRS, CH], F32, raw)
                    setup(nc, chip, dram)
                layer_norm(nc, chip, "ln1", 0, SA, CA)
                attention0(nc, chip)
            with ExitStack() as mlp:
                chip.logits = keep("logits0", [P, NTILE, EXPERTS], F32, mlp)
                chip.gates_b16 = keep("gates0_b16", [3 * EXPERTS, TOK], BF16, mlp)
                chip.gates_f32 = keep("gates0_f32", [3 * EXPERTS, TOK], F32, mlp)
                layer_norm(nc, chip, "ln2", 0, SB, CB, bias_of=0, router=chip.cols[:, ROW_AT["gate0"][0]:ROW_AT["gate0"][0] + EXPERTS],
                           logits=chip.logits)
                chip.w12T = keep("w12T", [P, 2, 2 * EXPERTS * HT, P], F16, mlp)
                gates(nc, chip, 0)
                experts(nc, chip, 0, chip.w12T[:, :, 0:EXPERTS * HT, :], chip.w12T[:, :, EXPERTS * HT:, :], "b1", chip.b2_rows, 0)
        clear_semaphores(nc)
        with ExitStack() as layer1:
            layer_norm(nc, chip, "ln3", 1, SA, CA)
            with ExitStack() as att:
                chip.q1 = [keep(f"q1_{half}", [P, TOK], F16, att) for half in range(2)]
                chip.k1 = [keep(f"k1_{half}", [P, TOK], F16, att) for half in range(2)]
                chip.v1 = keep("v1", [P, NTILE, CH], F32, att)
                project1(nc, chip)
                attention1(nc, chip)
            chip.logits = keep("logits1", [P, NTILE, EXPERTS], F32, layer1)
            chip.gates_b16 = keep("gates1_b16", [3 * EXPERTS, TOK], BF16, layer1)
            chip.gates_f32 = keep("gates1_f32", [3 * EXPERTS, TOK], F32, layer1)
            chip.up1 = keep("up1", [P, 2, HT * (EXPERTS + 1), P], F16, layer1)
            chip.down1 = keep("down1", [P, 2, HT * (EXPERTS + 1), P], F16, layer1)
            chip.mlp1_raw = [keep(f"{what}_raw", [P, HT * (EXPERTS + 1), P], F32, layer1) for what in ("up1", "down1")]
            chip.mlp1_loaded = layer1.enter_context(nc.semaphore("mlp1_loaded"))
            load_mlp1(nc, chip, dram)
            layer_norm(nc, chip, "ln4", 1, SB, CB, bias_of=1, router=chip.w_router1[:], logits=chip.logits)
            gates(nc, chip, 1)
            experts(nc, chip, 1, chip.up1, chip.down1, "bfc_s", chip.bproj_rows, HT)
        store(nc, chip, out)


INPUTS = ['L0_attn_x', 'L0_attn_w_qkv', 'L0_attn_b_qkv', 'L0_attn_w_out', 'L0_attn_b_out', 'L0_ffn_gate_weight', 'L0_ffn_w1',
          'L0_ffn_b1', 'L0_ffn_w2', 'L0_ffn_b2', 'L0_c', 'L0_wmod', 'L1_attn_Wq', 'L1_attn_bq', 'L1_attn_Wk', 'L1_attn_bk',
          'L1_attn_Wv', 'L1_attn_bv', 'L1_ffn_Wfc_s', 'L1_ffn_bfc_s', 'L1_ffn_Wproj_s', 'L1_ffn_bproj_s', 'L1_ffn_Wr',
          'L1_ffn_Wfc', 'L1_ffn_bfc', 'L1_ffn_Wproj', 'L1_ffn_bproj', 'L1_c', 'L1_wmod']


def kernel(**inputs):
    import concourse.bacc as bacc
    from concourse.bass_utils import run_bass_kernel_spmd

    nc = bacc.Bacc("TRN2", target_bir_lowering=False, num_devices=1)
    arrays, dram = {}, {}
    for name in INPUTS:
        arrays[name] = np.ascontiguousarray(inputs[name])
        dram[name] = nc.dram_tensor(name, arrays[name].shape, mybir.dt.from_np(arrays[name].dtype), kind="ExternalInput").ap()
    arrays["consts"] = constants()
    dram["consts"] = nc.dram_tensor("consts", arrays["consts"].shape, F32, kind="ExternalInput").ap()
    out = nc.dram_tensor("out", (BATCH, SEQ, CH), F32, kind="ExternalOutput").ap()
    program(nc, dram, out)
    result = run_bass_kernel_spmd(nc, [arrays], core_ids=[0])
    return result.results[0]["out"]
```
